# Optimizing a Trainium2 kernel written in Bass

```python
import numpy as np
import jax
import jax.numpy as jnp

def _softmax(x, axis=-1):
    return jax.nn.softmax(x, axis=axis)

def _gelu(x):
    return jax.nn.gelu(x, approximate=True)

def _silu(x):
    return jax.nn.silu(x)

def _sigmoid(x):
    return jax.nn.sigmoid(x)

def _layernorm(x, axis=-1, eps=1e-05):
    m = jnp.mean(x, axis=axis, keepdims=True)
    v = jnp.var(x, axis=axis, keepdims=True)
    return (x - m) / jnp.sqrt(v + eps)

def _scatter_add(tgt, idx, src, axis=0):
    return tgt.at[idx].add(src)

def _segment_sum(src, seg, n):
    return jax.ops.segment_sum(src, seg, n)
kernel_name = 'mk_gps_d1_gnn_r32_99d6c5'

def setup_inputs(seed: int=0):
    np.random.seed(seed)
    _w = jnp.asarray

    def _rec_inputs():
        import jax
        import jax.numpy as jnp
        _gk = jax.random.key(seed)
        x = -0.0003713 + 1 * jax.random.normal(jax.random.fold_in(_gk, 1), (3125, 256), jnp.float32)
        _s = jax.random.randint(jax.random.fold_in(_gk, 2), (25000,), 0, 3125, jnp.int32)
        _d = jax.random.randint(jax.random.fold_in(_gk, 3), (25000,), 0, 3125, jnp.int32)
        _loop = jnp.arange(3125, dtype=jnp.int32)
        src = jnp.concatenate([_s, _d, _loop])
        dst = jnp.concatenate([_d, _s, _loop])
        _o = jnp.argsort(dst, stable=True)
        src = src[_o]
        dst = dst[_o]
        return (x, src, dst)
    x, src, dst = _rec_inputs()

    def _L0_gnn_setup():
        import jax, jax.numpy as jnp
        import numpy as np
        N = 50000
        E = 25000
        IN_C = 256
        HEADS = 8
        OUT_C = 32
        key = jax.random.key(seed)
        k1, k2, k3, k4, k5 = jax.random.split(key, 5)
        x = jax.random.normal(k1, (N, IN_C), dtype=jnp.float32)
        edge_index = jax.random.randint(k2, (2, E), 0, N, dtype=jnp.int64)
        lim_W = float(np.sqrt(6.0 / (IN_C + HEADS * OUT_C)))
        lim_a = float(np.sqrt(6.0 / (HEADS + OUT_C)))
        W = jax.random.uniform(k3, (IN_C, HEADS * OUT_C), minval=-lim_W, maxval=lim_W, dtype=jnp.float32)
        a_src = jax.random.uniform(k4, (HEADS, OUT_C), minval=-lim_a, maxval=lim_a, dtype=jnp.float32)
        a_dst = jax.random.uniform(k5, (HEADS, OUT_C), minval=-lim_a, maxval=lim_a, dtype=jnp.float32)
        return {'x': x, 'edge_index': edge_index, 'W': W, 'a_src': a_src, 'a_dst': a_dst}
    _L0_gnn_all = _L0_gnn_setup()
    _L0_gnn_in = {k: v for k, v in _L0_gnn_all.items() if k in ('W', 'a_src', 'a_dst')}
    del _L0_gnn_all

    def _L0_mix_setup():
        import jax, jax.numpy as jnp
        import numpy as np
        A, Bc, Cc = (0.5, 1.0, 1.0)
        H = 8
        EPS = 1e-12

        def _normalize(t):
            n = jnp.linalg.norm(t, axis=-1, keepdims=True)
            return t / jnp.maximum(n, EPS)
        key = jax.random.key(seed)
        ks = jax.random.split(key, 5)
        B, N, C = (8, 64, 256)
        D = C // H
        x = jax.random.normal(ks[0], (B, N, C), dtype=jnp.float32)
        Wqkv = jax.random.normal(ks[1], (3 * H * D, C), dtype=jnp.float32) * 0.02
        bqkv = jnp.zeros((3 * H * D,), dtype=jnp.float32)
        Wproj = jax.random.normal(ks[2], (C, H * D), dtype=jnp.float32) * 0.02
        bproj = jnp.zeros((C,), dtype=jnp.float32)
        temperature = jnp.ones((1, H, 1, 1), dtype=jnp.float32)
        return {'x': x, 'Wqkv': Wqkv, 'bqkv': bqkv, 'Wproj': Wproj, 'bproj': bproj, 'temperature': temperature}
    _L0_mix_all = _L0_mix_setup()
    _L0_mix_in = {k: v for k, v in _L0_mix_all.items() if k in ('Wqkv', 'bqkv', 'Wproj', 'bproj', 'temperature')}
    del _L0_mix_all

    def _L0_ffn_setup():
        import jax, jax.numpy as jnp
        import numpy as np
        C = 256
        HID = 1024
        E = 8
        TEMP = 1.0
        key = jax.random.key(seed)
        ks = jax.random.split(key, 7)
        x = jax.random.normal(ks[0], (8, 512, C), dtype=jnp.float32)
        W1 = jax.random.normal(ks[1], (C, HID), dtype=jnp.float32) * 0.02
        b1 = jnp.zeros((HID,), dtype=jnp.float32)
        Wg = jax.random.normal(ks[2], (HID, E), dtype=jnp.float32) * 0.02
        bg = jnp.zeros((E,), dtype=jnp.float32)
        Wd = jax.random.normal(ks[3], (E, HID, C), dtype=jnp.float32) * 0.02
        bd = jnp.zeros((E, C), dtype=jnp.float32)
        return {'x': x, 'W1': W1, 'b1': b1, 'Wg': Wg, 'bg': bg, 'Wd': Wd, 'bd': bd}
    _L0_ffn_all = _L0_ffn_setup()
    _L0_ffn_in = {k: v for k, v in _L0_ffn_all.items() if k in ('W1', 'b1', 'Wg', 'bg', 'Wd', 'bd')}
    del _L0_ffn_all
    return {'x': x, 'src': src, 'dst': dst, 'L0_gnn_W': _L0_gnn_in['W'], 'L0_gnn_a_src': _L0_gnn_in['a_src'], 'L0_gnn_a_dst': _L0_gnn_in['a_dst'], 'L0_mix_Wqkv': _L0_mix_in['Wqkv'], 'L0_mix_bqkv': _L0_mix_in['bqkv'], 'L0_mix_Wproj': _L0_mix_in['Wproj'], 'L0_mix_bproj': _L0_mix_in['bproj'], 'L0_mix_temperature': _L0_mix_in['temperature'], 'L0_ffn_W1': _L0_ffn_in['W1'], 'L0_ffn_b1': _L0_ffn_in['b1'], 'L0_ffn_Wg': _L0_ffn_in['Wg'], 'L0_ffn_bg': _L0_ffn_in['bg'], 'L0_ffn_Wd': _L0_ffn_in['Wd'], 'L0_ffn_bd': _L0_ffn_in['bd']}

def reference(x, src, dst, L0_gnn_W, L0_gnn_a_src, L0_gnn_a_dst, L0_mix_Wqkv, L0_mix_bqkv, L0_mix_Wproj, L0_mix_bproj, L0_mix_temperature, L0_ffn_W1, L0_ffn_b1, L0_ffn_Wg, L0_ffn_bg, L0_ffn_Wd, L0_ffn_bd):
    import jax
    import jax.numpy as jnp

    def _L0_gnn_ref(x, edge_index, W, a_src, a_dst):
        import jax, jax.numpy as jnp
        import numpy as np
        N = 50000
        E = 25000
        IN_C = 256
        HEADS = 8
        OUT_C = 32
        n = x.shape[0]
        H, D = a_src.shape
        x_proj = (x @ W).reshape(n, H, D)
        alpha_src = jnp.einsum('nhd,hd->nh', x_proj, a_src)
        alpha_dst = jnp.einsum('nhd,hd->nh', x_proj, a_dst)
        row, col = (edge_index[0], edge_index[1])
        e = alpha_src[row] + alpha_dst[col]
        m = jax.ops.segment_max(e, col, num_segments=n)
        m = jnp.where(jnp.isfinite(m), m, 0.0)
        e_exp = jnp.exp(e - m[col])
        s = jax.ops.segment_sum(e_exp, col, num_segments=n)
        att = e_exp / (s[col] + 1e-16)
        out = jax.ops.segment_sum(att[:, :, None] * x_proj[row], col, num_segments=n)
        return out.reshape(n, H * D)

    def _L0_mix_ref(x, Wqkv, bqkv, Wproj, bproj, temperature):
        import jax, jax.numpy as jnp
        import numpy as np
        A, Bc, Cc = (0.5, 1.0, 1.0)
        H = 8
        EPS = 1e-12

        def _normalize(t):
            n = jnp.linalg.norm(t, axis=-1, keepdims=True)
            return t / jnp.maximum(n, EPS)
        B, N, C = x.shape
        D = C // H
        scale = float(D) ** 0.25
        qkv = (x @ Wqkv.T + bqkv).reshape(B, N, 3, H, D)
        qkv = jnp.transpose(qkv, (2, 0, 3, 1, 4))
        q, k, v = (qkv[0], qkv[1], qkv[2])
        q = q * scale
        v1 = jnp.concatenate([jnp.ones((B, H, N, 1), dtype=v.dtype), v], axis=-1)
        qn = _normalize(q) * (scale * temperature)
        kn = _normalize(k) * scale
        vN = v1 / N
        kv_mod = jnp.einsum('bhni,bhnj,bhne->bhije', kn, kn, vN)
        kv = jnp.einsum('bhnd,bhne->bhde', kn, vN)
        vsum = jnp.sum(vN, axis=-2)[:, :, None, :]
        y = A * jnp.einsum('bhni,bhnj,bhije->bhne', qn, qn, kv_mod) + scale ** 2 * Bc * jnp.einsum('bhnd,bhde->bhne', qn, kv) + scale ** 4 * Cc * vsum
        y_norm, y = (y[..., :1], y[..., 1:])
        y = y / y_norm
        out = jnp.transpose(y, (0, 2, 1, 3)).reshape(B, N, H * D)
        return out @ Wproj.T + bproj

    def _L0_ffn_ref(x, W1, b1, Wg, bg, Wd, bd):
        import jax, jax.numpy as jnp
        import numpy as np
        C = 256
        HID = 1024
        E = 8
        TEMP = 1.0
        orig_shape = x.shape
        xf = x.reshape(-1, orig_shape[-1])
        H = jax.nn.gelu(xf @ W1 + b1, approximate=False)
        probs = jax.nn.softmax((H @ Wg + bg) / TEMP, axis=-1)
        assign = jnp.argmax(probs, axis=-1)
        out = jnp.zeros_like(xf)
        for e in range(Wd.shape[0]):
            y = H @ Wd[e] + bd[e]
            sel = (assign == e)[:, None]
            out = out + jnp.where(sel, probs[:, e:e + 1] * y, 0.0)
        return out.reshape(orig_shape)
    edge_index = jnp.stack([src, dst])
    xn = _layernorm(x, axis=-1)
    x = x + _L0_gnn_ref(xn, edge_index, L0_gnn_W, L0_gnn_a_src, L0_gnn_a_dst) + _L0_mix_ref(xn[None], L0_mix_Wqkv, L0_mix_bqkv, L0_mix_Wproj, L0_mix_bproj, L0_mix_temperature)[0]
    x = x + _L0_ffn_ref(_layernorm(x, axis=-1)[None], L0_ffn_W1, L0_ffn_b1, L0_ffn_Wg, L0_ffn_bg, L0_ffn_Wd, L0_ffn_bd)[0]
    return x

_drawn_inputs = setup_inputs


def setup_inputs(seed=0):
    import zlib

    import numpy as np

    out = dict(_drawn_inputs(seed))
    spreads = {'L0_mix_bqkv': (0.0, 0.297),
     'L0_mix_bproj': (0.0, 0.1),
     'L0_mix_temperature': (1.0, 0.6),
     'L0_ffn_b1': (0.0, 0.66),
     'L0_ffn_bg': (0.0, 0.408),
     'L0_ffn_bd': (0.0, 0.613)}
    factors = {'L0_gnn_a_dst': 8.0,
     'L0_mix_Wqkv': 8.0,
     'L0_ffn_W1': 2.911,
     'L0_ffn_Wg': 3.181,
     'L0_ffn_Wd': 3.53}
    for name, (base, spread) in spreads.items():
        noise = np.random.default_rng([zlib.crc32(name.encode()), seed]).standard_normal(out[name].shape)
        drawn = base * np.exp(spread * noise) if base else spread * noise
        out[name] = jnp.asarray(drawn.astype(out[name].dtype))
    for name, factor in factors.items():
        out[name] = (out[name] * factor).astype(out[name].dtype)
    return out
```

```python
import concourse.bass as bass
from concourse import mybir
from contextlib import ExitStack

F32, BF16, I32 = mybir.dt.float32, mybir.dt.bfloat16, mybir.dt.int32
ALU, ACT, AX = mybir.AluOpType, mybir.ActivationFunctionType, mybir.AxisListType
ds = bass.ds

N, C, H, D = 3125, 256, 8, 32
P, T = 125, 25
E = 2 * 25000 + N
EP = 128
ET = -(-E // EP)
SLOTS = 8
XW = C + H
ROW = 3 * XW
NACC = N + EP
HID, NE = 1024, 8
ST = (N + NE * 127) // 128
HROW = HID + C
NOBODY = 4096
FD = 17
KW = FD * D
KROW = KW + D + 2
LN_EPS = 1e-5
SCALE = float(D) ** 0.25
PRE = 8
KK_DVE = 6


class Stage:

    def __init__(self, sem, pre=PRE):
        self.sem, self.pre = sem, pre

    def done(self, n):
        return n + (1 + self.pre)

    def ago(self, n, depth):
        return n + (1 + self.pre - depth)


def build(nc, x, src, dst, dst0, W, a_src, WqkvT, bqkv, WprojT, bproj, temp, W1, b1, Wg, bg, Wd, bd, out,
          table, hidden, order):
    with ExitStack() as ctx:
        def sb(name, shape, dt=F32):
            return ctx.enter_context(nc.sbuf_tensor(name, shape, dt))

        def bank(name):
            return ctx.enter_context(nc.psum_tensor(name, [128, 512], F32))

        def region(*alternatives):
            found, most = [], 0
            for tensors in alternatives:
                with ExitStack() as st:
                    size = 0
                    for name, shape, dt in tensors:
                        found.append(st.enter_context(nc.sbuf_tensor(name, shape, dt)))
                        n = 2 if dt == BF16 else 4
                        for s in shape[1:]:
                            n *= s
                        size += -(-n // 32) * 32
                most = max(most, size)
            sb(f"region_{found[0].name}", [128, most // 4])
            return found

        def over(a, parts, off, dims):
            return bass.AP(a.tensor, a.offset + off, [[a.ap[0][0], parts], *dims])

        def at(a, t, lo=0, hi=None):
            hi = a.shape[-1] if hi is None else hi
            return a[:, ds(t, 1), lo:hi].rearrange("p o c -> p (o c)")

        ident = sb("ident", [128, 128])
        W_sb = sb("W_sb", [128, 2, XW])
        WqkvT_sb = sb("WqkvT_sb", [128, 2, 3 * C])
        WprojT_sb = sb("WprojT_sb", [128, 2, C])
        bqkv_bc = sb("bqkv_bc", [P, 3 * C])
        bproj_bc = sb("bproj_bc", [P, C])
        Wg_sb = sb("Wg_sb", [128, 8, NE])
        bg_bc = sb("bg_bc", [P, NE])
        temp_bc = sb("temp_bc", [P, H])
        iota_bf = sb("iota_bf", [128, 128], BF16)
        src_sb = sb("src_sb", [128, ET], I32)
        dloc = sb("dloc", [128, ET])
        base_row = sb("base_row", [1, ET], I32)
        headsel = sb("headsel", [24, 2, 128])
        rtri = sb("rtri", [P, P])
        rones = sb("rones", [P, P])
        pay_st = sb("pay_st", [P, 5, 2], I32)
        slot_st = sb("slot_st", [P, 5], I32)
        blockones = sb("blockones", [128, 128])
        headmask = sb("headmask", [128, 128])
        normfac = sb("normfac", [P, 2 * H])
        normeps = sb("normeps", [P, 2 * H])
        Mpair = sb("Mpair", [128, 2, 4, 128])
        Mdiag = sb("Mdiag", [128, 2, 128])
        Mlin = sb("Mlin", [128, 2, 128])
        Mgram = sb("Mgram", [128, 2, 128])
        ksum = sb("ksum", [128, 2])
        vsum = sb("vsum", [128, 2])
        st_all = sb("st_all", [P, T, 6])
        mean = sb("mean", [P, T])
        delta = sb("delta", [P, T])
        var = sb("var", [P, T])
        rstd = sb("rstd", [P, T])
        nmr = sb("nmr", [P, T])
        iidx = sb("iidx", [128, 2, SLOTS], I32)
        onehot = sb("onehot", [128, 4, EP], BF16)
        hmax = sb("hmax", [P, H])
        hmaxall = sb("hmaxall", [P, H])
        prob = sb("prob", [P, T])
        pay = sb("pay", [P, T, 2], I32)
        slot_i = sb("slot_i", [P, T], I32)
        order_sb = sb("order_sb", [128, ST, 2], I32)
        experts_i = sb("experts_i", [1, ST], I32)

        raw_all, mixo = region(
            [("raw_all", [P, T, XW], F32)],
            [("mixo", [P, T, C], F32)])
        (tb_all, acc, wsum, hp, h0, h1, hT, dxn, dxs,
         lg_all, ex, r_a, r_b, r_c, r_d, r_e, r_f, r_g, r_h, ev32, hs0, hs1, hs2, hs3) = region(
            [("tb_all", [P, T, ROW], BF16)],
            [("acc", [128, 2, NACC], F32), ("wsum", [24, NACC], F32)],
            [("hp", [P, 2, HID], F32), ("h0", [P, HID], F32), ("h1", [P, HID], F32), ("hT", [128, 8, P], F32),
             ("dxn", [P, 2, C], F32), ("dxs", [128, 2, 2, P], F32),
             ("lg_all", [P, T, NE], F32), ("ex", [P, T, NE], F32), ("r_a", [P, T, NE], F32), ("r_b", [P, T, NE], F32),
             ("r_c", [P, NE, T], F32), ("r_d", [P, NE, T], F32), ("r_e", [P, T], F32), ("r_f", [P, NE], F32),
             ("r_g", [P, NE], I32), ("r_h", [P, NE], F32), ("ev32", [1, ST, NE], F32)],
            [(f"hs{b}", [128, HROW], F32) for b in range(4)])
        (xnT_all, W1_sb, b1_bc, bd_bc, qsk) = region(
            [("xnT_all", [128, 2, N], F32)],
            [("W1_sb", [128, 2, HID], F32), ("b1_bc", [P, HID], F32), ("bd_bc", [128, NE * C], F32),
             ("qsk", [P, H, 128], F32)])
        (x_all, xn, xs, yw, y1, w1, waste, baseb, asrc_bc, wa_prod, iota_i, head_i, head_f,
         q_all, rows, kkx, kd, kc, qkv, sq, kxs, ss, ss2, nrm, rcp, rn,
         q_all2, rows2, F, qs, qper, bab, qT, F0, TQ, nn, rnn, yT, xq, xb,
         q_all3, rows3, KV, KX, KL,
         Wd_sb, hsT, so, t1, ix, cs, crs, cg) = region(
            [("x_all", [P, T, C], F32), ("xn", [P, 2, C], F32), ("xs", [128, 2, 2, P], F32), ("yw", [P, 2, C], F32),
             ("y1", [P, 2, C], F32), ("w1", [P, T, H], F32), ("waste", [128, ET], I32), ("baseb", [128, ET], I32), ("asrc_bc", [128, C], F32),
             ("wa_prod", [128, 2, C], F32), ("iota_i", [128, 128], I32), ("head_i", [24, 2, 128], I32),
             ("head_f", [24, 2, 2, 128], F32)],
            [("q_all", [P, T, C], F32), ("rows", [128, 2, SLOTS, ROW], BF16), ("kkx", [P, H, KROW], F32),
             ("kd", [P, H, 48], F32), ("kc", [P, C], F32), ("qkv", [P, 3 * C], F32), ("sq", [P, 2 * C], F32), ("kxs", [128, 2, 2, P], F32),
             ("ss", [P, 16], F32), ("ss2", [P, 16], F32), ("nrm", [P, 16], F32), ("rcp", [P, 16], F32),
             ("rn", [P, 16], F32)],
            [("q_all2", [P, T, C], F32), ("rows2", [128, 2, SLOTS, ROW], BF16), ("F", [128, H, 4, P], F32),
             ("qs", [P, C], F32), ("qper", [P, H, 144], F32), ("bab", [128, H, P], F32), ("qT", [128, 2, P], F32), ("F0", [128, 2, P], F32),
             ("TQ", [128, 2, P], F32), ("nn", [128, 2, P], F32), ("rnn", [128, 2, P], F32), ("yT", [128, 2, P], F32),
             ("xq", [P, 2, C], F32), ("xb", [P, 2, C], F32)],
            [("q_all3", [P, T, C], F32), ("rows3", [128, 2, SLOTS, ROW], BF16), ("KV", [128, FD, 64], F32),
             ("KX", [128, 4, 128], F32), ("KL", [128, 2, 3, D], F32)],
            [("Wd_sb", [128, 8, NE * C], F32), ("hsT", [128, 2, 2, 512], F32), 
             ("so", [128, 2, C], F32), ("t1", [128, C], F32), ("ix", [128, 4], I32),
             ("cs", [128, 2, P], F32), ("crs", [128, 2, P], F32), ("cg", [128, 2, P], F32)])
        iota8 = sb("iota8", [P, NE])
        iota8i = sb("iota8i", [P, NE], I32)
        s128 = sb("s128", [1, ST])
        s128i = sb("s128i", [1, ST], I32)
        rexp = sb("rexp", [1, ST])
        empty = sb("empty", [128, 64], I32)
        hb = [h0, h1]
        hsb = [hs0, hs1, hs2, hs3]

        B = [bank(f"bank{i}") for i in range(8)]
        psG = [B[0], B[1]]
        psH = [3, 0]

        names = []

        def sem(name):
            names.append(name)
            return ctx.enter_context(nc.semaphore(name))

        stages = []

        def stage(name, pre=PRE):
            s = Stage(sem(name), pre)
            stages.append(s)
            return s

        x_in, w_in, e_in, c_in, late_in, wd_in = (sem(s) for s in
                                                 ("x_in", "w_in", "e_in", "c_in", "late_in", "wd_in"))
        tab_out, x1_out, h_dma, empty_out, slot_out, order_in = (sem(s) for s in (
            "tab_out", "x1_out", "h_dma", "empty_out", "slot_out", "order_in"))
        rows_in = [sem("rows_in0"), sem("rows_in1")]
        xq_in = [sem("xq_in0"), sem("xq_in1")]
        hs_in = [sem(f"hs_in{b}") for b in range(4)]
        out_done = [sem(f"out_done{b}") for b in range(4)]
        dve_chain, pool_chain, kx_ready, kx_turned, r_shifted, r_chosen, r_counts = (sem(s) for s in (
            "dve_chain", "pool_chain", "kx_ready", "kx_turned", "r_shifted", "r_chosen", "r_counts"))
        consts = sem("consts")
        waited = {k: sem(f"waited_{k}") for k in ("act", "dve", "pool", "pe")}

        (a_xn, a_tr, a_xs, a_xnT, a_mm, a_raw, a_y, a_hi, a_r1, a_mid, a_lo) = (stage(s) for s in (
            "a_xn", "a_tr", "a_xs", "a_xnT", "a_mm", "a_raw", "a_y", "a_hi", "a_r1", "a_mid", "a_lo"))
        g_idx, g_oh, g_acc = stage("g_idx"), stage("g_oh"), stage("g_acc")
        g_mm = stage("g_mm", 12)
        (k_xs, k_mm, k_qkv, k_sq, k_ss, k_mx, k_nrm, k_rc, k_rn, k_kn, k_kkv, k_kkp, k_acc) = (stage(s) for s in (
            "k_xs", "k_mm", "k_qkv", "k_sq", "k_ss", "k_mx", "k_nrm", "k_rc", "k_rn", "k_kn", "k_kkv", "k_kkp",
            "k_acc"))
        (q_qd, q_sk, q_t, q_b, q_g, q_qTs, q_f0, q_bab, q_f, q_T, q_ym, q_tq, q_nr, q_nn, q_rn, q_yev, q_pm, q_mo,
         q_xb) = (stage(s) for s in (
            "q_qd", "q_sk", "q_t", "q_b", "q_g", "q_qTs", "q_f0", "q_bab", "q_f", "q_T", "q_ym", "q_tq", "q_nr", "q_nn",
            "q_rn", "q_yev", "q_pm", "q_mo", "q_xb"))
        (c_s, c_s1, c_rs, c_gt, c_tr, c_x1) = (stage(s) for s in ("c_s", "c_s1", "c_rs", "c_gt", "c_tr", "c_x1"))
        (d_xn, d_tr, d_xs, d_mm, d_hb, d_ge, d_hout, d_ht, d_e0, d_e1, d_lm, d_lg) = (stage(s) for s in (
            "d_xn", "d_tr", "d_xs", "d_mm", "d_hb", "d_ge", "d_hout", "d_ht", "d_e0", "d_e1", "d_lm", "d_lg"))
        p_idx = stage("p_idx")
        (e_ix, e_tr, e_e0, e_e1, e_mm, e_t1, e_o, e_scd) = (stage(s) for s in (
            "e_ix", "e_tr", "e_e0", "e_e1", "e_mm", "e_t1", "e_o", "e_scd"))
        stats_v, stats_s, big_v, big_s, big_p = (sem(s) for s in ("stats_v", "stats_s", "big_v", "big_s", "big_p"))

        def pairs(e, body):
            with e.Fori(0, T // 2) as i:
                body(i * 2, 0, i)
                body(i * 2 + 1, 1, i)
            body(T - 1, 0, T // 2)

        def skewed(e, front, back):
            front(0, 0, 0)
            with e.Fori(0, T // 2) as i:
                front(i * 2 + 1, 1, i)
                back(i * 2, 0, i)
                front(i * 2 + 2, 0, i + 1)
                back(i * 2 + 1, 1, i)
            back(T - 1, 0, T // 2)

        def pipeline(e, count, unroll, *bodies):
            lead = max(l for _, l in bodies)

            def step(n, j, i):
                for body, l in bodies:
                    body(n + l, (j + l) % unroll, i + (j + l) // unroll)

            def edge(n):
                for body, l in bodies:
                    if 0 <= n + l < count:
                        body(n + l, (n + l) % unroll, (n + l) // unroll)
            for n in range(-lead, 0):
                edge(n)
            rounds = (count - lead) // unroll
            with e.Fori(0, rounds) as i:
                for j in range(unroll):
                    step(i * unroll + j, j, i)
            for n in range(rounds * unroll, count):
                edge(n)

        def row_bc(a, n, parts):
            return bass.AP(a.tensor, a.offset, [[0, parts], [1, n]])

        block = ctx.enter_context(nc.Block())

        @block.sync
        def _(sp):
            for c in range(5):
                sp.dma_start(x_all[:, 5 * c:5 * c + 5, :],
                             x[5 * c * P:5 * (c + 1) * P, :].rearrange("(t p) c -> p t c", p=P)).then_inc(x_in, 16)
            for s in stages:
                sp.sem_inc(s.sem, s.pre)
            sp.dma_start(W_sb[:, :, 0:C], W.rearrange("(k p) n -> p k n", p=128)).then_inc(w_in, 16)
            sp.dma_start(asrc_bc[:, :], row_bc(a_src, C, 128)).then_inc(w_in, 16)
            sp.dma_start(src_sb[:, :], src).then_inc(e_in, 16)
            sp.dma_start(waste[:, :], dst).then_inc(e_in, 16)
            sp.dma_start(baseb[:, :], row_bc(dst0, ET, 128)).then_inc(e_in, 16)
            sp.dma_start(base_row[:, :], row_bc(dst0, ET, 1)).then_inc(e_in, 16)
            sp.dma_start(WqkvT_sb[:, :, :], WqkvT.rearrange("(k p) n -> p k n", p=128)).then_inc(c_in, 16)
            sp.dma_start(WprojT_sb[:, :, :], WprojT.rearrange("(k p) n -> p k n", p=128)).then_inc(c_in, 16)
            sp.dma_start(bqkv_bc[:, :], row_bc(bqkv, 3 * C, P)).then_inc(c_in, 16)
            sp.dma_start(bproj_bc[:, :], row_bc(bproj, C, P)).then_inc(c_in, 16)
            sp.dma_start(temp_bc[:, :], row_bc(temp, H, P)).then_inc(c_in, 16)
            sp.dma_start(Wg_sb[:, :, :], Wg.rearrange("(k p) e -> p k e", p=128)).then_inc(c_in, 16)
            sp.dma_start(bg_bc[:, :], row_bc(bg, NE, P)).then_inc(c_in, 16)

            def table_out(t, b, i):
                sp.wait_ge(a_lo.sem, a_lo.done(t))
                sp.dma_start(table[ds(t * P, P), :], at(tb_all, t)).then_inc(tab_out, 16)
            pairs(sp, table_out)

            sp.wait_ge(k_acc.sem, k_acc.done(T - 1))
            sp.wait_ge(big_v, 1)
            def xq_load(t, b, i):
                sp.wait_ge(q_xb.sem, q_xb.ago(t, 2))
                sp.dma_start(xq[:, b, :], x[ds(t * P, P), :]).then_inc(xq_in[b], 16)
            pairs(sp, xq_load)

            sp.wait_ge(k_mm.sem, k_mm.done(T - 1))
            sp.dma_start(W1_sb[:, :, :], W1.rearrange("(k p) n -> p k n", p=128)).then_inc(late_in, 16)
            sp.dma_start(b1_bc[:, :], row_bc(b1, HID, P)).then_inc(late_in, 16)
            sp.dma_start(bd_bc[:, :], row_bc(bd, NE * C, 128)).then_inc(late_in, 16)
            sp.wait_ge(g_mm.sem, g_mm.done(ET - 1))
            sp.wait_ge(q_mo.sem, q_mo.done(T - 1))
            sp.wait_ge(q_pm.sem, q_pm.done(T - 1))
            for e in range(NE):
                sp.dma_start(Wd_sb[:, :, e * C:(e + 1) * C], Wd[e].rearrange("(k p) c -> p k c", p=128)).then_inc(wd_in, 16)

            def x1_store(t, b, i):
                sp.wait_ge(c_x1.sem, c_x1.done(t))
                sp.dma_start(hidden[ds(t * P, P), HID:HROW], at(mixo, t)).then_inc(x1_out, 16)
            pairs(sp, x1_store)

            def h_store(t, b, i):
                sp.wait_ge(d_ge.sem, d_ge.done(t * 2 + 1))
                sp.dma_start(hidden[ds(t * P, P), 0:HID], hb[b][:, :]).then_inc(h_dma, 16)
                sp.wait_ge(h_dma, t * 16 + 16)
                sp.sem_inc(d_hout.sem, 1)
            pairs(sp, h_store)

            sp.wait_ge(x1_out, 16 * T)
            sp.wait_ge(tab_out, 16 * T)
            sp.wait_ge(slot_out, 16 * T)
            sp.dma_start(order_sb[:, :, :], order[0:ST * 128, :].rearrange("(s p) c -> p s c", p=128)).then_inc(order_in, 16)

            def out_stored(s, b, i):
                sp.wait_ge(out_done[b], i * 16 + 16)
                sp.sem_inc(e_scd.sem, 1)
            pipeline(sp, ST, 4, (out_stored, 0))

        @block.gpsimd
        def _(pool):
            n = [0]

            def link(ins):
                n[0] += 1
                ins.then_inc(pool_chain, 1)
                pool.wait_ge(pool_chain, n[0])

            def gate():
                pool.sem_inc(waited["pool"], 1)

            link(pool.memset(ident[:, :], 0.0))
            link(pool.affine_select(out=ident[:, :], in_=ident[:, :], compare_op=ALU.not_equal, fill=1.0, base=0,
                                    pattern=[[-1, 128]], channel_multiplier=1))
            link(pool.iota(iota_i[:, :], pattern=[[1, 128]], base=0, channel_multiplier=0))
            link(pool.tensor_copy(iota_bf[:, :], iota_i[:, :]))
            link(pool.iota(iota8i[:, :], pattern=[[1, NE]], base=0, channel_multiplier=0))
            link(pool.tensor_copy(iota8[:, :], iota8i[:, :]))
            link(pool.iota(s128i[:, :], pattern=[[128, ST]], base=0, channel_multiplier=0))
            link(pool.tensor_copy(s128[:, :], s128i[:, :]))
            link(pool.iota(pay[:, :, 0:1], pattern=[[P, T], [1, 1]], base=0, channel_multiplier=1))
            link(pool.memset(headmask[:, :], 0.0))
            for hq in range(4):
                link(pool.memset(headmask[D * hq:D * hq + D, D * hq:D * hq + D], 1.0))
            link(pool.tensor_copy(blockones[:, :], headmask[:, :]))
            link(pool.iota(head_i[:, :, :], pattern=[[4, 2], [1, 4], [0, D]], base=0, channel_multiplier=-1))
            link(pool.tensor_copy(head_f[:, 0, :, :], head_i[:, :, :]))
            link(pool.tensor_scalar(headsel[:, :, :], head_f[:, 0, :, :], 0.0, None, ALU.is_equal))
            for s in (1, 2):
                link(pool.tensor_scalar(head_f[:, 1, :, :], head_f[:, 0, :, :], -8.0 * s, None, ALU.is_equal))
                link(pool.tensor_tensor(headsel[:, :, :], headsel[:, :, :], head_f[:, 1, :, :], ALU.add))
            link(pool.memset(rones[:, :], 1.0))
            link(pool.affine_select(out=rtri[:, :], in_=rones[:, :], compare_op=ALU.is_gt, fill=0.0, base=0,
                                    pattern=[[1, P]], channel_multiplier=-1))
            link(pool.memset(empty[:, :], 0))
            link(pool.memset(over(empty[:, :], 128, 0, [[2, 32]]), NOBODY))
            link(pool.memset(Mdiag[:, :, :], 0.0))
            link(pool.memset(Mlin[:, :, :], 0.0))
            pool.memset(pay[:, :, 1:2], 0).then_inc(consts, 1)
            pool.dma_start(order.rearrange("(p s) c -> p (s c)", p=128), empty[:, 0:64]).then_inc(empty_out, 16)

            def keep_xnT(t, b, i):
                pool.wait_ge(a_xs.sem, a_xs.done(t))
                gate()
                pool.tensor_copy(xnT_all[:, :, ds(t * P, P)], xs[:, b, :, :]).then_inc(a_xnT.sem, 1)
            pairs(pool, keep_xnT)

            pool.wait_ge(big_v, 2)
            pool.partition_all_reduce(hmaxall[:, :], hmax[:, :], P, bass.bass_isa.ReduceOp.max).then_inc(big_p, 1)

            pool.wait_ge(tab_out, 16 * T)
            pool.wait_ge(e_in, 64)

            def gather(u, s, g):
                pool.wait_ge(g_mm.sem, u * 8 + (g_mm.pre - 8))
                gate()
                pool.tensor_copy(iidx[:, s, :], src_sb[:, ds(u * SLOTS, SLOTS)]).then_inc(g_idx.sem, 1)
                pool.wait_ge(g_idx.sem, g_idx.done(u))
                gate()
                for j in range(SLOTS):
                    pool.indirect_dma_start(out=rows[:, s, j, :], out_offset=None, in_=table,
                                            in_offset=bass.IndirectOffsetOnAxis(ap=iidx[:, s, j:j + 1], axis=0)
                                            ).then_inc(rows_in[s], 16)

            with pool.Fori(0, ET // (2 * SLOTS)) as g:
                gather(g * 2, 0, g)
                gather(g * 2 + 1, 1, g)

            def k_features(t, b, i):
                pool.wait_ge(k_acc.sem, k_acc.ago(t, 1))
                pool.wait_ge(k_kn.sem, k_kn.done(t))
                pool.tensor_tensor(over(kkx[:, :, :], P, KK_DVE * KROW, [[KROW, H - KK_DVE], [D, FD], [1, D]]),
                                   over(kd[:, :, :], P, KK_DVE * 48, [[48, H - KK_DVE], [0, FD], [1, D]]),
                                   over(kd[:, :, :], P, KK_DVE * 48, [[48, H - KK_DVE], [1, FD], [1, D]]),
                                   ALU.mult)
                pool.tensor_copy(over(kc[:, :], P, 0, [[D, H], [1, D]]), kd[:, :, 0:D]).then_inc(k_kkp.sem, 1)
            pairs(pool, k_features)

            def residual(t, b, i):
                pool.wait_ge(q_b.sem, q_b.ago(t * 2, 1))
                pool.wait_ge(q_qd.sem, q_qd.done(t))
                gate()
                pool.tensor_copy(over(qsk[:, :, :], P, 0, [[128, H], [D, 4], [1, D]]),
                                 over(qper[:, :, :], P, 0, [[144, H], [1, 4], [1, D]])).then_inc(q_sk.sem, 1)
                pool.wait_ge(xq_in[b], i * 16 + 16)
                pool.wait_ge(q_mo.sem, q_mo.ago(t, 2))
                pool.tensor_tensor(xb[:, b, :], xq[:, b, :], bproj_bc[:, :], ALU.add).then_inc(q_xb.sem, 1)
            pool.wait_ge(c_in, 112)
            pool.wait_ge(big_v, 5)
            pairs(pool, residual)

            pool.wait_ge(empty_out, 16)
            pool.wait_ge(big_v, 6)
            with pool.Fori(0, T // 5) as i:
                pool.tensor_copy(slot_st[:, :], slot_i[:, ds(i * 5, 5)])
                pool.tensor_copy(pay_st[:, :, :], pay[:, ds(i * 5, 5), :]).then_inc(p_idx.sem, 1)
                pool.wait_ge(p_idx.sem, p_idx.done(i))
                gate()
                for j in range(5):
                    pool.indirect_dma_start(out=order, out_offset=bass.IndirectOffsetOnAxis(ap=slot_st[:, j:j + 1], axis=0),
                                            in_=pay_st[:, j, :], in_offset=None).then_inc(slot_out, 16)
                pool.wait_ge(slot_out, i * 80 + 80)
                gate()

            pool.wait_ge(order_in, 16)
            pool.wait_ge(d_hout.sem, d_hout.done(T - 1))
            pool.wait_ge(x1_out, 16 * T)
            pool.wait_ge(big_v, 7)

            def fetch(s, b, i):
                pool.wait_ge(e_o.sem, e_o.ago(s, 4))
                pool.wait_ge(e_scd.sem, e_scd.ago(s, 4))
                gate()
                pool.tensor_copy(ix[:, b:b + 1], at(order_sb, s, 0, 1)).then_inc(e_ix.sem, 1)
                pool.wait_ge(e_ix.sem, e_ix.done(s))
                gate()
                pool.indirect_dma_start(out=hsb[b][:, :], out_offset=None, in_=hidden,
                                        in_offset=bass.IndirectOffsetOnAxis(ap=ix[:, b:b + 1], axis=0),
                                        bounds_check=N - 1, oob_is_err=False).then_inc(hs_in[b], 16)

            def put(s, b, i):
                pool.wait_ge(e_o.sem, e_o.done(s))
                gate()
                pool.indirect_dma_start(out=out, out_offset=bass.IndirectOffsetOnAxis(ap=ix[:, b:b + 1], axis=0),
                                        in_=so[:, b % 2, :], in_offset=None, bounds_check=N - 1,
                                        oob_is_err=False).then_inc(out_done[b], 16)
            pipeline(pool, ST, 4, (fetch, 3), (put, 0))

        @block.scalar
        def _(act):
            def gate():
                act.sem_inc(waited["act"], 1)

            act.wait_ge(stats_v, 1)
            act.activation(rstd[:, :], var[:, :], ACT.Sqrt).then_inc(stats_s, 1)

            def keep(t, b, i):
                act.wait_ge(a_tr.sem, a_tr.done(t))
                act.wait_ge(a_mm.sem, a_mm.ago(t, 2))
                act.wait_ge(a_xnT.sem, a_xnT.ago(t, 2))
                act.activation(xs[:, b, :, :], over(B[2 + b][:, :], 128, 0, [[P, 2], [1, P]]), ACT.Copy).then_inc(a_xs.sem, 1)

            def raw(t, b, i):
                act.wait_ge(a_mm.sem, a_mm.done(t))
                gate()
                act.activation(at(raw_all, t), B[4 + b][0:P, 0:XW], ACT.Copy).then_inc(a_raw.sem, 1)
            skewed(act, keep, raw)

            act.wait_ge(big_v, 3)
            act.activation(raw_all[:, :, C:XW], raw_all[:, :, C:XW], ACT.Exp).then_inc(big_s, 1)

            def parts(t, b, i):
                act.wait_ge(a_y.sem, a_y.done(t))
                gate()
                act.activation(at(tb_all, t, 0, C), yw[:, b, :], ACT.Copy).then_inc(a_hi.sem, 1)
                act.wait_ge(a_r1.sem, a_r1.done(t))
                gate()
                act.activation(at(tb_all, t, C, 2 * C), y1[:, b, :], ACT.Copy).then_inc(a_mid.sem, 1)
            pairs(act, parts)

            def k_stage(t, b, i):
                act.wait_ge(k_mm.sem, k_mm.ago(t, 2))
                gate()
                act.activation(kxs[:, b, :, :], xnT_all[:, :, ds(t * P, P)], ACT.Copy).then_inc(k_xs.sem, 1)

            def k_norm(t, b, i):
                act.wait_ge(k_qkv.sem, k_qkv.done(t))
                act.wait_ge(k_ss.sem, k_ss.ago(t, 1))
                act.activation(sq[:, :], qkv[:, 0:2 * C], ACT.Square).then_inc(k_sq.sem, 1)
                act.wait_ge(k_mx.sem, k_mx.done(t))
                act.wait_ge(k_rc.sem, k_rc.ago(t, 1))
                act.activation(nrm[:, :], ss2[:, :], ACT.Sqrt).then_inc(k_nrm.sem, 1)
            act.wait_ge(tab_out, 16 * T)
            act.wait_ge(a_xnT.sem, a_xnT.done(T - 1))
            skewed(act, k_stage, k_norm)

            act.wait_ge(big_v, 5)

            def q_tile(t, b, i):
                act.wait_ge(q_g.sem, q_g.ago(t * 8, 1))
                act.wait_ge(q_sk.sem, q_sk.ago(t, 1))
                gate()
                act.activation(qs[:, :], at(q_all, t), ACT.Copy)
                act.activation(over(qper[:, :, :], P, 0, [[144, H], [D, 4], [1, D]]),
                               over(at(q_all, t), P, 0, [[D, H], [0, 4], [1, D]]), ACT.Copy)
                act.activation(qper[:, :, 128:144], over(at(q_all, t), P, 0, [[D, H], [1, 16]]), ACT.Copy).then_inc(q_qd.sem, 1)
                act.wait_ge(q_t.sem, q_t.done(t))
                act.wait_ge(q_ym.sem, q_ym.ago(t, 1))
                act.wait_ge(q_tq.sem, q_tq.ago(t, 1))
                act.activation(qT[:, :, :], over(B[5][:, :], 128, 0, [[P, 2], [1, P]]), ACT.Copy).then_inc(q_qTs.sem, 1)
                act.activation(F0[:, :, :], over(B[5][:, :], 128, 0, [[P, 2], [1, P]]), ACT.Square).then_inc(q_f0.sem, 1)
                for hf in range(2):
                    act.wait_ge(q_b.sem, q_b.done(t * 2 + hf))
                    act.wait_ge(q_f.sem, q_f.ago(t * 8 + 4 * hf, 5))
                    act.activation(bab[:, 4 * hf:4 * hf + 4, :], over(B[4][:, :], 128, 0, [[P, 4], [1, P]]),
                                   ACT.Copy).then_inc(q_bab.sem, 1)
            pairs(act, q_tile)

            act.wait_ge(stats_v, 2)
            act.activation(rstd[:, :], var[:, :], ACT.Sqrt).then_inc(stats_s, 1)

            def d_keep(t, b, i):
                act.wait_ge(d_tr.sem, d_tr.done(t))
                act.wait_ge(d_mm.sem, d_mm.ago(t * 2, 3))
                act.activation(dxs[:, b, :, :], over(B[2][:, :], 128, 0, [[P, 2], [1, P]]), ACT.Copy).then_inc(d_xs.sem, 1)

            def d_gelu(t, b, i):
                act.wait_ge(d_hout.sem, d_hout.ago(t, 2))
                act.wait_ge(d_ht.sem, d_ht.ago(t * 2, 3))
                for hf in range(2):
                    act.wait_ge(d_hb.sem, d_hb.done(t * 2 + hf))
                    act.activation(hb[b][:, 512 * hf:512 * hf + 512], hp[:, b, 512 * hf:512 * hf + 512],
                                   ACT.Gelu).then_inc(d_ge.sem, 1)

            def d_evac(t, b, i):
                act.wait_ge(d_ht.sem, d_ht.done(t * 2 + 1))
                act.wait_ge(d_lm.sem, d_lm.ago(t, 1))
                act.activation(hT[:, 4:8, :], over(B[6][:, :], 128, 0, [[P, 4], [1, P]]), ACT.Copy).then_inc(d_e1.sem, 1)
            pipeline(act, T, 2, (d_keep, 3), (d_gelu, 2), (d_evac, 1))

            act.wait_ge(r_shifted, 1)
            act.activation(ex[:, :, :], r_a[:, :, :], ACT.Exp).then_inc(big_s, 1)

            def e_evac(s, b, i):
                act.wait_ge(e_tr.sem, e_tr.done(s * 2 + 1))
                act.wait_ge(e_mm.sem, e_mm.ago(s, 2))
                act.activation(hsT[:, b, 1, :], B[5 + 2 * b][:, :], ACT.Copy).then_inc(e_e1.sem, 1)
            pipeline(act, ST, 2, (e_evac, 0))

        @block.vector
        def _(dve):
            n = [0]

            def link(ins):
                n[0] += 1
                ins.then_inc(dve_chain, 1)
                dve.wait_ge(dve_chain, n[0])

            def gate():
                dve.sem_inc(waited["dve"], 1)

            def layer_norm_stats(k):
                def col(c):
                    return st_all[:, :, c:c + 1].rearrange("p t o -> p (t o)")
                link(dve.memset(delta[:, :], 0.0))
                link(dve.tensor_tensor(mean[:, :], col(1), col(4), ALU.add))
                link(dve.tensor_tensor(delta[:, :], col(1), col(4), ALU.subtract))
                link(dve.tensor_tensor(var[:, :], col(2), col(5), ALU.add))
                link(dve.scalar_tensor_tensor(nmr[:, :], delta[:, :], 0.25, delta[:, :], ALU.mult, ALU.mult))
                link(dve.scalar_tensor_tensor(var[:, :], var[:, :], 1.0 / C, nmr[:, :], ALU.mult, ALU.add))
                dve.tensor_scalar(var[:, :], var[:, :], LN_EPS, None, ALU.add).then_inc(stats_v, 1)
                dve.wait_ge(stats_s, k)
                link(dve.reciprocal(delta[:, :], rstd[:, :]))
                link(dve.tensor_copy(rstd[:, :], delta[:, :]))
                link(dve.scalar_tensor_tensor(nmr[:, :], mean[:, :], -0.5, rstd[:, :], ALU.mult, ALU.mult))

            dve.wait_ge(x_in, 80)
            with dve.Fori(0, T) as t:
                dve.bn_stats(at(st_all, t), at(x_all, t))
            link(dve.memset(normeps[:, H:], 1e-24))
            layer_norm_stats(1)
            dve.wait_ge(w_in, 32)
            link(dve.tensor_tensor(wa_prod[:, :, :], W_sb[:, :, 0:C], over(asrc_bc[:, :], 128, 0, [[0, 2], [1, C]]), ALU.mult))
            for k in range(2):
                link(dve.tensor_reduce(W_sb[:, k, C:XW], over(wa_prod[:, :, :], 128, k * C, [[D, H], [1, D]]), AX.X, ALU.add))
            dve.memset(normeps[:, 0:H], (1e-12 / SCALE) ** 2).then_inc(big_v, 1)

            def normalise(t, b, i):
                dve.wait_ge(a_tr.sem, a_tr.ago(t, 2))
                dve.tensor_scalar(xn[:, b, :], at(x_all, t), rstd[:, ds(t, 1)], nmr[:, ds(t, 1)],
                                  ALU.mult, ALU.add).then_inc(a_xn.sem, 1)
            pairs(dve, normalise)

            dve.wait_ge(e_in, 64)
            link(dve.tensor_tensor(dloc[:, :], waste[:, :], baseb[:, :], ALU.subtract))
            dve.wait_ge(a_raw.sem, a_raw.done(T - 1))
            dve.tensor_reduce(hmax[:, :], raw_all[:, :, C:XW].rearrange("p t h -> p h t"), AX.X, ALU.max).then_inc(big_v, 1)
            dve.wait_ge(big_p, 1)
            dve.tensor_tensor(raw_all[:, :, C:XW], raw_all[:, :, C:XW], over(hmaxall[:, :], P, 0, [[0, T], [1, H]]),
                              ALU.subtract).then_inc(big_v, 1)
            dve.wait_ge(big_s, 1)
            w0, wp = raw_all[:, :, C:XW], [tb_all[:, :, 3 * C + H * k:3 * C + H * k + H] for k in range(3)]
            link(dve.tensor_copy(wp[0], w0))
            link(dve.tensor_tensor(w1[:, :, :], w0, wp[0], ALU.subtract))
            link(dve.tensor_copy(wp[1], w1[:, :, :]))
            link(dve.tensor_tensor(wp[2], w1[:, :, :], wp[1], ALU.subtract))

            def weigh(t, b, i):
                dve.wait_ge(a_lo.sem, a_lo.ago(t, 2))
                dve.tensor_tensor(over(yw[:, b, :], P, 0, [[D, H], [1, D]]),
                                  over(at(raw_all, t), P, 0, [[D, H], [1, D]]),
                                  over(at(raw_all, t), P, C, [[1, H], [0, D]]), ALU.mult).then_inc(a_y.sem, 1)
                dve.wait_ge(a_hi.sem, a_hi.done(t))
                dve.tensor_tensor(y1[:, b, :], yw[:, b, :], at(tb_all, t, 0, C), ALU.subtract).then_inc(a_r1.sem, 1)
                dve.wait_ge(a_mid.sem, a_mid.done(t))
                dve.tensor_tensor(at(tb_all, t, 2 * C, 3 * C), y1[:, b, :], at(tb_all, t, C, 2 * C),
                                  ALU.subtract).then_inc(a_lo.sem, 1)
            pairs(dve, weigh)

            dve.wait_ge(tab_out, 16 * T)
            dve.wait_ge(consts, 1)
            dve.memset(acc[:, :, :], 0.0)
            dve.memset(wsum[:, :], 0.0).then_inc(big_v, 1)
            dve.wait_ge(big_v, 4)

            def make_onehot(m, j):
                dve.wait_ge(g_mm.sem, g_mm.ago(m, 4))
                dve.tensor_scalar(onehot[:, j % 4, :], iota_bf[:, :], dloc[:, ds(m, 1)], None, ALU.is_equal).then_inc(g_oh.sem, 1)

            def add_tile(m, j):
                first = dve.value_load(base_row[0:1, ds(m, 1)], min_val=0, max_val=N - 1)
                dve.wait_ge(g_mm.sem, g_mm.done(m))
                dve.wait_ge(g_acc.sem, g_acc.ago(m, 1))
                dve.tensor_tensor(acc[:, :, ds(first, EP)], acc[:, :, ds(first, EP)],
                                  over(psG[j % 2][:, :], 128, 0, [[EP, 2], [1, EP]]), ALU.add)
                dve.tensor_tensor(wsum[:, ds(first, EP)], wsum[:, ds(first, EP)], psG[j % 2][0:24, 2 * EP:3 * EP],
                                  ALU.add).then_inc(g_acc.sem, 1)

            make_onehot(0, 0)
            make_onehot(1, 1)
            with dve.Fori(0, ET // 4 - 1) as g:
                for j in range(4):
                    make_onehot(g * 4 + j + 2, j + 2)
                    add_tile(g * 4 + j, j)
            for j in range(4):
                if j < 2:
                    make_onehot(ET - 4 + j + 2, j + 2)
                add_tile(ET - 4 + j, j)

            dve.wait_ge(c_in, 112)
            link(dve.tensor_scalar(normfac[:, 0:H], temp_bc[:, :], SCALE, None, ALU.mult))
            link(dve.memset(normfac[:, H:], SCALE))
            link(dve.memset(kkx[:, :, KW + D:KROW], 1.0))

            def k_bias(t, b, i):
                dve.wait_ge(k_mm.sem, k_mm.done(t))
                dve.wait_ge(k_acc.sem, k_acc.ago(t, 1))
                dve.wait_ge(k_kn.sem, k_kn.ago(t, 1))
                dve.tensor_tensor(qkv[:, 0:512], B[2][0:P, :], bqkv_bc[:, 0:512], ALU.add)
                dve.tensor_tensor(qkv[:, 512:768], B[3][0:P, 0:C], bqkv_bc[:, 512:768], ALU.add).then_inc(k_qkv.sem, 1)
                dve.wait_ge(k_sq.sem, k_sq.done(t))
                dve.wait_ge(k_mx.sem, k_mx.ago(t, 1))
                dve.tensor_reduce(ss[:, :], sq[:, :].rearrange("p (a d) -> p a d", d=D), AX.X, ALU.add).then_inc(k_ss.sem, 1)
                dve.wait_ge(k_ss.sem, k_ss.done(t))
                dve.wait_ge(k_nrm.sem, k_nrm.ago(t, 1))
                dve.tensor_tensor(ss2[:, :], ss[:, :], normeps[:, :], ALU.max).then_inc(k_mx.sem, 1)
                dve.wait_ge(k_nrm.sem, k_nrm.done(t))
                dve.reciprocal(rcp[:, :], nrm[:, :]).then_inc(k_rc.sem, 1)
                dve.wait_ge(k_rc.sem, k_rc.done(t))
                dve.tensor_tensor(rn[:, :], rcp[:, :], normfac[:, :], ALU.mult).then_inc(k_rn.sem, 1)
                dve.wait_ge(k_rn.sem, k_rn.done(t))
                dve.wait_ge(k_kkp.sem, k_kkp.ago(t, 1))
                dve.wait_ge(k_kkv.sem, k_kkv.ago(t, 1))
                dve.tensor_tensor(over(at(q_all, t), P, 0, [[D, H], [1, D]]),
                                  over(qkv[:, :], P, 0, [[D, H], [1, D]]), over(rn[:, :], P, 0, [[1, H], [0, D]]), ALU.mult)
                k_in = over(qkv[:, :], P, C, [[D, H], [1, D]])
                k_rnb = over(rn[:, :], P, H, [[1, H], [0, D]])
                dve.tensor_tensor(kkx[:, :, KW:KW + D], k_in, k_rnb, ALU.mult)
                dve.tensor_tensor(kd[:, :, 0:D], k_in, k_rnb, ALU.mult)
                dve.tensor_tensor(kd[:, :, D:48], over(qkv[:, :], P, C, [[D, H], [1, 16]]),
                                  over(rn[:, :], P, H, [[1, H], [0, 16]]), ALU.mult).then_inc(k_kn.sem, 1)
                dve.wait_ge(k_kn.sem, k_kn.done(t))
                dve.tensor_tensor(over(kkx[:, :, :], P, 0, [[KROW, KK_DVE], [D, FD], [1, D]]),
                                  over(kd[:, :, :], P, 0, [[48, KK_DVE], [0, FD], [1, D]]),
                                  over(kd[:, :, :], P, 0, [[48, KK_DVE], [1, FD], [1, D]]), ALU.mult).then_inc(k_kkv.sem, 1)
            pairs(dve, k_bias)

            for g in range(2):
                dve.wait_ge(k_acc.sem, k_acc.done(T - 1))
                accA, accC = B[4 + g], B[6]
                for dd, nd, f in ((0, 1, 0.5 / N), (1, 15, 1.0 / N), (16, 1, 0.5 / N)):
                    srcA = over(accA[:, :], 128, dd * D, [[D, nd], [1, D]]) if dd < 16 else over(accC[:, :], 128, 66 * g, [[D, 1], [1, D]])
                    for half in range(2):
                        link(dve.tensor_scalar(over(KV[:, :, :], 128, dd * 64 + 32 * half, [[64, nd], [1, D]]), srcA, f, None, ALU.mult))
                link(dve.tensor_scalar(KL[:, g, 0, :], accC[:, 66 * g + D:66 * g + 2 * D], SCALE ** 2 / N, None, ALU.mult))
                link(dve.tensor_scalar(vsum[:, g:g + 1], accC[:, 66 * g + 2 * D:66 * g + 2 * D + 1], SCALE ** 4 / N, None, ALU.mult))
                for G in range(4):
                    for r in range(4):
                        link(dve.tensor_copy(KX[:, G, D * r:D * r + D], KV[:, 4 * (G + 1) - r, r:r + D]))
                dve.sem_inc(kx_ready, 1)
                link(dve.transpose(KL[:, g, 2, :], KV[:, 0, 0:D]))
                for hq in range(4):
                    link(dve.tensor_copy(Mdiag[D * hq:D * hq + D, g, D * hq:D * hq + D], KL[D * hq:D * hq + D, g, 2, :]))
                link(dve.transpose(KL[:, g, 1, :], KL[:, g, 0, :]))
                for hq in range(4):
                    link(dve.tensor_copy(Mlin[D * hq:D * hq + D, g, D * hq:D * hq + D], KL[D * hq:D * hq + D, g, 1, :]))
                link(dve.scalar_tensor_tensor(Mgram[:, g, :], accC[:, 132 + 129 * g:132 + 129 * g + 128], 0.5 / N,
                                              headmask[:, :], ALU.mult, ALU.mult))
                link(dve.tensor_scalar(ksum[:, g:g + 1], accC[:, 132 + 129 * g + 128:132 + 129 * g + 129], SCALE ** 2 / N, None, ALU.mult))
                dve.wait_ge(kx_turned, g + 1)
                link(dve.tensor_copy(Mpair[:, g, :, :], over(B[2][:, :], 128, 0, [[128, 4], [1, 128]])))
            dve.sem_inc(big_v, 1)

            def q_feat(t, b, i):
                dve.wait_ge(q_ym.sem, q_ym.ago(t, 1))
                for h in range(H):
                    dve.wait_ge(q_g.sem, q_g.done(t * 8 + h))
                    dve.wait_ge(q_bab.sem, q_bab.done(t * 2 + h // 4))
                    dve.tensor_tensor(F[:, h, :, :], over(B[2 + h % 2][:, :], 128, 0, [[P, 4], [1, P]]),
                                      over(bab[:, h, :], 128, 0, [[0, 4], [1, P]]), ALU.mult).then_inc(q_f.sem, 1)
                    if h == 3:
                        dve.wait_ge(q_T.sem, q_T.done(t))
                        dve.wait_ge(q_nr.sem, q_nr.ago(t, 1))
                        for g in range(2):
                            ins = dve.scalar_tensor_tensor(TQ[:, g, :], B[6][:, (2 + g) * P:(3 + g) * P], ksum[:, g:g + 1],
                                                           qT[:, g, :], ALU.add, ALU.mult)
                        ins.then_inc(q_tq.sem, 1)
                dve.wait_ge(q_nr.sem, q_nr.done(t))
                dve.wait_ge(q_rn.sem, q_rn.ago(t, 1))
                dve.tensor_scalar(nn[:, :, :], over(B[5][:, :], 128, 2 * P, [[P, 2], [1, P]]), SCALE ** 4, None,
                                  ALU.add).then_inc(q_nn.sem, 1)
                dve.wait_ge(q_nn.sem, q_nn.done(t))
                dve.wait_ge(q_yev.sem, q_yev.ago(t, 1))
                dve.reciprocal(rnn[:, :, :], nn[:, :, :]).then_inc(q_rn.sem, 1)
                dve.wait_ge(q_rn.sem, q_rn.done(t))
                dve.wait_ge(q_ym.sem, q_ym.done(t))
                dve.wait_ge(q_pm.sem, q_pm.ago(t, 1))
                for g in range(2):
                    ins = dve.scalar_tensor_tensor(yT[:, g, :], B[6][:, g * P:(g + 1) * P], vsum[:, g:g + 1],
                                                   rnn[:, g, :], ALU.add, ALU.mult)
                ins.then_inc(q_yev.sem, 1)
                dve.wait_ge(q_pm.sem, q_pm.done(t))
                dve.wait_ge(q_xb.sem, q_xb.done(t))
                dve.tensor_tensor(at(mixo, t), B[7][0:P, 0:C], xb[:, b, :], ALU.add).then_inc(q_mo.sem, 1)
            pairs(dve, q_feat)

            def c_tile(t, b, i):
                dve.wait_ge(c_s.sem, c_s.done(t))
                dve.wait_ge(c_rs.sem, c_rs.ago(t, 1))
                dve.tensor_scalar(cs[:, :, :], over(B[2][:, :], 128, 0, [[P, 2], [1, P]]), 1e-16, None, ALU.add).then_inc(c_s1.sem, 1)
                dve.wait_ge(c_s1.sem, c_s1.done(t))
                dve.wait_ge(c_gt.sem, c_gt.ago(t, 1))
                dve.reciprocal(crs[:, :, :], cs[:, :, :]).then_inc(c_rs.sem, 1)
                dve.wait_ge(c_rs.sem, c_rs.done(t))
                dve.wait_ge(c_tr.sem, c_tr.ago(t, 1))
                dve.tensor_tensor(cg[:, :, :], acc[:, :, ds(t * P, P)], crs[:, :, :], ALU.mult).then_inc(c_gt.sem, 1)
                dve.wait_ge(c_tr.sem, c_tr.done(t))
                dve.tensor_tensor(at(mixo, t), B[3][0:P, 0:C], at(mixo, t), ALU.add).then_inc(c_x1.sem, 1)
                dve.wait_ge(c_x1.sem, c_x1.done(t))
                gate()
                dve.bn_stats(at(st_all, t), at(mixo, t))
            dve.wait_ge(g_acc.sem, g_acc.done(ET - 1))
            dve.wait_ge(q_mo.sem, q_mo.done(T - 1))
            pairs(dve, c_tile)
            layer_norm_stats(2)

            dve.wait_ge(late_in, 48)
            dve.wait_ge(c_gt.sem, c_gt.done(T - 1))

            def d_norm(t, b, i):
                dve.wait_ge(d_tr.sem, d_tr.ago(t, 2))
                dve.tensor_scalar(dxn[:, b, :], at(mixo, t), rstd[:, ds(t, 1)], nmr[:, ds(t, 1)],
                                  ALU.mult, ALU.add).then_inc(d_xn.sem, 1)

            def d_bias(t, b, i):
                for hf in range(2):
                    dve.wait_ge(d_mm.sem, d_mm.done(t * 2 + hf))
                    dve.wait_ge(d_ge.sem, d_ge.ago(t * 2 + hf, 4))
                    dve.tensor_tensor(hp[:, b, 512 * hf:512 * hf + 512], B[psH[b] + hf][0:P, :],
                                      b1_bc[:, 512 * hf:512 * hf + 512], ALU.add).then_inc(d_hb.sem, 1)

            def d_evac(t, b, i):
                dve.wait_ge(d_ht.sem, d_ht.done(t * 2))
                dve.wait_ge(d_lm.sem, d_lm.ago(t, 1))
                dve.tensor_copy(hT[:, 0:4, :], over(B[5][:, :], 128, 0, [[P, 4], [1, P]])).then_inc(d_e0.sem, 1)

            def d_logits(t, b, i):
                dve.wait_ge(d_lm.sem, d_lm.done(t))
                dve.tensor_tensor(at(lg_all, t), B[7][0:P, 0:NE], bg_bc[:, :], ALU.add).then_inc(d_lg.sem, 1)
            pipeline(dve, T, 2, (d_norm, 4), (d_bias, 2), (d_logits, 0), (d_evac, 1))

            dve.wait_ge(d_lg.sem, d_lg.done(T - 1))
            link(dve.tensor_reduce(r_e[:, :], lg_all[:, :, :], AX.X, ALU.max))
            link(dve.tensor_tensor(r_a[:, :, :], lg_all[:, :, :], over(r_e[:, :], P, 0, [[1, T], [0, NE]]), ALU.subtract))
            dve.sem_inc(r_shifted, 1)
            dve.wait_ge(big_s, 2)
            link(dve.tensor_reduce(r_e[:, :], ex[:, :, :], AX.X, ALU.add))
            link(dve.reciprocal(prob[:, :], r_e[:, :]))
            link(dve.tensor_copy(over(pay[:, :, :], P, 1, [[2, T]]).bitcast(F32), prob[:, :]))
            link(dve.tensor_scalar(r_a[:, :, :], ex[:, :, :], 1.0, -8.0, ALU.is_ge, ALU.mult))
            link(dve.tensor_tensor(r_b[:, :, :], r_a[:, :, :], over(iota8[:, :], P, 0, [[0, T], [1, NE]]), ALU.add))
            link(dve.tensor_reduce(r_e[:, :], r_b[:, :, :], AX.X, ALU.min))
            link(dve.tensor_tensor(r_a[:, :, :], r_b[:, :, :], over(r_e[:, :], P, 0, [[1, T], [0, NE]]), ALU.is_equal))
            dve.sem_inc(r_chosen, 1)
            dve.wait_ge(r_counts, 1)
            link(dve.tensor_copy(r_c[:, :, :], over(B[3][:, :], P, 0, [[1, NE], [NE, T]])))
            for e in range(NE):
                link(dve.tensor_tensor_scan(r_d[:, e, :], rones[:, 0:T], r_c[:, e, :], 0.0, ALU.mult, ALU.add))
            link(dve.tensor_scalar(r_g[:, :], over(r_d[:, :, :], P, T - 1, [[T, NE]]), 127.0, None, ALU.add))
            link(dve.tensor_scalar(r_g[:, :], r_g[:, :], 7, 7, ALU.arith_shift_right, ALU.arith_shift_left))
            link(dve.tensor_copy(r_f[:, :], r_g[:, :]))
            link(dve.tensor_tensor_scan(r_h[:, :], rones[:, 0:NE], r_f[:, :], 0.0, ALU.mult, ALU.add))
            link(dve.tensor_tensor(r_f[:, :], r_h[:, :], r_f[:, :], ALU.subtract))
            link(dve.tensor_tensor(r_c[:, :, :], r_d[:, :, :], r_c[:, :, :], ALU.subtract))
            link(dve.tensor_tensor(r_b[:, :, :], over(B[2][:, :], P, 0, [[NE, T], [1, NE]]),
                                   over(r_c[:, :, :], P, 0, [[1, T], [T, NE]]), ALU.add))
            link(dve.tensor_tensor(r_b[:, :, :], r_b[:, :, :], over(r_f[:, :], P, 0, [[0, T], [1, NE]]), ALU.add))
            link(dve.tensor_tensor(r_b[:, :, :], r_b[:, :, :], r_a[:, :, :], ALU.mult))
            link(dve.tensor_reduce(r_e[:, :], r_b[:, :, :], AX.X, ALU.add))
            link(dve.tensor_copy(slot_i[:, :], r_e[:, :]))
            dve.sem_inc(big_v, 1)
            link(dve.tensor_tensor(ev32[:, :, :], over(s128[:, :], 1, 0, [[1, ST], [0, NE]]),
                                   over(r_h[:, :], 1, 0, [[0, ST], [1, NE]]), ALU.is_ge))
            link(dve.tensor_reduce(rexp[:, :], ev32[:, :, :], AX.X, ALU.add))
            link(dve.tensor_scalar(rexp[:, :], rexp[:, :], float(NE - 1), float(C), ALU.min, ALU.mult))
            link(dve.tensor_copy(experts_i[:, :], rexp[:, :]))
            dve.wait_ge(d_hout.sem, d_hout.done(T - 1))
            for b in range(4):
                link(dve.memset(hsb[b][:, :], 0.0))
            dve.sem_inc(big_v, 1)

            dve.wait_ge(order_in, 16)

            def e_evac(s, b, i):
                dve.wait_ge(e_tr.sem, e_tr.done(s * 2))
                dve.wait_ge(e_mm.sem, e_mm.ago(s, 2))
                dve.tensor_copy(hsT[:, b % 2, 0, :], B[4 + 2 * (b % 2)][:, :]).then_inc(e_e0.sem, 1)

            def e_out(s, b, i):
                col = dve.value_load(experts_i[0:1, ds(s, 1)], min_val=0, max_val=(NE - 1) * C)
                dve.wait_ge(e_mm.sem, e_mm.done(s))
                dve.wait_ge(e_o.sem, e_o.ago(s, 1))
                dve.tensor_tensor(t1[:, :], B[2 + b % 2][:, 0:C], bd_bc[:, ds(col, C)], ALU.add).then_inc(e_t1.sem, 1)
                dve.wait_ge(e_scd.sem, e_scd.ago(s, 2))
                dve.wait_ge(e_t1.sem, e_t1.done(s))
                dve.scalar_tensor_tensor(so[:, b % 2, :], t1[:, :], at(order_sb, s, 1, 2).bitcast(F32), hsb[b][:, HID:HROW],
                                         ALU.mult, ALU.add).then_inc(e_o.sem, 1)
            pipeline(dve, ST, 4, (e_evac, 1), (e_out, 0))

        @block.tensor
        def _(pe):
            pe.wait_ge(pool_chain, 2)
            pe.wait_ge(big_v, 1)

            def a_front(t, b, i):
                pe.wait_ge(a_xn.sem, a_xn.done(t))
                pe.wait_ge(a_xs.sem, a_xs.ago(t, 2))
                for k in range(2):
                    ins = pe.transpose(B[2 + b][:, k * P:(k + 1) * P], xn[:, b, 128 * k:128 * k + 128], ident[0:P, 0:P])
                ins.then_inc(a_tr.sem, 1)

            def a_back(t, b, i):
                pe.wait_ge(a_xs.sem, a_xs.done(t))
                pe.wait_ge(a_raw.sem, a_raw.ago(t, 2))
                for k in range(2):
                    ins = pe.matmul(B[4 + b][0:P, 0:XW], xs[:, b, k, :], W_sb[:, k, :], start=(k == 0), stop=(k == 1))
                ins.then_inc(a_mm.sem, 1)
            skewed(pe, a_front, a_back)

            def edge_tile(m, j):
                s = j // SLOTS
                pe.wait_ge(g_oh.sem, g_oh.done(m))
                pe.wait_ge(g_acc.sem, g_acc.ago(m, 2))
                ps = psG[j % 2]
                for c in range(2):
                    for part in range(3):
                        pe.matmul(ps[:, EP * c:EP * c + EP], rows[:, s, j % SLOTS, part * C + 128 * c:part * C + 128 * c + 128],
                                  onehot[:, j % 4, :], start=(part == 0), stop=(part == 2))
                pe.matmul(ps[0:24, 2 * EP:3 * EP], rows[:, s, j % SLOTS, 3 * C:ROW],
                          onehot[:, j % 4, :], start=True, stop=True).then_inc(g_mm.sem, 1)

            with pe.Fori(0, ET // (2 * SLOTS)) as g:
                for j in range(2 * SLOTS):
                    if j % SLOTS == 0:
                        pe.wait_ge(rows_in[j // SLOTS], g * (16 * SLOTS) + 16 * SLOTS)
                    edge_tile(g * (2 * SLOTS) + j, j)

            pe.wait_ge(consts, 1)
            pe.wait_ge(c_in, 112)
            for bnk in (4, 5, 6):
                pe.matmul(B[bnk][:, :], Mdiag[:, 0, :], over(Mdiag[:, :, :], 128, 0, [[0, 4], [1, 128]]), start=True, stop=True)

            def k_front(t, b, i):
                pe.wait_ge(k_xs.sem, k_xs.done(t))
                pe.wait_ge(k_qkv.sem, k_qkv.ago(t, 1))
                for k in range(2):
                    pe.matmul(B[2][0:P, :], kxs[:, b, k, :], WqkvT_sb[:, k, 0:512], start=(k == 0), stop=(k == 1))
                for k in range(2):
                    ins = pe.matmul(B[3][0:P, 0:C], kxs[:, b, k, :], WqkvT_sb[:, k, 512:768], start=(k == 0), stop=(k == 1))
                ins.then_inc(k_mm.sem, 1)

            def k_back(t, b, i):
                pe.wait_ge(k_kkv.sem, k_kkv.done(t))
                pe.wait_ge(k_kkp.sem, k_kkp.done(t))
                for g in range(2):
                    for hq in range(4):
                        h = 4 * g + hq
                        pe.matmul(B[4 + g][D * hq:D * hq + D, :], qkv[:, 2 * C + D * h:2 * C + D * h + D], kkx[:, h, 0:512],
                                  start=False, stop=False, skip_group_check=True)
                for g in range(2):
                    for hq in range(4):
                        h = 4 * g + hq
                        pe.matmul(B[6][D * hq:D * hq + D, 66 * g:66 * g + 65], qkv[:, 2 * C + D * h:2 * C + D * h + D],
                                  kkx[:, h, 512:577], start=False, stop=False, skip_group_check=True)
                for g in range(2):
                    kn = kc[:, 128 * g:128 * g + 128]
                    pe.matmul(B[6][:, 132 + 129 * g:132 + 129 * g + 128], kn, kn, start=False, stop=False, skip_group_check=True)
                    ins = pe.matmul(B[6][:, 132 + 129 * g + 128:132 + 129 * g + 129], kn, kkx[:, 0, 576:577],
                                    start=False, stop=False, skip_group_check=True)
                ins.then_inc(k_acc.sem, 1)
            skewed(pe, k_front, k_back)

            for g in range(2):
                pe.wait_ge(kx_ready, 1 + g)
                for G in range(4):
                    ins = pe.transpose(B[2][:, 128 * G:128 * G + 128], KX[:, G, :], ident[:, :])
                ins.then_inc(kx_turned, 1)
            pe.wait_ge(big_v, 5)

            def q_linear(t):
                pe.wait_ge(q_qTs.sem, q_qTs.done(t))
                pe.wait_ge(q_f0.sem, q_f0.done(t))
                pe.wait_ge(q_yev.sem, q_yev.ago(t, 1))
                for g in range(2):
                    pe.matmul(B[6][:, g * P:(g + 1) * P], Mdiag[:, g, :], F0[:, g, :], start=(g == 0), stop=False, skip_group_check=True)
                for g in range(2):
                    pe.matmul(B[6][:, g * P:(g + 1) * P], Mlin[:, g, :], qT[:, g, :], start=False, stop=False, skip_group_check=True)
                for g in range(2):
                    ins = pe.matmul(B[6][:, (2 + g) * P:(3 + g) * P], Mgram[:, g, :], qT[:, g, :], start=False, stop=False, skip_group_check=True)
                ins.then_inc(q_T.sem, 1)

            def q_front(t, b, i):
                pe.wait_ge(q_qd.sem, q_qd.done(t))
                pe.wait_ge(q_f0.sem, q_f0.ago(t, 1))
                for g in range(2):
                    ins = pe.transpose(B[5][:, g * P:(g + 1) * P], qs[:, 128 * g:128 * g + 128], ident[0:P, 0:P])
                ins.then_inc(q_t.sem, 1)
                for hf in range(2):
                    if hf:
                        q_linear(t)
                    pe.wait_ge(q_bab.sem, q_bab.ago(t * 2 + hf, 1))
                    pe.wait_ge(q_sk.sem, q_sk.done(t))
                    for hq in range(4):
                        h = 4 * hf + hq
                        ins = pe.transpose(B[4][:, hq * P:(hq + 1) * P], qsk[:, h, :], ident[0:P, 0:P])
                    ins.then_inc(q_b.sem, 1)
                    for hq in range(4):
                        h = 4 * hf + hq
                        pe.wait_ge(q_f.sem, q_f.ago(t * 8 + h, 2))
                        for G in range(4):
                            ins = pe.transpose(B[2 + h % 2][:, G * P:(G + 1) * P],
                                               qper[:, h, 4 * (G + 1):4 * (G + 1) + 128], ident[0:P, 0:P])
                        ins.then_inc(q_g.sem, 1)

            def q_back(t, b, i):
                for g in range(2):
                    pe.wait_ge(q_f.sem, q_f.done(t * 8 + 4 * g + 3))
                    for G in range(4):
                        for hq in range(4):
                            ins = pe.matmul(B[6][D * hq:D * hq + D, g * P:(g + 1) * P], Mpair[:, g, G, D * hq:D * hq + D],
                                            F[:, 4 * g + hq, G, :], start=False, stop=(G == 3), skip_group_check=True)
                ins.then_inc(q_ym.sem, 1)
                pe.wait_ge(q_tq.sem, q_tq.done(t))
                pe.wait_ge(q_nn.sem, q_nn.ago(t, 1))
                pe.matmul(over(B[5][:, :], 128, 2 * P, [[1, 2 * P]]), blockones[:, :], over(TQ[:, :, :], 128, 0, [[1, 2 * P]]),
                          start=True, stop=True).then_inc(q_nr.sem, 1)
                pe.wait_ge(q_yev.sem, q_yev.done(t))
                pe.wait_ge(q_mo.sem, q_mo.ago(t, 1))
                for g in range(2):
                    ins = pe.matmul(B[7][0:P, 0:C], yT[:, g, :], WprojT_sb[:, g, :], start=(g == 0), stop=(g == 1))
                ins.then_inc(q_pm.sem, 1)

            def q_both(t, b, i):
                q_front(t, b, i)
                q_back(t, b, i)
            pairs(pe, q_both)

            pe.wait_ge(g_acc.sem, g_acc.done(ET - 1))

            def c_front(t, b, i):
                pe.wait_ge(c_s1.sem, c_s1.ago(t, 1))
                pe.sem_inc(waited["pe"], 1)
                for g in range(2):
                    ins = pe.matmul(B[2][:, g * P:(g + 1) * P], headsel[:, g, :], wsum[:, ds(t * P, P)], start=True, stop=True)
                ins.then_inc(c_s.sem, 1)

            def c_back(t, b, i):
                pe.wait_ge(c_gt.sem, c_gt.done(t))
                pe.wait_ge(c_x1.sem, c_x1.ago(t, 1))
                for g in range(2):
                    ins = pe.transpose(B[3][0:P, 128 * g:128 * g + 128], cg[:, g, :], ident[:, :])
                ins.then_inc(c_tr.sem, 1)
            skewed(pe, c_front, c_back)

            pe.wait_ge(late_in, 48)
            pe.wait_ge(c_in, 112)

            def d_turn(t, b, i):
                pe.wait_ge(d_xn.sem, d_xn.done(t))
                pe.wait_ge(d_xs.sem, d_xs.ago(t, 1))
                for k in range(2):
                    ins = pe.transpose(B[2][:, k * P:(k + 1) * P], dxn[:, b, 128 * k:128 * k + 128], ident[0:P, 0:P])
                ins.then_inc(d_tr.sem, 1)

            def d_hidden(t, b, i):
                pe.wait_ge(d_xs.sem, d_xs.done(t))
                for hf in range(2):
                    pe.wait_ge(d_hb.sem, d_hb.ago(t * 2 + hf, 4))
                    for k in range(2):
                        ins = pe.matmul(B[psH[b] + hf][0:P, :], dxs[:, b, k, :], W1_sb[:, k, 512 * hf:512 * hf + 512], start=(k == 0), stop=(k == 1))
                    ins.then_inc(d_mm.sem, 1)

            def d_turn_hidden(t, b, i):
                for hf in range(2):
                    pe.wait_ge(d_ge.sem, d_ge.done(t * 2 + hf))
                    pe.wait_ge((d_e0, d_e1)[hf].sem, d_e0.ago(t, 1))
                    for k in range(4):
                        ins = pe.transpose(B[5 + hf][:, k * P:(k + 1) * P], hb[b][:, 512 * hf + 128 * k:512 * hf + 128 * k + 128], ident[0:P, 0:P])
                    ins.then_inc(d_ht.sem, 1)

            def d_gate(t, b, i):
                pe.wait_ge(d_e0.sem, d_e0.done(t))
                pe.wait_ge(d_e1.sem, d_e1.done(t))
                pe.wait_ge(d_lg.sem, d_lg.ago(t, 1))
                for k in range(8):
                    ins = pe.matmul(B[7][0:P, 0:NE], hT[:, k, :], Wg_sb[:, k, :], start=(k == 0), stop=(k == 7))
                ins.then_inc(d_lm.sem, 1)
            pipeline(pe, T, 2, (d_turn, 3), (d_hidden, 2), (d_gate, 0), (d_turn_hidden, 1))

            pe.wait_ge(r_chosen, 1)
            pe.matmul(B[2][0:P, 0:T * NE], rtri[:, :], r_a[:, :, :].rearrange("p t e -> p (t e)"), start=True, stop=True)
            pe.matmul(B[3][0:P, 0:T * NE], rones[:, :], r_a[:, :, :].rearrange("p t e -> p (t e)"), start=True, stop=True).then_inc(r_counts, 1)

            pe.wait_ge(wd_in, 16 * NE)
            pe.wait_ge(big_v, 7)

            def e_turn(s, b, i):
                pe.wait_ge(hs_in[b], i * 16 + 16)
                for hf in range(2):
                    pe.wait_ge((e_e0, e_e1)[hf].sem, e_e0.ago(s, 2))
                    for k in range(4):
                        ins = pe.transpose(B[4 + 2 * (b % 2) + hf][:, 128 * k:128 * k + 128],
                                           hsb[b][:, 512 * hf + 128 * k:512 * hf + 128 * k + 128], ident[:, :])
                    ins.then_inc(e_tr.sem, 1)

            def e_product(s, b, i):
                col = pe.value_load(experts_i[0:1, ds(s, 1)], min_val=0, max_val=(NE - 1) * C)
                pe.wait_ge(e_e0.sem, e_e0.done(s))
                pe.wait_ge(e_e1.sem, e_e1.done(s))
                pe.wait_ge(e_t1.sem, e_t1.ago(s, 2))
                for k in range(8):
                    ins = pe.matmul(B[2 + b % 2][:, 0:C], hsT[:, b % 2, k // 4, 128 * (k % 4):128 * (k % 4) + 128], Wd_sb[:, k, ds(col, C)],
                                    start=(k == 0), stop=(k == 7))
                ins.then_inc(e_mm.sem, 1)
            pipeline(pe, ST, 4, (e_turn, 1), (e_product, 0))


def kernel(**inputs):
    import numpy as _np
    import concourse.bacc as _bacc
    from concourse import mybir as _mybir
    from concourse.bass_utils import run_bass_kernel_spmd as _run

    def edges(a, fill):
        return _np.concatenate([_np.asarray(a), _np.full(ET * EP - E, fill, _np.asarray(a).dtype)]).reshape(ET, EP)

    f = {k: _np.asarray(v) for k, v in inputs.items()}
    src, dst = edges(f["src"], 0), edges(f["dst"], -1)
    laid_out = {
        "x": f["x"], "src": src.T, "dst": dst.T, "dst0": dst[:, 0], "W": f["L0_gnn_W"],
        "a_src": f["L0_gnn_a_src"].reshape(-1), "WqkvT": f["L0_mix_Wqkv"].T, "bqkv": f["L0_mix_bqkv"],
        "WprojT": f["L0_mix_Wproj"].T, "bproj": f["L0_mix_bproj"], "temp": f["L0_mix_temperature"].reshape(-1),
        "W1": f["L0_ffn_W1"], "b1": f["L0_ffn_b1"], "Wg": f["L0_ffn_Wg"], "bg": f["L0_ffn_bg"],
        "Wd": f["L0_ffn_Wd"], "bd": f["L0_ffn_bd"].reshape(-1),
    }
    nc = _bacc.Bacc("TRN2", target_bir_lowering=False, num_devices=1)
    arrays, args = {}, []
    for name, a in laid_out.items():
        a = _np.ascontiguousarray(a)
        arrays[f"in_{name}"] = a
        args.append(nc.dram_tensor(f"in_{name}", a.shape, _mybir.dt.from_np(a.dtype), kind="ExternalInput").ap())
    args.append(nc.dram_tensor("out_0", (N, C), _mybir.dt.float32, kind="ExternalOutput").ap())
    args.append(nc.dram_tensor("table", (N, ROW), _mybir.dt.bfloat16, kind="Internal").ap())
    args.append(nc.dram_tensor("hidden", (N, HROW), _mybir.dt.float32, kind="Internal").ap())
    args.append(nc.dram_tensor("order", (ST * 128, 2), _mybir.dt.int32, kind="Internal").ap())
    build(nc, *args)
    r = _run(nc, [arrays], core_ids=[0])
    return r.results[0]["out_0"]
```

```python
import concourse.bass as bass
from concourse import mybir
from contextlib import ExitStack

F32, BF16, I32 = mybir.dt.float32, mybir.dt.bfloat16, mybir.dt.int32
ALU, ACT, AX = mybir.AluOpType, mybir.ActivationFunctionType, mybir.AxisListType
ds = bass.ds

N, C, H, D = 3125, 256, 8, 32
P, T = 125, 25
E = 2 * 25000 + N
EP = 128
ET = -(-E // EP)
SLOTS = 8
SETS = ET // SLOTS
XW = C + H
ROW = 3 * XW
NACC = N + EP
HID, NE = 1024, 8
ST = (N + NE * 127) // 128
HROW = HID + C
NOBODY = 4096
FD = 17
KW = FD * D
KROW = KW + D + 2
LN_EPS = 1e-5
SCALE = float(D) ** 0.25
PRE = 8


class Stage:

    def __init__(self, sem, pre=PRE):
        self.sem, self.pre = sem, pre

    def done(self, n):
        return n + (1 + self.pre)

    def ago(self, n, depth):
        return n + (1 + self.pre - depth)


def build(nc, x, src, dst, dst0, W, a_src, WqkvT, bqkv, WprojT, bproj, temp, W1, b1, Wg, bg, Wd, bd, out,
          table, hidden, order):
    with ExitStack() as ctx:
        def sb(name, shape, dt=F32):
            return ctx.enter_context(nc.sbuf_tensor(name, shape, dt))

        def bank(name):
            return ctx.enter_context(nc.psum_tensor(name, [128, 512], F32))

        def region(*alternatives):
            found, most = [], 0
            for tensors in alternatives:
                with ExitStack() as st:
                    size = 0
                    for name, shape, dt in tensors:
                        found.append(st.enter_context(nc.sbuf_tensor(name, shape, dt)))
                        n = 2 if dt == BF16 else 4
                        for s in shape[1:]:
                            n *= s
                        size += -(-n // 32) * 32
                most = max(most, size)
            sb(f"region_{found[0].name}", [128, most // 4])
            return found

        def over(a, parts, off, dims):
            return bass.AP(a.tensor, a.offset + off, [[a.ap[0][0], parts], *dims])

        def at(a, t, lo=0, hi=None):
            hi = a.shape[-1] if hi is None else hi
            return a[:, ds(t, 1), lo:hi].rearrange("p o c -> p (o c)")

        ident = sb("ident", [128, 128])
        W_sb = sb("W_sb", [128, 2, XW])
        WqkvT_sb = sb("WqkvT_sb", [128, 2, 3 * C])
        WprojT_sb = sb("WprojT_sb", [128, 2, C])
        bqkv_bc = sb("bqkv_bc", [P, 3 * C])
        bproj_bc = sb("bproj_bc", [P, C])
        Wg_sb = sb("Wg_sb", [128, 8, NE])
        bg_bc = sb("bg_bc", [P, NE])
        temp_bc = sb("temp_bc", [P, H])
        identx = sb("identx", [128, 4, 48])
        iota_bf = sb("iota_bf", [128, 128], BF16)
        src_sb = sb("src_sb", [128, ET], I32)
        dloc_set = sb("dloc_set", [128, ET])
        dloc_tile = sb("dloc_tile", [128, ET])
        span = sb("span", [128, 1])
        span_all = sb("span_all", [128, 1])
        span_i = sb("span_i", [128, 1], I32)
        base_row = sb("base_row", [1, ET], I32)
        headsel = sb("headsel", [24, 2, 128])
        rtri = sb("rtri", [P, P])
        rones = sb("rones", [P, P])
        pay_st = sb("pay_st", [P, 5, 2], I32)
        slot_st = sb("slot_st", [P, 5], I32)
        blockones = sb("blockones", [128, 128])
        headmask = sb("headmask", [128, 128])
        normfac = sb("normfac", [P, 2 * H])
        normeps = sb("normeps", [P, 2 * H])
        Mpair = sb("Mpair", [128, 2, 4, 128])
        Mdiag = sb("Mdiag", [128, 2, 128])
        Mlin = sb("Mlin", [128, 2, 128])
        Mgram = sb("Mgram", [128, 2, 128])
        ksum = sb("ksum", [128, 2])
        vsum = sb("vsum", [128, 2])
        st_all = sb("st_all", [P, T, 6])
        mean = sb("mean", [P, T])
        delta = sb("delta", [P, T])
        var = sb("var", [P, T])
        rstd = sb("rstd", [P, T])
        nmr = sb("nmr", [P, T])
        iidx = sb("iidx", [128, 2, SLOTS], I32)
        onehot = sb("onehot", [128, 2, SLOTS, EP], BF16)
        hmax = sb("hmax", [P, H])
        hmaxall = sb("hmaxall", [P, H])
        prob = sb("prob", [P, T])
        pay = sb("pay", [P, T, 2], I32)
        slot_i = sb("slot_i", [P, T], I32)
        order_sb = sb("order_sb", [128, ST, 2], I32)
        experts_i = sb("experts_i", [1, ST], I32)

        raw_all, kkx0, qkv, ss, ss2, nrm, rcp, rn, mixo = region(
            [("raw_all", [P, T, XW], F32)],
            [("kkx0", [P, H, KROW], F32), ("qkv", [P, 2, 3 * C], F32), ("ss", [P, 16], F32), ("ss2", [P, 16], F32),
             ("nrm", [P, 16], F32), ("rcp", [P, 16], F32), ("rn", [P, 16], F32)],
            [("mixo", [P, T, C], F32)])
        (tb_all, acc, wsum, hp, h0, h1, hT, dxn, dxs,
         lg_all, ex, r_a, r_b, r_c, r_d, r_e, r_f, r_g, r_h, ev32, hs0, hs1, hs2, hs3) = region(
            [("tb_all", [P, T, ROW], BF16)],
            [("acc", [128, 2, NACC], F32), ("wsum", [24, NACC], F32)],
            [("hp", [P, 2, HID], F32), ("h0", [P, HID], F32), ("h1", [P, HID], F32), ("hT", [128, 8, P], F32),
             ("dxn", [P, 2, C], F32), ("dxs", [128, 2, 2, P], F32),
             ("lg_all", [P, T, NE], F32), ("ex", [P, T, NE], F32), ("r_a", [P, T, NE], F32), ("r_b", [P, T, NE], F32),
             ("r_c", [P, NE, T], F32), ("r_d", [P, NE, T], F32), ("r_e", [P, T], F32), ("r_f", [P, NE], F32),
             ("r_g", [P, NE], I32), ("r_h", [P, NE], F32), ("ev32", [1, ST, NE], F32)],
            [(f"hs{b}", [128, HROW], F32) for b in range(4)])
        (xnT_all, W1_sb, b1_bc, bd_bc) = region(
            [("xnT_all", [128, 2, N], F32)],
            [("W1_sb", [128, 2, HID], F32), ("b1_bc", [P, HID], F32), ("bd_bc", [128, NE * C], F32)])
        (x_all, xn, xs, yw, y1, w1, waste, baseb, asrc_bc, wa_prod, iota_i, head_i, head_f,
         qT_all, rows, kkx1, kd, kc, qn, sq, kxs,
         qT_all2, rows2, F, sel, F0, TQ, nn, rnn, yT,
         qT_all3, rows3, KV, KX, KL, KS,
         Wd_sb, hsT, so, t1, ix, cs, crs, cg) = region(
            [("x_all", [P, T, C], F32), ("xn", [P, 2, C], F32), ("xs", [128, 2, 2, P], F32), ("yw", [P, 2, C], F32),
             ("y1", [P, 2, C], F32), ("w1", [P, T, H], F32), ("waste", [128, ET], I32), ("baseb", [128, ET], I32), ("asrc_bc", [128, C], F32),
             ("wa_prod", [128, 2, C], F32), ("iota_i", [128, 128], I32), ("head_i", [24, 2, 128], I32),
             ("head_f", [24, 2, 2, 128], F32)],
            [("qT_all", [128, 2, N], F32), ("rows", [128, 2, SLOTS, ROW], BF16), ("kkx1", [P, H, KROW], F32),
             ("kd", [P, H, 48], F32), ("kc", [P, 2, C], F32), ("qn", [P, C], F32),
             ("sq", [P, 2 * C], F32), ("kxs", [128, 2, 2, P], F32)],
            [("qT_all2", [128, 2, N], F32), ("rows2", [128, 2, SLOTS, ROW], BF16), ("F", [128, H, 4, P], F32),
             ("sel", [128, 4, 4, 128], F32), ("F0", [128, 2, 2, P], F32),
             ("TQ", [128, 2, P], F32), ("nn", [128, 2, P], F32), ("rnn", [128, 2, P], F32), ("yT", [128, 2, P], F32)],
            [("qT_all3", [128, 2, N], F32), ("rows3", [128, 2, SLOTS, ROW], BF16), ("KV", [128, FD, 64], F32),
             ("KX", [128, 4, 128], F32), ("KL", [128, 2, 3, D], F32), ("KS", [128, 3, D], F32)],
            [("Wd_sb", [128, 8, NE * C], F32), ("hsT", [128, 2, 2, 512], F32), 
             ("so", [128, 2, C], F32), ("t1", [128, C], F32), ("ix", [128, 4], I32),
             ("cs", [128, 2, P], F32), ("crs", [128, 2, P], F32), ("cg", [128, 2, P], F32)])
        iota8 = sb("iota8", [P, NE])
        iota8i = sb("iota8i", [P, NE], I32)
        s128 = sb("s128", [1, ST])
        s128i = sb("s128i", [1, ST], I32)
        rexp = sb("rexp", [1, ST])
        empty = sb("empty", [128, 64], I32)
        hb = [h0, h1]
        kkx = [kkx0, kkx1]
        hsb = [hs0, hs1, hs2, hs3]

        B = [bank(f"bank{i}") for i in range(8)]
        psG = [B[0], B[1]]
        psN = [B[5], B[6]]
        psH = [3, 0]

        names = []

        def sem(name):
            names.append(name)
            return ctx.enter_context(nc.semaphore(name))

        stages = []

        def stage(name, pre=PRE):
            s = Stage(sem(name), pre)
            stages.append(s)
            return s

        x_in, w_in, e_in, c_in, late_in, wd_in = (sem(s) for s in
                                                 ("x_in", "w_in", "e_in", "c_in", "late_in", "wd_in"))
        tab_out, x1_out, h_dma, empty_out, slot_out, order_in = (sem(s) for s in (
            "tab_out", "x1_out", "h_dma", "empty_out", "slot_out", "order_in"))
        rows_in = [sem("rows_in0"), sem("rows_in1")]
        redo_in = [sem("redo_in0"), sem("redo_in1")]
        xb_out, xb_in, xb_made, g_final = sem("xb_out"), sem("xb_in"), sem("xb_made"), sem("g_final")
        hs_in = [sem(f"hs_in{b}") for b in range(4)]
        out_done = [sem(f"out_done{b}") for b in range(4)]
        dve_chain, pool_chain, kx_ready, kx_turned, r_shifted, r_chosen, r_counts = (sem(s) for s in (
            "dve_chain", "pool_chain", "kx_ready", "kx_turned", "r_shifted", "r_chosen", "r_counts"))
        consts, routed = sem("consts"), sem("routed")
        waited = {k: sem(f"waited_{k}") for k in ("act", "dve", "pool", "pe")}

        (a_xn, a_tr, a_xs, a_xnT, a_mm, a_raw, a_y, a_hi, a_r1, a_mid, a_lo) = (stage(s) for s in (
            "a_xn", "a_tr", "a_xs", "a_xnT", "a_mm", "a_raw", "a_y", "a_hi", "a_r1", "a_mid", "a_lo"))
        g_idx, g_oh, g_mm, g_acc = (stage(s) for s in ("g_idx", "g_oh", "g_mm", "g_acc"))
        r_idx, r_oh, r_acc = stage("r_idx"), stage("r_oh"), stage("r_acc")
        r_mm = stage("r_mm", 12)
        (k_xs, k_mm, k_qkv, k_sq, k_ss, k_mx, k_nrm, k_rc, k_rn, k_kn, k_kkv, k_kc, k_acc, k_qt, k_qk) = (
            stage(s) for s in ("k_xs", "k_mm", "k_qkv", "k_sq", "k_ss", "k_mx", "k_nrm", "k_rc", "k_rn", "k_kn", "k_kkv",
                               "k_kc", "k_acc", "k_qt", "k_qk"))
        (q_s, q_f0, q_f, q_T, q_ym, q_tq, q_nr, q_nn, q_rn, q_yev, q_pm, q_mo) = (stage(s) for s in (
            "q_s", "q_f0", "q_f", "q_T", "q_ym", "q_tq", "q_nr", "q_nn", "q_rn", "q_yev", "q_pm", "q_mo"))
        (c_s, c_s1, c_rs, c_gt, c_tr, c_x1) = (stage(s) for s in ("c_s", "c_s1", "c_rs", "c_gt", "c_tr", "c_x1"))
        (d_xn, d_tr, d_xs, d_mm, d_hb, d_ge, d_hout, d_ht, d_e0, d_e1, d_lm, d_lg) = (stage(s) for s in (
            "d_xn", "d_tr", "d_xs", "d_mm", "d_hb", "d_ge", "d_hout", "d_ht", "d_e0", "d_e1", "d_lm", "d_lg"))
        p_idx = stage("p_idx")
        (e_ix, e_tr, e_e0, e_e1, e_mm, e_t1, e_o, e_scd) = (stage(s) for s in (
            "e_ix", "e_tr", "e_e0", "e_e1", "e_mm", "e_t1", "e_o", "e_scd"))
        stats_v, stats_s, big_v, big_s, big_p = (sem(s) for s in ("stats_v", "stats_s", "big_v", "big_s", "big_p"))

        def pairs(e, body):
            with e.Fori(0, T // 2) as i:
                body(i * 2, 0, i)
                body(i * 2 + 1, 1, i)
            body(T - 1, 0, T // 2)

        def skewed(e, front, back):
            front(0, 0, 0)
            with e.Fori(0, T // 2) as i:
                front(i * 2 + 1, 1, i)
                back(i * 2, 0, i)
                front(i * 2 + 2, 0, i + 1)
                back(i * 2 + 1, 1, i)
            back(T - 1, 0, T // 2)

        def pipeline(e, count, unroll, *bodies):
            lead = max(l for _, l in bodies)

            def step(n, j, i):
                for body, l in bodies:
                    body(n + l, (j + l) % unroll, i + (j + l) // unroll)

            def edge(n):
                for body, l in bodies:
                    if 0 <= n + l < count:
                        body(n + l, (n + l) % unroll, (n + l) // unroll)
            for n in range(-lead, 0):
                edge(n)
            rounds = (count - lead) // unroll
            with e.Fori(0, rounds) as i:
                for j in range(unroll):
                    step(i * unroll + j, j, i)
            for n in range(rounds * unroll, count):
                edge(n)

        def beside_q(body):
            def shifted(t, b, i):
                body(t + T, (T + b) % 2, i + (T + b) // 2)
            return shifted

        def last_sets(body):
            for u in range(2 * T, SETS):
                body(u, u % 2, u // 2)

        def if_spread(e):
            return e.If(e.value_load(span_i[0:1, 0:1], min_val=0, max_val=N) > EP - 1)

        def row_bc(a, n, parts):
            return bass.AP(a.tensor, a.offset, [[0, parts], [1, n]])

        block = ctx.enter_context(nc.Block())

        @block.sync
        def _(sp):
            for c in range(5):
                sp.dma_start(x_all[:, 5 * c:5 * c + 5, :],
                             x[5 * c * P:5 * (c + 1) * P, :].rearrange("(t p) c -> p t c", p=P)).then_inc(x_in, 16)
            for s in stages:
                sp.sem_inc(s.sem, s.pre)
            sp.dma_start(W_sb[:, :, 0:C], W.rearrange("(k p) n -> p k n", p=128)).then_inc(w_in, 16)
            sp.dma_start(asrc_bc[:, :], row_bc(a_src, C, 128)).then_inc(w_in, 16)
            sp.dma_start(src_sb[:, :], src).then_inc(e_in, 16)
            sp.dma_start(waste[:, :], dst).then_inc(e_in, 16)
            sp.dma_start(baseb[:, :], row_bc(dst0, ET, 128)).then_inc(e_in, 16)
            sp.dma_start(base_row[:, :], row_bc(dst0, ET, 1)).then_inc(e_in, 16)
            sp.dma_start(WqkvT_sb[:, :, :], WqkvT.rearrange("(k p) n -> p k n", p=128)).then_inc(c_in, 16)
            sp.dma_start(WprojT_sb[:, :, :], WprojT.rearrange("(k p) n -> p k n", p=128)).then_inc(c_in, 16)
            sp.dma_start(bqkv_bc[:, :], row_bc(bqkv, 3 * C, P)).then_inc(c_in, 16)
            sp.dma_start(bproj_bc[:, :], row_bc(bproj, C, P)).then_inc(c_in, 16)
            sp.dma_start(temp_bc[:, :], row_bc(temp, H, P)).then_inc(c_in, 16)
            sp.dma_start(Wg_sb[:, :, :], Wg.rearrange("(k p) e -> p k e", p=128)).then_inc(c_in, 16)
            sp.dma_start(bg_bc[:, :], row_bc(bg, NE, P)).then_inc(c_in, 16)

            def table_out(t, b, i):
                sp.wait_ge(a_lo.sem, a_lo.done(t))
                sp.dma_start(table[ds(t * P, P), :], at(tb_all, t)).then_inc(tab_out, 16)
            pairs(sp, table_out)

            sp.wait_ge(xb_out, 80)
            sp.wait_ge(k_acc.sem, k_acc.done(T - 1))
            for c in range(5):
                sp.dma_start(mixo[:, 5 * c:5 * c + 5, :],
                             hidden[5 * c * P:5 * (c + 1) * P, HID:HROW].rearrange("(t p) c -> p t c", p=P)).then_inc(xb_in, 16)

            sp.wait_ge(k_mm.sem, k_mm.done(T - 1))
            sp.dma_start(W1_sb[:, :, :], W1.rearrange("(k p) n -> p k n", p=128)).then_inc(late_in, 16)
            sp.dma_start(b1_bc[:, :], row_bc(b1, HID, P)).then_inc(late_in, 16)
            sp.dma_start(bd_bc[:, :], row_bc(bd, NE * C, 128)).then_inc(late_in, 16)
            sp.wait_ge(g_final, 1)
            sp.wait_ge(q_mo.sem, q_mo.done(T - 1))
            sp.wait_ge(q_pm.sem, q_pm.done(T - 1))
            for e in range(NE):
                sp.dma_start(Wd_sb[:, :, e * C:(e + 1) * C], Wd[e].rearrange("(k p) c -> p k c", p=128)).then_inc(wd_in, 16)

            def x1_store(t, b, i):
                sp.wait_ge(c_x1.sem, c_x1.done(t))
                sp.dma_start(hidden[ds(t * P, P), HID:HROW], at(mixo, t)).then_inc(x1_out, 16)
            pairs(sp, x1_store)

            def h_store(t, b, i):
                sp.wait_ge(d_ge.sem, d_ge.done(t * 2 + 1))
                sp.dma_start(hidden[ds(t * P, P), 0:HID], hb[b][:, :]).then_inc(h_dma, 16)
                sp.wait_ge(h_dma, t * 16 + 16)
                sp.sem_inc(d_hout.sem, 1)
            pairs(sp, h_store)

            sp.wait_ge(x1_out, 16 * T)
            sp.wait_ge(tab_out, 16 * T)
            sp.wait_ge(slot_out, 16 * T)
            sp.dma_start(order_sb[:, :, :], order[0:ST * 128, :].rearrange("(s p) c -> p s c", p=128)).then_inc(order_in, 16)

            def out_stored(s, b, i):
                sp.wait_ge(out_done[b], i * 16 + 16)
                sp.sem_inc(e_scd.sem, 1)
            pipeline(sp, ST, 4, (out_stored, 0))

        @block.gpsimd
        def _(pool):
            n = [0]

            def link(ins):
                n[0] += 1
                ins.then_inc(pool_chain, 1)
                pool.wait_ge(pool_chain, n[0])

            def gate():
                pool.sem_inc(waited["pool"], 1)

            link(pool.memset(ident[:, :], 0.0))
            link(pool.affine_select(out=ident[:, :], in_=ident[:, :], compare_op=ALU.not_equal, fill=1.0, base=0,
                                    pattern=[[-1, 128]], channel_multiplier=1))
            link(pool.iota(iota_i[:, :], pattern=[[1, 128]], base=0, channel_multiplier=0))
            link(pool.tensor_copy(iota_bf[:, :], iota_i[:, :]))
            link(pool.iota(iota8i[:, :], pattern=[[1, NE]], base=0, channel_multiplier=0))
            link(pool.tensor_copy(iota8[:, :], iota8i[:, :]))
            link(pool.iota(s128i[:, :], pattern=[[128, ST]], base=0, channel_multiplier=0))
            link(pool.tensor_copy(s128[:, :], s128i[:, :]))
            link(pool.iota(pay[:, :, 0:1], pattern=[[P, T], [1, 1]], base=0, channel_multiplier=1))
            link(pool.memset(headmask[:, :], 0.0))
            for hq in range(4):
                link(pool.memset(headmask[D * hq:D * hq + D, D * hq:D * hq + D], 1.0))
                link(pool.tensor_copy(identx[:, hq, 0:D], ident[:, D * hq:D * hq + D]))
                link(pool.tensor_copy(identx[:, hq, D:48], ident[:, D * hq:D * hq + 16]))
            link(pool.tensor_copy(blockones[:, :], headmask[:, :]))
            link(pool.iota(head_i[:, :, :], pattern=[[4, 2], [1, 4], [0, D]], base=0, channel_multiplier=-1))
            link(pool.tensor_copy(head_f[:, 0, :, :], head_i[:, :, :]))
            link(pool.tensor_scalar(headsel[:, :, :], head_f[:, 0, :, :], 0.0, None, ALU.is_equal))
            for s in (1, 2):
                link(pool.tensor_scalar(head_f[:, 1, :, :], head_f[:, 0, :, :], -8.0 * s, None, ALU.is_equal))
                link(pool.tensor_tensor(headsel[:, :, :], headsel[:, :, :], head_f[:, 1, :, :], ALU.add))
            link(pool.memset(rones[:, :], 1.0))
            link(pool.affine_select(out=rtri[:, :], in_=rones[:, :], compare_op=ALU.is_gt, fill=0.0, base=0,
                                    pattern=[[1, P]], channel_multiplier=-1))
            link(pool.memset(empty[:, :], 0))
            link(pool.memset(over(empty[:, :], 128, 0, [[2, 32]]), NOBODY))
            link(pool.memset(Mdiag[:, :, :], 0.0))
            link(pool.memset(Mlin[:, :, :], 0.0))
            pool.memset(pay[:, :, 1:2], 0).then_inc(consts, 1)
            pool.dma_start(order.rearrange("(p s) c -> p (s c)", p=128), empty[:, 0:64]).then_inc(empty_out, 16)

            def keep_xnT(t, b, i):
                pool.wait_ge(a_xs.sem, a_xs.done(t))
                gate()
                pool.tensor_copy(xnT_all[:, :, ds(t * P, P)], xs[:, b, :, :]).then_inc(a_xnT.sem, 1)
            pairs(pool, keep_xnT)

            pool.wait_ge(big_v, 2)
            pool.partition_all_reduce(hmaxall[:, :], hmax[:, :], P, bass.bass_isa.ReduceOp.max).then_inc(big_p, 1)

            pool.wait_ge(c_in, 112)
            pool.wait_ge(a_xn.sem, a_xn.done(T - 1))
            for c in range(5):
                pool.tensor_tensor(x_all[:, 5 * c:5 * c + 5, :], x_all[:, 5 * c:5 * c + 5, :],
                                   over(bproj_bc[:, :], P, 0, [[0, 5], [1, C]]), ALU.add).then_inc(xb_made, 1)
                pool.wait_ge(xb_made, c + 1)
                pool.dma_start(hidden[5 * c * P:5 * (c + 1) * P, HID:HROW].rearrange("(t p) c -> p t c", p=P),
                               x_all[:, 5 * c:5 * c + 5, :]).then_inc(xb_out, 16)
            pool.wait_ge(big_v, 4)
            pool.partition_all_reduce(span_all[:, :], span[:, :], 128, bass.bass_isa.ReduceOp.max).then_inc(big_p, 1)

            pool.wait_ge(tab_out, 16 * T)
            pool.wait_ge(e_in, 64)
            pool.wait_ge(xb_out, 80)

            def gather(u, b, i):
                pool.wait_ge(g_mm.sem, g_mm.ago(u, 2))
                gate()
                pool.tensor_copy(iidx[:, b, :], src_sb[:, ds(u * SLOTS, SLOTS)]).then_inc(g_idx.sem, 1)
                pool.wait_ge(g_idx.sem, g_idx.done(u))
                gate()
                for j in range(SLOTS):
                    pool.indirect_dma_start(out=rows[:, b, j, :], out_offset=None, in_=table,
                                            in_offset=bass.IndirectOffsetOnAxis(ap=iidx[:, b, j:j + 1], axis=0)
                                            ).then_inc(rows_in[b], 16)
            pipeline(pool, SETS, 2, (gather, 0))

            def regather(u, b, i):
                pool.wait_ge(r_mm.sem, u * SLOTS + (r_mm.pre - SLOTS))
                gate()
                pool.tensor_copy(iidx[:, b, :], src_sb[:, ds(u * SLOTS, SLOTS)]).then_inc(r_idx.sem, 1)
                pool.wait_ge(r_idx.sem, r_idx.done(u))
                gate()
                for j in range(SLOTS):
                    pool.indirect_dma_start(out=rows[:, b, j, :], out_offset=None, in_=table,
                                            in_offset=bass.IndirectOffsetOnAxis(ap=iidx[:, b, j:j + 1], axis=0)
                                            ).then_inc(redo_in[b], 16)
            pool.wait_ge(big_v, 5)
            with if_spread(pool):
                pool.wait_ge(g_mm.sem, g_mm.done(SETS - 1))
                pipeline(pool, SETS, 2, (regather, 0))

            pool.wait_ge(empty_out, 16)
            pool.wait_ge(routed, 1)
            with pool.Fori(0, T // 5) as i:
                pool.tensor_copy(slot_st[:, :], slot_i[:, ds(i * 5, 5)])
                pool.tensor_copy(pay_st[:, :, :], pay[:, ds(i * 5, 5), :]).then_inc(p_idx.sem, 1)
                pool.wait_ge(p_idx.sem, p_idx.done(i))
                gate()
                for j in range(5):
                    pool.indirect_dma_start(out=order, out_offset=bass.IndirectOffsetOnAxis(ap=slot_st[:, j:j + 1], axis=0),
                                            in_=pay_st[:, j, :], in_offset=None).then_inc(slot_out, 16)
                pool.wait_ge(slot_out, i * 80 + 80)
                gate()

            pool.wait_ge(order_in, 16)
            pool.wait_ge(d_hout.sem, d_hout.done(T - 1))
            pool.wait_ge(x1_out, 16 * T)
            pool.wait_ge(routed, 2)

            def fetch(s, b, i):
                pool.wait_ge(e_o.sem, e_o.ago(s, 4))
                pool.wait_ge(e_scd.sem, e_scd.ago(s, 4))
                gate()
                pool.tensor_copy(ix[:, b:b + 1], at(order_sb, s, 0, 1)).then_inc(e_ix.sem, 1)
                pool.wait_ge(e_ix.sem, e_ix.done(s))
                gate()
                pool.indirect_dma_start(out=hsb[b][:, :], out_offset=None, in_=hidden,
                                        in_offset=bass.IndirectOffsetOnAxis(ap=ix[:, b:b + 1], axis=0),
                                        bounds_check=N - 1, oob_is_err=False).then_inc(hs_in[b], 16)

            def put(s, b, i):
                pool.wait_ge(e_o.sem, e_o.done(s))
                gate()
                pool.indirect_dma_start(out=out, out_offset=bass.IndirectOffsetOnAxis(ap=ix[:, b:b + 1], axis=0),
                                        in_=so[:, b % 2, :], in_offset=None, bounds_check=N - 1,
                                        oob_is_err=False).then_inc(out_done[b], 16)
            pipeline(pool, ST, 4, (fetch, 3), (put, 0))

        @block.scalar
        def _(act):
            def gate():
                act.sem_inc(waited["act"], 1)

            act.wait_ge(stats_v, 1)
            act.activation(rstd[:, :], var[:, :], ACT.Sqrt).then_inc(stats_s, 1)

            def keep(t, b, i):
                act.wait_ge(a_tr.sem, a_tr.done(t))
                act.wait_ge(a_mm.sem, a_mm.ago(t, 2))
                act.wait_ge(a_xnT.sem, a_xnT.ago(t, 2))
                act.activation(xs[:, b, :, :], over(B[2 + b][:, :], 128, 0, [[P, 2], [1, P]]), ACT.Copy).then_inc(a_xs.sem, 1)

            def raw(t, b, i):
                act.wait_ge(a_mm.sem, a_mm.done(t))
                gate()
                act.activation(at(raw_all, t), B[4 + b][0:P, 0:XW], ACT.Copy).then_inc(a_raw.sem, 1)
            skewed(act, keep, raw)

            act.wait_ge(big_v, 3)
            act.activation(raw_all[:, :, C:XW], raw_all[:, :, C:XW], ACT.Exp).then_inc(big_s, 1)

            def parts(t, b, i):
                act.wait_ge(a_y.sem, a_y.done(t))
                gate()
                act.activation(at(tb_all, t, 0, C), yw[:, b, :], ACT.Copy).then_inc(a_hi.sem, 1)
                act.wait_ge(a_r1.sem, a_r1.done(t))
                gate()
                act.activation(at(tb_all, t, C, 2 * C), y1[:, b, :], ACT.Copy).then_inc(a_mid.sem, 1)
            pairs(act, parts)

            def k_stage(t, b, i):
                act.wait_ge(k_mm.sem, k_mm.ago(t, 2))
                gate()
                act.activation(kxs[:, b, :, :], xnT_all[:, :, ds(t * P, P)], ACT.Copy).then_inc(k_xs.sem, 1)

            def k_norm(t, b, i):
                act.wait_ge(k_qkv.sem, k_qkv.done(t))
                act.wait_ge(k_ss.sem, k_ss.ago(t, 1))
                act.activation(sq[:, :], qkv[:, b, 0:2 * C], ACT.Square).then_inc(k_sq.sem, 1)
                act.wait_ge(k_mx.sem, k_mx.done(t))
                act.wait_ge(k_rc.sem, k_rc.ago(t, 1))
                act.activation(nrm[:, :], ss2[:, :], ACT.Sqrt).then_inc(k_nrm.sem, 1)

            def k_keep(t, b, i):
                act.wait_ge(k_kn.sem, k_kn.done(t))
                act.wait_ge(k_acc.sem, k_acc.ago(t, 2))
                act.activation(kkx[b][:, :, KW:KW + D], kd[:, :, 0:D], ACT.Copy)
                act.activation(over(kc[:, b, :], P, 0, [[D, H], [1, D]]), kd[:, :, 0:D], ACT.Copy).then_inc(k_kc.sem, 1)
                act.wait_ge(k_qt.sem, k_qt.done(t))
                gate()
                act.activation(qT_all[:, :, ds(t * P, P)], over(B[7][:, :], 128, 0, [[P, 2], [1, P]]),
                               ACT.Copy).then_inc(k_qk.sem, 1)
            act.wait_ge(tab_out, 16 * T)
            act.wait_ge(xb_out, 80)
            act.wait_ge(a_xnT.sem, a_xnT.done(T - 1))
            pipeline(act, T, 2, (k_stage, 3), (k_norm, 1), (k_keep, 1))

            act.wait_ge(big_v, 7)

            def q_square(t, b, i):
                act.wait_ge(q_ym.sem, q_ym.ago(t, 2))
                gate()
                act.activation(F0[:, b, :, :], qT_all[:, :, ds(t * P, P)], ACT.Square).then_inc(q_f0.sem, 1)

            def q_pairs(t, b, i):
                act.wait_ge(q_ym.sem, q_ym.ago(t, 1))
                for h in range(H):
                    act.wait_ge(q_s.sem, q_s.done(t * 8 + h))
                    act.activation(F[:, h, :, :], over(B[2 + h % 2][:, :], 128, 0, [[P, 4], [1, P]]),
                                   ACT.Square).then_inc(q_f.sem, 1)
            pipeline(act, T, 2, (q_square, 1), (q_pairs, 0))

            act.wait_ge(stats_v, 2)
            act.activation(rstd[:, :], var[:, :], ACT.Sqrt).then_inc(stats_s, 1)

            def d_keep(t, b, i):
                act.wait_ge(d_tr.sem, d_tr.done(t))
                act.wait_ge(d_mm.sem, d_mm.ago(t * 2, 3))
                act.activation(dxs[:, b, :, :], over(B[2][:, :], 128, 0, [[P, 2], [1, P]]), ACT.Copy).then_inc(d_xs.sem, 1)

            def d_gelu(t, b, i):
                act.wait_ge(d_hout.sem, d_hout.ago(t, 2))
                act.wait_ge(d_ht.sem, d_ht.ago(t * 2, 3))
                for hf in range(2):
                    act.wait_ge(d_hb.sem, d_hb.done(t * 2 + hf))
                    act.activation(hb[b][:, 512 * hf:512 * hf + 512], hp[:, b, 512 * hf:512 * hf + 512],
                                   ACT.Gelu).then_inc(d_ge.sem, 1)

            def d_evac(t, b, i):
                act.wait_ge(d_ht.sem, d_ht.done(t * 2 + 1))
                act.wait_ge(d_lm.sem, d_lm.ago(t, 1))
                act.activation(hT[:, 4:8, :], over(B[6][:, :], 128, 0, [[P, 4], [1, P]]), ACT.Copy).then_inc(d_e1.sem, 1)
            pipeline(act, T, 2, (d_keep, 3), (d_gelu, 2), (d_evac, 1))

            act.wait_ge(r_shifted, 1)
            act.activation(ex[:, :, :], r_a[:, :, :], ACT.Exp).then_inc(big_s, 1)

            def e_evac(s, b, i):
                act.wait_ge(e_tr.sem, e_tr.done(s * 2 + 1))
                act.wait_ge(e_mm.sem, e_mm.ago(s, 2))
                act.activation(hsT[:, b, 1, :], B[5 + 2 * b][:, :], ACT.Copy).then_inc(e_e1.sem, 1)
            pipeline(act, ST, 2, (e_evac, 0))

        @block.vector
        def _(dve):
            n = [0]

            def link(ins):
                n[0] += 1
                ins.then_inc(dve_chain, 1)
                dve.wait_ge(dve_chain, n[0])

            def gate():
                dve.sem_inc(waited["dve"], 1)

            def layer_norm_stats(k):
                def col(c):
                    return st_all[:, :, c:c + 1].rearrange("p t o -> p (t o)")
                link(dve.memset(delta[:, :], 0.0))
                link(dve.tensor_tensor(mean[:, :], col(1), col(4), ALU.add))
                link(dve.tensor_tensor(delta[:, :], col(1), col(4), ALU.subtract))
                link(dve.tensor_tensor(var[:, :], col(2), col(5), ALU.add))
                link(dve.scalar_tensor_tensor(nmr[:, :], delta[:, :], 0.25, delta[:, :], ALU.mult, ALU.mult))
                link(dve.scalar_tensor_tensor(var[:, :], var[:, :], 1.0 / C, nmr[:, :], ALU.mult, ALU.add))
                dve.tensor_scalar(var[:, :], var[:, :], LN_EPS, None, ALU.add).then_inc(stats_v, 1)
                dve.wait_ge(stats_s, k)
                link(dve.reciprocal(delta[:, :], rstd[:, :]))
                link(dve.tensor_copy(rstd[:, :], delta[:, :]))
                link(dve.scalar_tensor_tensor(nmr[:, :], mean[:, :], -0.5, rstd[:, :], ALU.mult, ALU.mult))

            dve.wait_ge(x_in, 80)
            with dve.Fori(0, T) as t:
                dve.bn_stats(at(st_all, t), at(x_all, t))
            link(dve.memset(normeps[:, H:], 1e-24))
            layer_norm_stats(1)
            dve.wait_ge(w_in, 32)
            link(dve.tensor_tensor(wa_prod[:, :, :], W_sb[:, :, 0:C], over(asrc_bc[:, :], 128, 0, [[0, 2], [1, C]]), ALU.mult))
            for k in range(2):
                link(dve.tensor_reduce(W_sb[:, k, C:XW], over(wa_prod[:, :, :], 128, k * C, [[D, H], [1, D]]), AX.X, ALU.add))
            dve.memset(normeps[:, 0:H], (1e-12 / SCALE) ** 2).then_inc(big_v, 1)

            def normalise(t, b, i):
                dve.wait_ge(a_tr.sem, a_tr.ago(t, 2))
                dve.tensor_scalar(xn[:, b, :], at(x_all, t), rstd[:, ds(t, 1)], nmr[:, ds(t, 1)],
                                  ALU.mult, ALU.add).then_inc(a_xn.sem, 1)
            pairs(dve, normalise)

            dve.wait_ge(e_in, 64)
            link(dve.tensor_tensor(dloc_tile[:, :], waste[:, :], baseb[:, :], ALU.subtract))
            link(dve.tensor_tensor(dloc_set[:, :], waste[:, :], over(baseb[:, :], 128, 0, [[SLOTS, SETS], [0, SLOTS]]),
                                   ALU.subtract))
            link(dve.tensor_reduce(span[:, :], dloc_set[:, :], AX.X, ALU.max))
            dve.wait_ge(a_raw.sem, a_raw.done(T - 1))
            dve.tensor_reduce(hmax[:, :], raw_all[:, :, C:XW].rearrange("p t h -> p h t"), AX.X, ALU.max).then_inc(big_v, 1)
            dve.wait_ge(big_p, 1)
            dve.tensor_tensor(raw_all[:, :, C:XW], raw_all[:, :, C:XW], over(hmaxall[:, :], P, 0, [[0, T], [1, H]]),
                              ALU.subtract).then_inc(big_v, 1)
            dve.wait_ge(big_s, 1)
            w0, wp = raw_all[:, :, C:XW], [tb_all[:, :, 3 * C + H * k:3 * C + H * k + H] for k in range(3)]
            link(dve.tensor_copy(wp[0], w0))
            link(dve.tensor_tensor(w1[:, :, :], w0, wp[0], ALU.subtract))
            link(dve.tensor_copy(wp[1], w1[:, :, :]))
            link(dve.tensor_tensor(wp[2], w1[:, :, :], wp[1], ALU.subtract))

            def weigh(t, b, i):
                dve.wait_ge(a_lo.sem, a_lo.ago(t, 2))
                dve.tensor_tensor(over(yw[:, b, :], P, 0, [[D, H], [1, D]]),
                                  over(at(raw_all, t), P, 0, [[D, H], [1, D]]),
                                  over(at(raw_all, t), P, C, [[1, H], [0, D]]), ALU.mult).then_inc(a_y.sem, 1)
                dve.wait_ge(a_hi.sem, a_hi.done(t))
                dve.tensor_tensor(y1[:, b, :], yw[:, b, :], at(tb_all, t, 0, C), ALU.subtract).then_inc(a_r1.sem, 1)
                dve.wait_ge(a_mid.sem, a_mid.done(t))
                dve.tensor_tensor(at(tb_all, t, 2 * C, 3 * C), y1[:, b, :], at(tb_all, t, C, 2 * C),
                                  ALU.subtract).then_inc(a_lo.sem, 1)
            pairs(dve, weigh)

            dve.wait_ge(tab_out, 16 * T)
            dve.wait_ge(consts, 1)
            dve.memset(acc[:, :, :], 0.0)
            dve.memset(wsum[:, :], 0.0).then_inc(big_v, 1)
            dve.wait_ge(big_v, 4)

            def g_onehot(u, b, i):
                dve.wait_ge(g_mm.sem, g_mm.ago(u, 2))
                dve.tensor_tensor(onehot[:, b, :, :], over(iota_bf[:, :], 128, 0, [[0, SLOTS], [1, EP]]),
                                  over(dloc_set[:, ds(u * SLOTS, SLOTS)], 128, 0, [[1, SLOTS], [0, EP]]),
                                  ALU.is_equal).then_inc(g_oh.sem, 1)

            def g_add(u, b, i):
                first = dve.value_load(base_row[0:1, ds(u * SLOTS, 1)], min_val=0, max_val=N - 1)
                dve.wait_ge(g_mm.sem, g_mm.done(u))
                dve.wait_ge(g_acc.sem, g_acc.ago(u, 1))
                dve.tensor_tensor(acc[:, :, ds(first, EP)], acc[:, :, ds(first, EP)],
                                  over(psG[b][:, :], 128, 0, [[EP, 2], [1, EP]]), ALU.add)
                dve.tensor_tensor(wsum[:, ds(first, EP)], wsum[:, ds(first, EP)], psG[b][0:24, 2 * EP:3 * EP],
                                  ALU.add).then_inc(g_acc.sem, 1)

            dve.wait_ge(big_p, 2)
            dve.tensor_copy(span_i[:, :], span_all[:, :]).then_inc(big_v, 1)
            dve.wait_ge(c_in, 112)
            dve.wait_ge(xb_out, 80)
            link(dve.tensor_scalar(normfac[:, 0:H], temp_bc[:, :], SCALE, None, ALU.mult))
            link(dve.memset(normfac[:, H:], SCALE))
            dve.wait_ge(a_lo.sem, a_lo.done(T - 1))
            for b in range(2):
                link(dve.memset(kkx[b][:, :, KW + D:KROW], 1.0))
            dve.sem_inc(big_v, 1)

            def k_bias(t, b, i):
                dve.wait_ge(k_mm.sem, k_mm.done(t))
                dve.wait_ge(k_acc.sem, k_acc.ago(t, 2))
                dve.tensor_tensor(qkv[:, b, 0:512], B[2][0:P, :], bqkv_bc[:, 0:512], ALU.add)
                dve.tensor_tensor(qkv[:, b, 512:768], B[3][0:P, 0:C], bqkv_bc[:, 512:768], ALU.add).then_inc(k_qkv.sem, 1)

            def k_sums(t, b, i):
                dve.wait_ge(k_sq.sem, k_sq.done(t))
                dve.wait_ge(k_mx.sem, k_mx.ago(t, 1))
                dve.tensor_reduce(ss[:, :], sq[:, :].rearrange("p (a d) -> p a d", d=D), AX.X, ALU.add).then_inc(k_ss.sem, 1)
                dve.wait_ge(k_ss.sem, k_ss.done(t))
                dve.wait_ge(k_nrm.sem, k_nrm.ago(t, 1))
                dve.tensor_tensor(ss2[:, :], ss[:, :], normeps[:, :], ALU.max).then_inc(k_mx.sem, 1)

            def k_features(t, b, i):
                dve.wait_ge(k_nrm.sem, k_nrm.done(t))
                dve.reciprocal(rcp[:, :], nrm[:, :]).then_inc(k_rc.sem, 1)
                dve.wait_ge(k_rc.sem, k_rc.done(t))
                dve.tensor_tensor(rn[:, :], rcp[:, :], normfac[:, :], ALU.mult).then_inc(k_rn.sem, 1)
                dve.wait_ge(k_rn.sem, k_rn.done(t))
                dve.wait_ge(k_kkv.sem, k_kkv.ago(t, 1))
                dve.wait_ge(k_kc.sem, k_kc.ago(t, 1))
                dve.wait_ge(k_qt.sem, k_qt.ago(t, 1))
                k_rnb = over(rn[:, :], P, H, [[1, H], [0, D]])
                dve.tensor_tensor(kd[:, :, 0:D], over(qkv[:, b, :], P, C, [[D, H], [1, D]]), k_rnb, ALU.mult)
                dve.tensor_tensor(kd[:, :, D:48], over(qkv[:, b, :], P, C, [[D, H], [1, 16]]),
                                  over(rn[:, :], P, H, [[1, H], [0, 16]]), ALU.mult)
                dve.tensor_tensor(over(qn[:, :], P, 0, [[D, H], [1, D]]),
                                  over(qkv[:, b, :], P, 0, [[D, H], [1, D]]), over(rn[:, :], P, 0, [[1, H], [0, D]]),
                                  ALU.mult).then_inc(k_kn.sem, 1)
                dve.wait_ge(k_kn.sem, k_kn.done(t))
                dve.wait_ge(k_acc.sem, k_acc.ago(t, 2))
                dve.tensor_tensor(over(kkx[b][:, :, :], P, 0, [[KROW, H], [D, FD], [1, D]]),
                                  over(kd[:, :, :], P, 0, [[48, H], [0, FD], [1, D]]),
                                  over(kd[:, :, :], P, 0, [[48, H], [1, FD], [1, D]]), ALU.mult).then_inc(k_kkv.sem, 1)
            pipeline(dve, T, 2, (k_bias, 1), (g_onehot, 1), (k_sums, 1), (g_add, 0), (k_features, 1))

            dve.wait_ge(k_kc.sem, k_kc.done(T - 1))
            dve.wait_ge(k_qt.sem, k_qt.done(T - 1))
            for g in range(2):
                dve.wait_ge(k_acc.sem, k_acc.done(T - 1))
                accA, accC = B[4 + g], B[6]
                for dd, nd, f in ((0, 1, 0.5 / N), (1, 15, 1.0 / N), (16, 1, 0.5 / N)):
                    srcA = over(accA[:, :], 128, dd * D, [[D, nd], [1, D]]) if dd < 16 else over(accC[:, :], 128, 66 * g, [[D, 1], [1, D]])
                    for half in range(2):
                        link(dve.tensor_scalar(over(KV[:, :, :], 128, dd * 64 + 32 * half, [[64, nd], [1, D]]), srcA, f, None, ALU.mult))
                link(dve.tensor_scalar(KL[:, g, 0, :], accC[:, 66 * g + D:66 * g + 2 * D], SCALE ** 2 / N, None, ALU.mult))
                link(dve.tensor_scalar(vsum[:, g:g + 1], accC[:, 66 * g + 2 * D:66 * g + 2 * D + 1], SCALE ** 4 / N, None, ALU.mult))
                for G in range(4):
                    for r in range(4):
                        link(dve.tensor_copy(KX[:, G, D * r:D * r + D], KV[:, 4 * (G + 1) - r, r:r + D]))
                dve.sem_inc(kx_ready, 1)
                link(dve.tensor_reduce(KS[:, 0, :], over(KV[:, :, :], 128, 64, [[1, D], [64, 16]]), AX.X, ALU.add))
                link(dve.tensor_reduce(KS[:, 1, :], over(KV[:, :, :], 128, 64 + D - 1, [[1, D], [63, 16]]), AX.X, ALU.add))
                link(dve.tensor_tensor(KS[:, 2, :], KS[:, 0, :], KS[:, 1, :], ALU.add))
                link(dve.scalar_tensor_tensor(KS[:, 0, :], KS[:, 2, :], -0.5, KV[:, 0, 0:D], ALU.mult, ALU.add))
                link(dve.transpose(KL[:, g, 2, :], KS[:, 0, :]))
                for hq in range(4):
                    link(dve.tensor_copy(Mdiag[D * hq:D * hq + D, g, D * hq:D * hq + D], KL[D * hq:D * hq + D, g, 2, :]))
                link(dve.transpose(KL[:, g, 1, :], KL[:, g, 0, :]))
                for hq in range(4):
                    link(dve.tensor_copy(Mlin[D * hq:D * hq + D, g, D * hq:D * hq + D], KL[D * hq:D * hq + D, g, 1, :]))
                link(dve.scalar_tensor_tensor(Mgram[:, g, :], accC[:, 132 + 129 * g:132 + 129 * g + 128], 0.5 / N,
                                              headmask[:, :], ALU.mult, ALU.mult))
                link(dve.tensor_scalar(ksum[:, g:g + 1], accC[:, 132 + 129 * g + 128:132 + 129 * g + 129], SCALE ** 2 / N, None, ALU.mult))
                dve.wait_ge(kx_turned, g + 1)
                link(dve.tensor_scalar(Mpair[:, g, :, :], over(B[2][:, :], 128, 0, [[128, 4], [1, 128]]), 0.5, None, ALU.mult))
            for hq in range(4):
                link(dve.tensor_tensor(over(sel[:, hq, :, :], 128, 0, [[128, 4], [D, 4], [1, D]]),
                                       over(identx[:, hq, :], 128, 0, [[0, 4], [1, 4], [1, D]]),
                                       over(identx[:, hq, :], 128, 4, [[4, 4], [0, 4], [1, D]]), ALU.add))
            dve.sem_inc(big_v, 1)

            def q_weigh(t, b, i):
                dve.wait_ge(q_T.sem, q_T.done(t))
                dve.wait_ge(q_nr.sem, q_nr.ago(t, 1))
                for g in range(2):
                    ins = dve.scalar_tensor_tensor(TQ[:, g, :], B[4][:, g * P:(g + 1) * P], ksum[:, g:g + 1],
                                                   qT_all[:, g, ds(t * P, P)], ALU.add, ALU.mult)
                ins.then_inc(q_tq.sem, 1)

            def q_divide(t, b, i):
                dve.wait_ge(q_nr.sem, q_nr.done(t))
                dve.wait_ge(q_rn.sem, q_rn.ago(t, 1))
                dve.tensor_scalar(nn[:, :, :], over(B[4][:, :], 128, 2 * P, [[P, 2], [1, P]]), SCALE ** 4, None,
                                  ALU.add).then_inc(q_nn.sem, 1)
                dve.wait_ge(q_nn.sem, q_nn.done(t))
                dve.wait_ge(q_yev.sem, q_yev.ago(t, 1))
                dve.reciprocal(rnn[:, :, :], nn[:, :, :]).then_inc(q_rn.sem, 1)
                dve.wait_ge(q_rn.sem, q_rn.done(t))
                dve.wait_ge(q_ym.sem, q_ym.done(t))
                dve.wait_ge(q_pm.sem, q_pm.ago(t, 1))
                for g in range(2):
                    ins = dve.scalar_tensor_tensor(yT[:, g, :], psN[b][:, g * P:(g + 1) * P], vsum[:, g:g + 1],
                                                   rnn[:, g, :], ALU.add, ALU.mult)
                ins.then_inc(q_yev.sem, 1)

            def q_residual(t, b, i):
                dve.wait_ge(q_pm.sem, q_pm.done(t))
                dve.tensor_tensor(at(mixo, t), B[7][0:P, 0:C], at(mixo, t), ALU.add).then_inc(q_mo.sem, 1)
            dve.wait_ge(xb_in, 80)
            dve.wait_ge(k_qk.sem, k_qk.done(T - 1))
            pipeline(dve, T, 2, (beside_q(g_onehot), 1), (q_weigh, 1), (q_residual, 0), (q_divide, 1), (beside_q(g_add), 0))
            last_sets(g_onehot)
            last_sets(g_add)

            def redo_onehot(m, j, i):
                dve.wait_ge(r_mm.sem, r_mm.ago(m, 4))
                dve.tensor_scalar(onehot[:, 0, j, :], iota_bf[:, :], dloc_tile[:, ds(m, 1)], None, ALU.is_equal).then_inc(r_oh.sem, 1)

            def redo_add(m, j, i):
                first = dve.value_load(base_row[0:1, ds(m, 1)], min_val=0, max_val=N - 1)
                dve.wait_ge(r_mm.sem, r_mm.done(m))
                dve.wait_ge(r_acc.sem, r_acc.ago(m, 1))
                dve.tensor_tensor(acc[:, :, ds(first, EP)], acc[:, :, ds(first, EP)],
                                  over(psG[j % 2][:, :], 128, 0, [[EP, 2], [1, EP]]), ALU.add)
                dve.tensor_tensor(wsum[:, ds(first, EP)], wsum[:, ds(first, EP)], psG[j % 2][0:24, 2 * EP:3 * EP],
                                  ALU.add).then_inc(r_acc.sem, 1)
            dve.wait_ge(g_acc.sem, g_acc.done(SETS - 1))
            with if_spread(dve):
                dve.memset(acc[:, :, :], 0.0)
                dve.memset(wsum[:, :], 0.0).then_inc(big_v, 1)
                dve.wait_ge(big_v, 8)
                pipeline(dve, ET, 4, (redo_onehot, 2), (redo_add, 0))
                dve.wait_ge(r_acc.sem, r_acc.done(ET - 1))
            dve.sem_inc(g_final, 1)

            def c_tile(t, b, i):
                dve.wait_ge(c_s.sem, c_s.done(t))
                dve.wait_ge(c_rs.sem, c_rs.ago(t, 1))
                dve.tensor_scalar(cs[:, :, :], over(B[2][:, :], 128, 0, [[P, 2], [1, P]]), 1e-16, None, ALU.add).then_inc(c_s1.sem, 1)
                dve.wait_ge(c_s1.sem, c_s1.done(t))
                dve.wait_ge(c_gt.sem, c_gt.ago(t, 1))
                dve.reciprocal(crs[:, :, :], cs[:, :, :]).then_inc(c_rs.sem, 1)
                dve.wait_ge(c_rs.sem, c_rs.done(t))
                dve.wait_ge(c_tr.sem, c_tr.ago(t, 1))
                dve.tensor_tensor(cg[:, :, :], acc[:, :, ds(t * P, P)], crs[:, :, :], ALU.mult).then_inc(c_gt.sem, 1)
                dve.wait_ge(c_tr.sem, c_tr.done(t))
                dve.tensor_tensor(at(mixo, t), B[3][0:P, 0:C], at(mixo, t), ALU.add).then_inc(c_x1.sem, 1)
                dve.wait_ge(c_x1.sem, c_x1.done(t))
                gate()
                dve.bn_stats(at(st_all, t), at(mixo, t))
            dve.wait_ge(q_mo.sem, q_mo.done(T - 1))
            pairs(dve, c_tile)
            layer_norm_stats(2)

            dve.wait_ge(late_in, 48)
            dve.wait_ge(c_gt.sem, c_gt.done(T - 1))

            def d_norm(t, b, i):
                dve.wait_ge(d_tr.sem, d_tr.ago(t, 2))
                dve.tensor_scalar(dxn[:, b, :], at(mixo, t), rstd[:, ds(t, 1)], nmr[:, ds(t, 1)],
                                  ALU.mult, ALU.add).then_inc(d_xn.sem, 1)

            def d_bias(t, b, i):
                for hf in range(2):
                    dve.wait_ge(d_mm.sem, d_mm.done(t * 2 + hf))
                    dve.wait_ge(d_ge.sem, d_ge.ago(t * 2 + hf, 4))
                    dve.tensor_tensor(hp[:, b, 512 * hf:512 * hf + 512], B[psH[b] + hf][0:P, :],
                                      b1_bc[:, 512 * hf:512 * hf + 512], ALU.add).then_inc(d_hb.sem, 1)

            def d_evac(t, b, i):
                dve.wait_ge(d_ht.sem, d_ht.done(t * 2))
                dve.wait_ge(d_lm.sem, d_lm.ago(t, 1))
                dve.tensor_copy(hT[:, 0:4, :], over(B[5][:, :], 128, 0, [[P, 4], [1, P]])).then_inc(d_e0.sem, 1)

            def d_logits(t, b, i):
                dve.wait_ge(d_lm.sem, d_lm.done(t))
                dve.tensor_tensor(at(lg_all, t), B[7][0:P, 0:NE], bg_bc[:, :], ALU.add).then_inc(d_lg.sem, 1)
            pipeline(dve, T, 2, (d_norm, 4), (d_bias, 2), (d_logits, 0), (d_evac, 1))

            dve.wait_ge(d_lg.sem, d_lg.done(T - 1))
            link(dve.tensor_reduce(r_e[:, :], lg_all[:, :, :], AX.X, ALU.max))
            link(dve.tensor_tensor(r_a[:, :, :], lg_all[:, :, :], over(r_e[:, :], P, 0, [[1, T], [0, NE]]), ALU.subtract))
            dve.sem_inc(r_shifted, 1)
            dve.wait_ge(big_s, 2)
            link(dve.tensor_reduce(r_e[:, :], ex[:, :, :], AX.X, ALU.add))
            link(dve.reciprocal(prob[:, :], r_e[:, :]))
            link(dve.tensor_copy(over(pay[:, :, :], P, 1, [[2, T]]).bitcast(F32), prob[:, :]))
            link(dve.tensor_scalar(r_a[:, :, :], ex[:, :, :], 1.0, -8.0, ALU.is_ge, ALU.mult))
            link(dve.tensor_tensor(r_b[:, :, :], r_a[:, :, :], over(iota8[:, :], P, 0, [[0, T], [1, NE]]), ALU.add))
            link(dve.tensor_reduce(r_e[:, :], r_b[:, :, :], AX.X, ALU.min))
            link(dve.tensor_tensor(r_a[:, :, :], r_b[:, :, :], over(r_e[:, :], P, 0, [[1, T], [0, NE]]), ALU.is_equal))
            dve.sem_inc(r_chosen, 1)
            dve.wait_ge(r_counts, 1)
            link(dve.tensor_copy(r_c[:, :, :], over(B[3][:, :], P, 0, [[1, NE], [NE, T]])))
            for e in range(NE):
                link(dve.tensor_tensor_scan(r_d[:, e, :], rones[:, 0:T], r_c[:, e, :], 0.0, ALU.mult, ALU.add))
            link(dve.tensor_scalar(r_g[:, :], over(r_d[:, :, :], P, T - 1, [[T, NE]]), 127.0, None, ALU.add))
            link(dve.tensor_scalar(r_g[:, :], r_g[:, :], 7, 7, ALU.arith_shift_right, ALU.arith_shift_left))
            link(dve.tensor_copy(r_f[:, :], r_g[:, :]))
            link(dve.tensor_tensor_scan(r_h[:, :], rones[:, 0:NE], r_f[:, :], 0.0, ALU.mult, ALU.add))
            link(dve.tensor_tensor(r_f[:, :], r_h[:, :], r_f[:, :], ALU.subtract))
            link(dve.tensor_tensor(r_c[:, :, :], r_d[:, :, :], r_c[:, :, :], ALU.subtract))
            link(dve.tensor_tensor(r_b[:, :, :], over(B[2][:, :], P, 0, [[NE, T], [1, NE]]),
                                   over(r_c[:, :, :], P, 0, [[1, T], [T, NE]]), ALU.add))
            link(dve.tensor_tensor(r_b[:, :, :], r_b[:, :, :], over(r_f[:, :], P, 0, [[0, T], [1, NE]]), ALU.add))
            link(dve.tensor_tensor(r_b[:, :, :], r_b[:, :, :], r_a[:, :, :], ALU.mult))
            link(dve.tensor_reduce(r_e[:, :], r_b[:, :, :], AX.X, ALU.add))
            link(dve.tensor_copy(slot_i[:, :], r_e[:, :]))
            dve.sem_inc(routed, 1)
            link(dve.tensor_tensor(ev32[:, :, :], over(s128[:, :], 1, 0, [[1, ST], [0, NE]]),
                                   over(r_h[:, :], 1, 0, [[0, ST], [1, NE]]), ALU.is_ge))
            link(dve.tensor_reduce(rexp[:, :], ev32[:, :, :], AX.X, ALU.add))
            link(dve.tensor_scalar(rexp[:, :], rexp[:, :], float(NE - 1), float(C), ALU.min, ALU.mult))
            link(dve.tensor_copy(experts_i[:, :], rexp[:, :]))
            dve.wait_ge(d_hout.sem, d_hout.done(T - 1))
            for b in range(4):
                link(dve.memset(hsb[b][:, :], 0.0))
            dve.sem_inc(routed, 1)

            dve.wait_ge(order_in, 16)

            def e_evac(s, b, i):
                dve.wait_ge(e_tr.sem, e_tr.done(s * 2))
                dve.wait_ge(e_mm.sem, e_mm.ago(s, 2))
                dve.tensor_copy(hsT[:, b % 2, 0, :], B[4 + 2 * (b % 2)][:, :]).then_inc(e_e0.sem, 1)

            def e_out(s, b, i):
                col = dve.value_load(experts_i[0:1, ds(s, 1)], min_val=0, max_val=(NE - 1) * C)
                dve.wait_ge(e_mm.sem, e_mm.done(s))
                dve.wait_ge(e_o.sem, e_o.ago(s, 1))
                dve.tensor_tensor(t1[:, :], B[2 + b % 2][:, 0:C], bd_bc[:, ds(col, C)], ALU.add).then_inc(e_t1.sem, 1)
                dve.wait_ge(e_scd.sem, e_scd.ago(s, 2))
                dve.wait_ge(e_t1.sem, e_t1.done(s))
                dve.scalar_tensor_tensor(so[:, b % 2, :], t1[:, :], at(order_sb, s, 1, 2).bitcast(F32), hsb[b][:, HID:HROW],
                                         ALU.mult, ALU.add).then_inc(e_o.sem, 1)
            pipeline(dve, ST, 4, (e_evac, 1), (e_out, 0))

        @block.tensor
        def _(pe):
            pe.wait_ge(pool_chain, 2)
            pe.wait_ge(big_v, 1)

            def a_front(t, b, i):
                pe.wait_ge(a_xn.sem, a_xn.done(t))
                pe.wait_ge(a_xs.sem, a_xs.ago(t, 2))
                for k in range(2):
                    ins = pe.transpose(B[2 + b][:, k * P:(k + 1) * P], xn[:, b, 128 * k:128 * k + 128], ident[0:P, 0:P])
                ins.then_inc(a_tr.sem, 1)

            def a_back(t, b, i):
                pe.wait_ge(a_xs.sem, a_xs.done(t))
                pe.wait_ge(a_raw.sem, a_raw.ago(t, 2))
                for k in range(2):
                    ins = pe.matmul(B[4 + b][0:P, 0:XW], xs[:, b, k, :], W_sb[:, k, :], start=(k == 0), stop=(k == 1))
                ins.then_inc(a_mm.sem, 1)
            skewed(pe, a_front, a_back)

            def g_set(u, b, i):
                pe.wait_ge(rows_in[b], i * (16 * SLOTS) + 16 * SLOTS)
                pe.wait_ge(g_oh.sem, g_oh.done(u))
                pe.wait_ge(g_acc.sem, g_acc.ago(u, 2))
                for c in range(2):
                    for j in range(SLOTS):
                        for part in range(3):
                            pe.matmul(psG[b][:, EP * c:EP * c + EP], rows[:, b, j, part * C + 128 * c:part * C + 128 * c + 128],
                                      onehot[:, b, j, :], start=(j == 0 and part == 0), stop=(j == SLOTS - 1 and part == 2))
                for j in range(SLOTS):
                    ins = pe.matmul(psG[b][0:24, 2 * EP:3 * EP], rows[:, b, j, 3 * C:ROW],
                                    onehot[:, b, j, :], start=(j == 0), stop=(j == SLOTS - 1))
                ins.then_inc(g_mm.sem, 1)

            pe.wait_ge(consts, 1)
            pe.wait_ge(c_in, 112)
            pe.wait_ge(big_v, 6)
            for bnk in (4, 5, 6):
                pe.matmul(B[bnk][:, :], Mdiag[:, 0, :], over(Mdiag[:, :, :], 128, 0, [[0, 4], [1, 128]]), start=True, stop=True)

            def k_front(t, b, i):
                pe.wait_ge(k_xs.sem, k_xs.done(t))
                pe.wait_ge(k_qkv.sem, k_qkv.ago(t, 1))
                for k in range(2):
                    pe.matmul(B[2][0:P, :], kxs[:, b, k, :], WqkvT_sb[:, k, 0:512], start=(k == 0), stop=(k == 1))
                for k in range(2):
                    ins = pe.matmul(B[3][0:P, 0:C], kxs[:, b, k, :], WqkvT_sb[:, k, 512:768], start=(k == 0), stop=(k == 1))
                ins.then_inc(k_mm.sem, 1)

            def k_turn(t, b, i):
                pe.wait_ge(k_kn.sem, k_kn.done(t))
                pe.wait_ge(k_qk.sem, k_qk.ago(t, 1))
                for g in range(2):
                    ins = pe.transpose(B[7][:, g * P:(g + 1) * P], qn[:, 128 * g:128 * g + 128], ident[0:P, 0:P])
                ins.then_inc(k_qt.sem, 1)

            def k_back(t, b, i):
                v = qkv[:, b, 2 * C:3 * C]
                pe.wait_ge(k_kkv.sem, k_kkv.done(t))
                pe.wait_ge(k_kc.sem, k_kc.done(t))
                for g in range(2):
                    for hq in range(4):
                        h = 4 * g + hq
                        pe.matmul(B[4 + g][D * hq:D * hq + D, :], v[:, D * h:D * h + D], kkx[b][:, h, 0:512],
                                  start=False, stop=False, skip_group_check=True)
                for g in range(2):
                    for hq in range(4):
                        h = 4 * g + hq
                        pe.matmul(B[6][D * hq:D * hq + D, 66 * g:66 * g + 65], v[:, D * h:D * h + D],
                                  kkx[b][:, h, 512:577], start=False, stop=False, skip_group_check=True)
                for g in range(2):
                    kn = kc[:, b, 128 * g:128 * g + 128]
                    pe.matmul(B[6][:, 132 + 129 * g:132 + 129 * g + 128], kn, kn, start=False, stop=False, skip_group_check=True)
                    ins = pe.matmul(B[6][:, 132 + 129 * g + 128:132 + 129 * g + 129], kn, kkx[b][:, 0, 576:577],
                                    start=False, stop=False, skip_group_check=True)
                ins.then_inc(k_acc.sem, 1)
            pipeline(pe, T, 2, (k_back, 0), (k_front, 2), (g_set, 1), (k_turn, 1))

            for g in range(2):
                pe.wait_ge(kx_ready, 1 + g)
                for G in range(4):
                    ins = pe.transpose(B[2][:, 128 * G:128 * G + 128], KX[:, G, :], ident[:, :])
                ins.then_inc(kx_turned, 1)
            pe.wait_ge(big_v, 7)

            def q_tile(t, b, i):
                pe.wait_ge(q_f0.sem, q_f0.done(t))
                pe.wait_ge(q_yev.sem, q_yev.ago(t, 2))
                pe.wait_ge(q_nn.sem, q_nn.ago(t, 1))
                pe.sem_inc(waited["pe"], 1)
                ps = psN[b]
                for g in range(2):
                    pe.matmul(ps[:, g * P:(g + 1) * P], Mdiag[:, g, :], F0[:, b, g, :], start=(g == 0), stop=False, skip_group_check=True)
                for g in range(2):
                    pe.matmul(ps[:, g * P:(g + 1) * P], Mlin[:, g, :], qT_all[:, g, ds(t * P, P)], start=False, stop=False, skip_group_check=True)
                for g in range(2):
                    ins = pe.matmul(B[4][:, g * P:(g + 1) * P], Mgram[:, g, :], qT_all[:, g, ds(t * P, P)], start=True, stop=True)
                ins.then_inc(q_T.sem, 1)

                def products(h):
                    g, hq = h // 4, h % 4
                    pe.wait_ge(q_f.sem, q_f.done(t * 8 + h))
                    for G in range(4):
                        ins = pe.matmul(ps[D * hq:D * hq + D, g * P:(g + 1) * P], Mpair[:, g, G, D * hq:D * hq + D],
                                        F[:, h, G, :], start=False, stop=(G == 3), skip_group_check=True)
                    return ins

                for h in range(H):
                    pe.wait_ge(q_f.sem, q_f.ago(t * 8 + h, 2))
                    pe.sem_inc(waited["pe"], 1)
                    for G in range(4):
                        ins = pe.matmul(B[2 + h % 2][:, G * P:(G + 1) * P], sel[:, h % 4, G, :], qT_all[:, h // 4, ds(t * P, P)],
                                        start=True, stop=True)
                    ins.then_inc(q_s.sem, 1)
                    if h == 3:
                        pe.wait_ge(q_tq.sem, q_tq.done(t))
                        pe.matmul(over(B[4][:, :], 128, 2 * P, [[1, 2 * P]]), blockones[:, :], over(TQ[:, :, :], 128, 0, [[1, 2 * P]]),
                                  start=True, stop=True).then_inc(q_nr.sem, 1)
                    if h >= 2:
                        products(h - 2)
                products(H - 2)
                products(H - 1).then_inc(q_ym.sem, 1)

            def q_project(t, b, i):
                pe.wait_ge(q_yev.sem, q_yev.done(t))
                pe.wait_ge(q_mo.sem, q_mo.ago(t, 1))
                for g in range(2):
                    ins = pe.matmul(B[7][0:P, 0:C], yT[:, g, :], WprojT_sb[:, g, :], start=(g == 0), stop=(g == 1))
                ins.then_inc(q_pm.sem, 1)
            pipeline(pe, T, 2, (beside_q(g_set), 0), (q_project, 0), (q_tile, 1))
            last_sets(g_set)

            def redo_tile(m, j, i):
                if j % SLOTS == 0:
                    pe.wait_ge(redo_in[j // SLOTS], i * (16 * SLOTS) + 16 * SLOTS)
                pe.wait_ge(r_oh.sem, r_oh.done(m))
                pe.wait_ge(r_acc.sem, r_acc.ago(m, 2))
                for c in range(2):
                    for part in range(3):
                        pe.matmul(psG[j % 2][:, EP * c:EP * c + EP],
                                  rows[:, j // SLOTS, j % SLOTS, part * C + 128 * c:part * C + 128 * c + 128],
                                  onehot[:, 0, j % 4, :], start=(part == 0), stop=(part == 2))
                pe.matmul(psG[j % 2][0:24, 2 * EP:3 * EP], rows[:, j // SLOTS, j % SLOTS, 3 * C:ROW],
                          onehot[:, 0, j % 4, :], start=True, stop=True).then_inc(r_mm.sem, 1)
            with if_spread(pe):
                pipeline(pe, ET, 2 * SLOTS, (redo_tile, 0))

            pe.wait_ge(g_final, 1)

            def c_front(t, b, i):
                pe.wait_ge(c_s1.sem, c_s1.ago(t, 1))
                pe.sem_inc(waited["pe"], 1)
                for g in range(2):
                    ins = pe.matmul(B[2][:, g * P:(g + 1) * P], headsel[:, g, :], wsum[:, ds(t * P, P)], start=True, stop=True)
                ins.then_inc(c_s.sem, 1)

            def c_back(t, b, i):
                pe.wait_ge(c_gt.sem, c_gt.done(t))
                pe.wait_ge(c_x1.sem, c_x1.ago(t, 1))
                for g in range(2):
                    ins = pe.transpose(B[3][0:P, 128 * g:128 * g + 128], cg[:, g, :], ident[:, :])
                ins.then_inc(c_tr.sem, 1)
            skewed(pe, c_front, c_back)

            pe.wait_ge(late_in, 48)
            pe.wait_ge(c_in, 112)

            def d_turn(t, b, i):
                pe.wait_ge(d_xn.sem, d_xn.done(t))
                pe.wait_ge(d_xs.sem, d_xs.ago(t, 1))
                for k in range(2):
                    ins = pe.transpose(B[2][:, k * P:(k + 1) * P], dxn[:, b, 128 * k:128 * k + 128], ident[0:P, 0:P])
                ins.then_inc(d_tr.sem, 1)

            def d_hidden(t, b, i):
                pe.wait_ge(d_xs.sem, d_xs.done(t))
                for hf in range(2):
                    pe.wait_ge(d_hb.sem, d_hb.ago(t * 2 + hf, 4))
                    for k in range(2):
                        ins = pe.matmul(B[psH[b] + hf][0:P, :], dxs[:, b, k, :], W1_sb[:, k, 512 * hf:512 * hf + 512], start=(k == 0), stop=(k == 1))
                    ins.then_inc(d_mm.sem, 1)

            def d_turn_hidden(t, b, i):
                for hf in range(2):
                    pe.wait_ge(d_ge.sem, d_ge.done(t * 2 + hf))
                    pe.wait_ge((d_e0, d_e1)[hf].sem, d_e0.ago(t, 1))
                    for k in range(4):
                        ins = pe.transpose(B[5 + hf][:, k * P:(k + 1) * P], hb[b][:, 512 * hf + 128 * k:512 * hf + 128 * k + 128], ident[0:P, 0:P])
                    ins.then_inc(d_ht.sem, 1)

            def d_gate(t, b, i):
                pe.wait_ge(d_e0.sem, d_e0.done(t))
                pe.wait_ge(d_e1.sem, d_e1.done(t))
                pe.wait_ge(d_lg.sem, d_lg.ago(t, 1))
                for k in range(8):
                    ins = pe.matmul(B[7][0:P, 0:NE], hT[:, k, :], Wg_sb[:, k, :], start=(k == 0), stop=(k == 7))
                ins.then_inc(d_lm.sem, 1)
            pipeline(pe, T, 2, (d_turn, 3), (d_hidden, 2), (d_gate, 0), (d_turn_hidden, 1))

            pe.wait_ge(r_chosen, 1)
            pe.matmul(B[2][0:P, 0:T * NE], rtri[:, :], r_a[:, :, :].rearrange("p t e -> p (t e)"), start=True, stop=True)
            pe.matmul(B[3][0:P, 0:T * NE], rones[:, :], r_a[:, :, :].rearrange("p t e -> p (t e)"), start=True, stop=True).then_inc(r_counts, 1)

            pe.wait_ge(wd_in, 16 * NE)
            pe.wait_ge(big_v, 7)

            def e_turn(s, b, i):
                pe.wait_ge(hs_in[b], i * 16 + 16)
                for hf in range(2):
                    pe.wait_ge((e_e0, e_e1)[hf].sem, e_e0.ago(s, 2))
                    for k in range(4):
                        ins = pe.transpose(B[4 + 2 * (b % 2) + hf][:, 128 * k:128 * k + 128],
                                           hsb[b][:, 512 * hf + 128 * k:512 * hf + 128 * k + 128], ident[:, :])
                    ins.then_inc(e_tr.sem, 1)

            def e_product(s, b, i):
                col = pe.value_load(experts_i[0:1, ds(s, 1)], min_val=0, max_val=(NE - 1) * C)
                pe.wait_ge(e_e0.sem, e_e0.done(s))
                pe.wait_ge(e_e1.sem, e_e1.done(s))
                pe.wait_ge(e_t1.sem, e_t1.ago(s, 2))
                for k in range(8):
                    ins = pe.matmul(B[2 + b % 2][:, 0:C], hsT[:, b % 2, k // 4, 128 * (k % 4):128 * (k % 4) + 128], Wd_sb[:, k, ds(col, C)],
                                    start=(k == 0), stop=(k == 7))
                ins.then_inc(e_mm.sem, 1)
            pipeline(pe, ST, 4, (e_turn, 1), (e_product, 0))


def kernel(**inputs):
    import numpy as _np
    import concourse.bacc as _bacc
    from concourse import mybir as _mybir
    from concourse.bass_utils import run_bass_kernel_spmd as _run

    def edges(a, fill):
        return _np.concatenate([_np.asarray(a), _np.full(ET * EP - E, fill, _np.asarray(a).dtype)]).reshape(ET, EP)

    f = {k: _np.asarray(v) for k, v in inputs.items()}
    src, dst = edges(f["src"], 0), edges(f["dst"], -1)
    laid_out = {
        "x": f["x"], "src": src.T, "dst": dst.T, "dst0": dst[:, 0], "W": f["L0_gnn_W"],
        "a_src": f["L0_gnn_a_src"].reshape(-1), "WqkvT": f["L0_mix_Wqkv"].T, "bqkv": f["L0_mix_bqkv"],
        "WprojT": f["L0_mix_Wproj"].T, "bproj": f["L0_mix_bproj"], "temp": f["L0_mix_temperature"].reshape(-1),
        "W1": f["L0_ffn_W1"], "b1": f["L0_ffn_b1"], "Wg": f["L0_ffn_Wg"], "bg": f["L0_ffn_bg"],
        "Wd": f["L0_ffn_Wd"], "bd": f["L0_ffn_bd"].reshape(-1),
    }
    nc = _bacc.Bacc("TRN2", target_bir_lowering=False, num_devices=1)
    arrays, args = {}, []
    for name, a in laid_out.items():
        a = _np.ascontiguousarray(a)
        arrays[f"in_{name}"] = a
        args.append(nc.dram_tensor(f"in_{name}", a.shape, _mybir.dt.from_np(a.dtype), kind="ExternalInput").ap())
    args.append(nc.dram_tensor("out_0", (N, C), _mybir.dt.float32, kind="ExternalOutput").ap())
    args.append(nc.dram_tensor("table", (N, ROW), _mybir.dt.bfloat16, kind="Internal").ap())
    args.append(nc.dram_tensor("hidden", (N, HROW), _mybir.dt.float32, kind="Internal").ap())
    args.append(nc.dram_tensor("order", (ST * 128, 2), _mybir.dt.int32, kind="Internal").ap())
    build(nc, *args)
    r = _run(nc, [arrays], core_ids=[0])
    return r.results[0]["out_0"]
```

```python
import concourse.bass as bass
from concourse import mybir
from contextlib import ExitStack

F32, BF16, I32 = mybir.dt.float32, mybir.dt.bfloat16, mybir.dt.int32
ALU, ACT, AX = mybir.AluOpType, mybir.ActivationFunctionType, mybir.AxisListType
ds = bass.ds

N, C, H, D = 3125, 256, 8, 32
P, T = 125, 25
E = 2 * 25000 + N
EP = 128
ET = -(-E // EP)
SLOTS = 8
SETS = ET // SLOTS
WIN = 80
BETWEEN = range(T, SETS - T)
XW = C + H
ROW = 3 * XW
NACC = N + EP
HID, NE = 1024, 8
ST = (N + NE * 127) // 128
HROW = HID + C
NOBODY = 4096
FD = 17
KW = FD * D
KROW = KW + D + 2
LN_EPS = 1e-5
SCALE = float(D) ** 0.25
PRE = 8


class Stage:

    def __init__(self, sem, pre=PRE):
        self.sem, self.pre = sem, pre

    def done(self, n):
        return n + (1 + self.pre)

    def ago(self, n, depth):
        return n + (1 + self.pre - depth)


def build(nc, x, src, dst, dst0, W, a_src, WqkvT, bqkv, WprojT, bproj, temp, W1, b1, Wg, bg, Wd, bd, out,
          table, hidden):
    with ExitStack() as ctx:
        def sb(name, shape, dt=F32):
            return ctx.enter_context(nc.sbuf_tensor(name, shape, dt))

        def bank(name):
            return ctx.enter_context(nc.psum_tensor(name, [128, 512], F32))

        def region(*alternatives):
            found, most = [], 0
            for tensors in alternatives:
                with ExitStack() as st:
                    size = 0
                    for name, shape, dt in tensors:
                        found.append(st.enter_context(nc.sbuf_tensor(name, shape, dt)))
                        n = 2 if dt == BF16 else 4
                        for s in shape[1:]:
                            n *= s
                        size += -(-n // 32) * 32
                most = max(most, size)
            sb(f"region_{found[0].name}", [128, most // 4])
            return found

        def over(a, parts, off, dims):
            return bass.AP(a.tensor, a.offset + off, [[a.ap[0][0], parts], *dims])

        def at(a, t, lo=0, hi=None):
            hi = a.shape[-1] if hi is None else hi
            return a[:, ds(t, 1), lo:hi].rearrange("p o c -> p (o c)")

        ident = sb("ident", [128, 128])
        W_sb, slot_i, slot_hi, slot_lo, order_f, order_i, order_p = region(
            [("W_sb", [128, 2, XW], F32)],
            [("slot_i", [P, T], I32), ("slot_hi", [P, T], F32), ("slot_lo", [P, T], F32), ("order_f", [128, ST], F32),
             ("order_i", [128, ST], I32), ("order_p", [128, ST], F32)])
        WprojT_sb = sb("WprojT_sb", [128, 2, C])
        WqkvT_sb, bqkv_bc, F1 = region(
            [("WqkvT_sb", [128, 2, 3 * C], F32), ("bqkv_bc", [P, 3 * C], F32)],
            [("F1", [128, 4, 4, P], F32)])
        bproj_bc = sb("bproj_bc", [P, C])
        Wg_sb = sb("Wg_sb", [128, 8, 32])
        bg_bc = sb("bg_bc", [P, NE])
        temp_bc = sb("temp_bc", [P, H])
        iota_bf = sb("iota_bf", [128, 128], BF16)
        doff = sb("doff", [128, SLOTS])
        src_sb = sb("src_sb", [128, ET], I32)
        dloc_set = sb("dloc_set", [128, ET])
        dloc_tile = sb("dloc_tile", [128, ET])
        span = sb("span", [128, 1])
        span_all = sb("span_all", [128, 1])
        span_i = sb("span_i", [128, 1], I32)
        base_row = sb("base_row", [1, ET], I32)
        partsum = sb("partsum", [128, NE])
        gatesum = sb("gatesum", [128, NE])
        rtri = sb("rtri", [P, P])
        rones = sb("rones", [P, P])
        blockones = sb("blockones", [128, 128])
        headmask = sb("headmask", [128, 128])
        normfac = sb("normfac", [P, 2 * H])
        normeps = sb("normeps", [P, 2 * H])
        Mpair = sb("Mpair", [128, 2, 4, 128])
        Mdiag = sb("Mdiag", [128, 2, 128])
        Mlin = sb("Mlin", [128, 2, 128])
        Mgram = sb("Mgram", [128, 2, 128])
        ksum = sb("ksum", [128, 2])
        vsum = sb("vsum", [128, 2])
        st_all = sb("st_all", [P, T, 6])
        mean = sb("mean", [P, T])
        delta = sb("delta", [P, T])
        var = sb("var", [P, T])
        rstd = sb("rstd", [P, T])
        nmr = sb("nmr", [P, T])
        iidx = sb("iidx", [128, 2, SLOTS], I32)
        onehot = sb("onehot", [128, 2, SLOTS, EP], BF16)
        hmax = sb("hmax", [P, H])
        hmaxall = sb("hmaxall", [P, H])
        prob = sb("prob", [P, T])
        node_i = sb("node_i", [P, T], I32)
        node_f = sb("node_f", [P, T])
        experts_i = sb("experts_i", [1, ST], I32)

        raw_all, kkx0, qkv, ss, ss2, nrm, rcp, rn, mixo = region(
            [("raw_all", [P, T, XW], F32)],
            [("kkx0", [P, H, KROW], F32), ("qkv", [P, 2, 3 * C], F32), ("ss", [P, 16], F32), ("ss2", [P, 16], F32),
             ("nrm", [P, 16], F32), ("rcp", [P, 16], F32), ("rn", [P, 16], F32)],
            [("mixo", [P, T, C], F32)])
        (tb_all, acc, wsum, hp, h0, h1, hT, dxn, dxs, gl,
         lg_all, ex, r_a, r_b, r_c, r_d, r_e, r_f, r_g, r_h, ev32, is_lo, is_hi, spread, hs0, hs1, hs2, hs3) = region(
            [("tb_all", [P, T, ROW], BF16)],
            [("acc", [128, 2, NACC], F32), ("wsum", [128, NACC], F32)],
            [("hp", [P, 2, HID], F32), ("h0", [P, HID], F32), ("h1", [P, HID], F32), ("hT", [128, 8, P], F32),
             ("dxn", [P, 2, C], F32), ("dxs", [128, 2, 2, P], F32), ("gl", [128, P], F32),
             ("lg_all", [P, T, NE], F32), ("ex", [P, T, NE], F32), ("r_a", [P, T, NE], F32), ("r_b", [P, T, NE], F32),
             ("r_c", [P, NE, T], F32), ("r_d", [P, NE, T], F32), ("r_e", [P, T], F32), ("r_f", [P, NE], F32),
             ("r_g", [P, NE], I32), ("r_h", [P, NE], F32), ("ev32", [1, ST, NE], F32)],
            [("is_lo", [P, T, 128], F32), ("is_hi", [P, T, ST], F32), ("spread", [P, T, 2, ST], F32)],
            [(f"hs{b}", [128, HROW], F32) for b in range(4)])
        (xnT_all, W1_sb, b1_bc, bd_bc, TQ, nn, rnn, yT) = region(
            [("xnT_all", [128, 2, N], F32)],
            [("W1_sb", [128, 2, HID], F32), ("b1_bc", [P, HID], F32), ("bd_bc", [128, NE * C], F32),
             ("TQ", [128, 2, P], F32), ("nn", [128, 2, P], F32), ("rnn", [128, 2, P], F32), ("yT", [128, 2, P], F32)])
        (x_all, xn, xs, yw, y1, w1, waste, baseb, asrc_bc, wa_prod, iota_i,
         q_all, rows, kkx1, kd, kc, sq, kxs,
         q_all2, rows2, qq, F0h, qs, qd, qT, F0,
         q_all3, rows3, KV, KL,
         Wd_sb, hsT, so, t1, ix, c_acc, c_w, c_den, c_rcp, c_out) = region(
            [("x_all", [P, T, C], F32), ("xn", [P, 2, C], F32), ("xs", [128, 2, 2, P], F32), ("yw", [P, 4, C], F32),
             ("y1", [P, 4, C], F32), ("w1", [P, T, H], F32), ("waste", [128, ET], I32), ("baseb", [128, ET], I32), ("asrc_bc", [128, C], F32),
             ("wa_prod", [128, 2, C], F32), ("iota_i", [128, 128], I32)],
            [("q_all", [P, T, C], F32), ("rows", [128, 2, SLOTS, ROW], BF16), ("kkx1", [P, H, KROW], F32),
             ("kd", [P, H, 48], F32), ("kc", [P, 2, C], F32),
             ("sq", [P, 2 * C], F32), ("kxs", [128, 2, 2, P], F32)],
            [("q_all2", [P, T, C], F32), ("rows2", [128, 2, SLOTS, ROW], BF16), ("qq", [P, H, 16 * D], F32),
             ("F0h", [128, 4, 4, P], F32), ("qs", [P, C], F32), ("qd", [P, H, 48], F32), ("qT", [128, 2, 2, P], F32),
             ("F0", [128, 2, 2, P], F32)],
            [("q_all3", [P, T, C], F32), ("rows3", [128, 2, SLOTS, ROW], BF16), ("KV", [128, 2, FD, D], F32),
             ("KL", [128, 2, 3, D], F32)],
            [("Wd_sb", [128, 8, NE * C], F32), ("hsT", [128, 2, 2, 512], F32), 
             ("so", [128, 2, C], F32), ("t1", [128, C], F32), ("ix", [128, 8], I32),
             ("c_acc", [128, 2, 2, P], F32), ("c_w", [128, 2, P], F32), ("c_den", [P, 4, H], F32),
             ("c_rcp", [P, 4, H], F32), ("c_out", [P, 2, C], F32)])
        iota8 = sb("iota8", [P, NE])
        iota8i = sb("iota8i", [P, NE], I32)
        s128 = sb("s128", [1, ST])
        s128i = sb("s128i", [1, ST], I32)
        rexp = sb("rexp", [1, ST])
        hb = [h0, h1]
        F = [F0h, F1]
        kkx = [kkx0, kkx1]
        hsb = [hs0, hs1, hs2, hs3]

        B = [bank(f"bank{i}") for i in range(8)]
        psG = [B[0], B[1]]
        psN = [B[5], B[6]]
        psH = [3, 0]

        names = []

        def sem(name):
            names.append(name)
            return ctx.enter_context(nc.semaphore(name))

        stages = []

        def stage(name, pre=PRE):
            s = Stage(sem(name), pre)
            stages.append(s)
            return s

        w_in, e_in, c_in, late_in, wd_in = (sem(s) for s in ("w_in", "e_in", "c_in", "late_in", "wd_in"))
        x_in = [sem(f"x_in{c}") for c in range(5)]
        tab_out, x1_out, hidden_out = (sem(s) for s in ("tab_out", "x1_out", "hidden_out"))
        rows_in = [sem("rows_in0"), sem("rows_in1")]
        redo_in = [sem("redo_in0"), sem("redo_in1")]
        xb_out, xb_in, xb_made, g_final = sem("xb_out"), sem("xb_in"), sem("xb_made"), sem("g_final")
        hs_in = [sem(f"hs_in{b}") for b in range(4)]
        out_done = [sem(f"out_done{b}") for b in range(4)]
        dve_chain, pool_chain, kx_ready, kx_turned, r_shifted, r_chosen, r_counts, r_spread, r_ordered = (sem(s) for s in (
            "dve_chain", "pool_chain", "kx_ready", "kx_turned", "r_shifted", "r_chosen", "r_counts", "r_spread", "r_ordered"))
        consts, routed, acc_clear = sem("consts"), sem("routed"), sem("acc_clear")
        waited = {k: sem(f"waited_{k}") for k in ("act", "dve", "pool", "pe")}

        (a_xn, a_tr, a_xs, a_xnT, a_mm, a_raw, a_y, a_hi, a_r1, a_mid, a_lo) = (stage(s) for s in (
            "a_xn", "a_tr", "a_xs", "a_xnT", "a_mm", "a_raw", "a_y", "a_hi", "a_r1", "a_mid", "a_lo"))
        g_idx, g_oh, g_mm, g_acc = (stage(s) for s in ("g_idx", "g_oh", "g_mm", "g_acc"))
        g_do, g_dist = stage("g_do"), stage("g_dist")
        r_idx, r_oh, r_acc = stage("r_idx"), stage("r_oh"), stage("r_acc")
        r_mm = stage("r_mm", 12)
        (k_xs, k_mm, k_qkv, k_sq, k_ss, k_mx, k_nrm, k_rc, k_rn, k_kn, k_kkv, k_kc, k_acc) = (
            stage(s) for s in ("k_xs", "k_mm", "k_qkv", "k_sq", "k_ss", "k_mx", "k_nrm", "k_rc", "k_rn", "k_kn", "k_kkv",
                               "k_kc", "k_acc"))
        (q_qd, q_t, q_qq, q_s, q_qT, q_f0, q_f, q_p, q_T, q_tq, q_nr, q_nn, q_rn, q_yev, q_pm, q_mo) = (
            stage(s) for s in ("q_qd", "q_t", "q_qq", "q_s", "q_qT", "q_f0", "q_f", "q_p", "q_T", "q_tq", "q_nr", "q_nn",
                               "q_rn", "q_yev", "q_pm", "q_mo"))
        (c_in1, c_mm, c_dn, c_rc, c_q, c_x1) = (stage(s) for s in ("c_in1", "c_mm", "c_dn", "c_rc", "c_q", "c_x1"))
        (d_xn, d_tr, d_xs, d_mm, d_hb, d_ge, d_hout, d_ht, d_e0, d_e1, d_lm, d_gl, d_ls, d_lg) = (stage(s) for s in (
            "d_xn", "d_tr", "d_xs", "d_mm", "d_hb", "d_ge", "d_hout", "d_ht", "d_e0", "d_e1", "d_lm", "d_gl", "d_ls", "d_lg"))
        (e_ix, e_tr, e_e0, e_e1, e_mm, e_t1, e_o, e_scd) = (stage(s) for s in (
            "e_ix", "e_tr", "e_e0", "e_e1", "e_mm", "e_t1", "e_o", "e_scd"))
        stats_v, stats_s = sem("stats_v"), sem("stats_s")
        weights_exp, logits_exp = sem("weights_exp"), sem("logits_exp")
        (head_cols, spans, span_max, span_int, hmax_tile, hmax_all, a_shifted, kkx_ones, matrices, sums_cleared) = (
            sem(s) for s in ("head_cols", "spans", "span_max", "span_int", "hmax_tile", "hmax_all", "a_shifted",
                             "kkx_ones", "matrices", "sums_cleared"))

        def pairs(e, body):
            with e.Fori(0, T // 2) as i:
                body(i * 2, 0, i)
                body(i * 2 + 1, 1, i)
            body(T - 1, 0, T // 2)

        def skewed(e, front, back):
            front(0, 0, 0)
            with e.Fori(0, T // 2) as i:
                front(i * 2 + 1, 1, i)
                back(i * 2, 0, i)
                front(i * 2 + 2, 0, i + 1)
                back(i * 2 + 1, 1, i)
            back(T - 1, 0, T // 2)

        def pipeline(e, count, unroll, *bodies):
            lead = max(l for _, l in bodies)

            def step(n, j, i):
                for body, l in bodies:
                    body(n + l, (j + l) % unroll, i + (j + l) // unroll)

            def edge(n):
                for body, l in bodies:
                    if 0 <= n + l < count:
                        body(n + l, (n + l) % unroll, (n + l) // unroll)
            for n in range(-lead, 0):
                edge(n)
            rounds = (count - lead) // unroll
            with e.Fori(0, rounds) as i:
                for j in range(unroll):
                    step(i * unroll + j, j, i)
            for n in range(rounds * unroll, count):
                edge(n)

        def beside_q(body):
            first = SETS - T

            def shifted(t, b, i):
                body(t + first, (first + b) % 2, i + (first + b) // 2)
            return shifted

        def if_spread(e):
            return e.If(e.value_load(span_i[0:1, 0:1], min_val=0, max_val=N) > WIN - 1)

        def row_bc(a, n, parts):
            return bass.AP(a.tensor, a.offset, [[0, parts], [1, n]])

        block = ctx.enter_context(nc.Block())

        @block.sync
        def _(sp):
            for c in range(5):
                if c == 3:
                    sp.dma_start(W_sb[:, :, 0:C], W.rearrange("(k p) n -> p k n", p=128)).then_inc(w_in, 16)
                    sp.dma_start(asrc_bc[:, :], row_bc(a_src, C, 128)).then_inc(w_in, 16)
                sp.dma_start(x_all[:, 5 * c:5 * c + 5, :],
                             x[5 * c * P:5 * (c + 1) * P, :].rearrange("(t p) c -> p t c", p=P)).then_inc(x_in[c], 16)
            for s in stages:
                sp.sem_inc(s.sem, s.pre)
            sp.dma_start(src_sb[:, :], src).then_inc(e_in, 16)
            sp.dma_start(waste[:, :], dst).then_inc(e_in, 16)
            sp.dma_start(baseb[:, :], row_bc(dst0, ET, 128)).then_inc(e_in, 16)
            sp.dma_start(base_row[:, :], row_bc(dst0, ET, 1)).then_inc(e_in, 16)
            sp.dma_start(WqkvT_sb[:, :, :], WqkvT.rearrange("(k p) n -> p k n", p=128)).then_inc(c_in, 16)
            sp.dma_start(WprojT_sb[:, :, :], WprojT.rearrange("(k p) n -> p k n", p=128)).then_inc(c_in, 16)
            sp.dma_start(bqkv_bc[:, :], row_bc(bqkv, 3 * C, P)).then_inc(c_in, 16)
            sp.dma_start(bproj_bc[:, :], row_bc(bproj, C, P)).then_inc(c_in, 16)
            sp.dma_start(temp_bc[:, :], row_bc(temp, H, P)).then_inc(c_in, 16)
            sp.dma_start(bg_bc[:, :], row_bc(bg, NE, P)).then_inc(c_in, 16)

            def table_out(t, b, i):
                sp.wait_ge(a_lo.sem, a_lo.done(t))
                sp.dma_start(table[ds(t * P, P), :], at(tb_all, t)).then_inc(tab_out, 16)
            pairs(sp, table_out)

            sp.wait_ge(xb_out, 80)
            sp.wait_ge(k_acc.sem, k_acc.done(T - 1))
            for c in range(5):
                sp.dma_start(mixo[:, 5 * c:5 * c + 5, :],
                             hidden[5 * c * P:5 * (c + 1) * P, HID:HROW].rearrange("(t p) c -> p t c", p=P)).then_inc(xb_in, 16)

            sp.wait_ge(k_mm.sem, k_mm.done(T - 1))
            sp.wait_ge(consts, 1)
            sp.dma_start(Wg_sb[:, :, 0:NE], Wg.rearrange("(k p) e -> p k e", p=128)).then_inc(late_in, 16)
            sp.dma_start(W1_sb[:, :, :], W1.rearrange("(k p) n -> p k n", p=128)).then_inc(late_in, 16)
            sp.dma_start(b1_bc[:, :], row_bc(b1, HID, P)).then_inc(late_in, 16)
            sp.dma_start(bd_bc[:, :], row_bc(bd, NE * C, 128)).then_inc(late_in, 16)
            sp.wait_ge(g_final, 1)
            sp.wait_ge(q_mo.sem, q_mo.done(T - 1))
            for e in range(NE):
                sp.dma_start(Wd_sb[:, :, e * C:(e + 1) * C], Wd[e].rearrange("(k p) c -> p k c", p=128)).then_inc(wd_in, 16)

            def x1_store(t, b, i):
                sp.wait_ge(c_x1.sem, c_x1.done(t))
                sp.dma_start(hidden[ds(t * P, P), HID:HROW], at(mixo, t)).then_inc(x1_out, 16)
            pairs(sp, x1_store)

            def h_store(t, b, i):
                sp.wait_ge(d_ge.sem, d_ge.done(t * 2 + 1))
                sp.dma_start(hidden[ds(t * P, P), 0:HID], hb[b][:, :]).then_inc(hidden_out, 16)
                sp.wait_ge(hidden_out, t * 16 + 16)
                sp.sem_inc(d_hout.sem, 1)
            pairs(sp, h_store)

            sp.wait_ge(x1_out, 16 * T)
            sp.wait_ge(tab_out, 16 * T)

            def out_stored(s, b, i):
                sp.wait_ge(out_done[b], i * 16 + 16)
                sp.sem_inc(e_scd.sem, 1)
            pipeline(sp, ST, 4, (out_stored, 0))

        @block.gpsimd
        def _(pool):
            n = [0]

            def link(ins):
                n[0] += 1
                ins.then_inc(pool_chain, 1)
                pool.wait_ge(pool_chain, n[0])

            def gate():
                pool.sem_inc(waited["pool"], 1)

            link(pool.memset(ident[:, :], 0.0))
            link(pool.affine_select(out=ident[:, :], in_=ident[:, :], compare_op=ALU.not_equal, fill=1.0, base=0,
                                    pattern=[[-1, 128]], channel_multiplier=1))
            link(pool.iota(iota_i[:, :], pattern=[[1, 128]], base=0, channel_multiplier=0))
            link(pool.tensor_copy(iota_bf[:, :], iota_i[:, :]))
            link(pool.iota(iota8i[:, :], pattern=[[1, NE]], base=0, channel_multiplier=0))
            link(pool.tensor_copy(iota8[:, :], iota8i[:, :]))
            link(pool.iota(s128i[:, :], pattern=[[128, ST]], base=0, channel_multiplier=0))
            link(pool.tensor_copy(s128[:, :], s128i[:, :]))
            link(pool.iota(node_i[:, :], pattern=[[P, T]], base=-NOBODY, channel_multiplier=1))
            link(pool.tensor_copy(node_f[:, :], node_i[:, :]))
            link(pool.memset(headmask[:, :], 0.0))
            for hq in range(4):
                link(pool.memset(headmask[D * hq:D * hq + D, D * hq:D * hq + D], 1.0))
            link(pool.tensor_copy(blockones[:, :], headmask[:, :]))
            link(pool.memset(rones[:, :], 1.0))
            link(pool.affine_select(out=rtri[:, :], in_=rones[:, :], compare_op=ALU.is_gt, fill=0.0, base=0,
                                    pattern=[[1, P]], channel_multiplier=-1))
            link(pool.memset(Wg_sb[:, :, :], 0.0))
            link(pool.memset(Mdiag[:, :, :], 0.0))
            pool.memset(Mlin[:, :, :], 0.0).then_inc(consts, 1)

            def keep_xnT(t, b, i):
                pool.wait_ge(a_xs.sem, a_xs.done(t))
                gate()
                pool.tensor_copy(xnT_all[:, :, ds(t * P, P)], xs[:, b, :, :]).then_inc(a_xnT.sem, 1)
            pairs(pool, keep_xnT)

            pool.wait_ge(hmax_tile, 1)
            pool.partition_all_reduce(hmaxall[:, :], hmax[:, :], P, bass.bass_isa.ReduceOp.max).then_inc(hmax_all, 1)

            pool.wait_ge(c_in, 96)
            pool.wait_ge(a_xn.sem, a_xn.done(T - 1))
            for c in range(5):
                pool.tensor_tensor(x_all[:, 5 * c:5 * c + 5, :], x_all[:, 5 * c:5 * c + 5, :],
                                   over(bproj_bc[:, :], P, 0, [[0, 5], [1, C]]), ALU.add).then_inc(xb_made, 1)
                pool.wait_ge(xb_made, c + 1)
                pool.dma_start(hidden[5 * c * P:5 * (c + 1) * P, HID:HROW].rearrange("(t p) c -> p t c", p=P),
                               x_all[:, 5 * c:5 * c + 5, :]).then_inc(xb_out, 16)
            pool.wait_ge(spans, 1)
            pool.partition_all_reduce(span_all[:, :], span[:, :], 128, bass.bass_isa.ReduceOp.max).then_inc(span_max, 1)

            pool.wait_ge(tab_out, 16 * T)
            pool.wait_ge(e_in, 64)
            pool.wait_ge(xb_out, 80)

            def gather(u, b, i):
                pool.wait_ge(g_mm.sem, g_mm.ago(u, 2))
                gate()
                pool.tensor_copy(iidx[:, b, :], src_sb[:, ds(u * SLOTS, SLOTS)]).then_inc(g_idx.sem, 1)
                pool.wait_ge(g_idx.sem, g_idx.done(u))
                gate()
                for j in range(SLOTS):
                    pool.indirect_dma_start(out=rows[:, b, j, :], out_offset=None, in_=table,
                                            in_offset=bass.IndirectOffsetOnAxis(ap=iidx[:, b, j:j + 1], axis=0)
                                            ).then_inc(rows_in[b], 16)
            pipeline(pool, SETS, 2, (gather, 0))

            def regather(u, b, i):
                pool.wait_ge(r_mm.sem, u * SLOTS + (r_mm.pre - SLOTS))
                gate()
                pool.tensor_copy(iidx[:, b, :], src_sb[:, ds(u * SLOTS, SLOTS)]).then_inc(r_idx.sem, 1)
                pool.wait_ge(r_idx.sem, r_idx.done(u))
                gate()
                for j in range(SLOTS):
                    pool.indirect_dma_start(out=rows[:, b, j, :], out_offset=None, in_=table,
                                            in_offset=bass.IndirectOffsetOnAxis(ap=iidx[:, b, j:j + 1], axis=0)
                                            ).then_inc(redo_in[b], 16)
            pool.wait_ge(span_int, 1)
            with if_spread(pool):
                pool.wait_ge(g_mm.sem, g_mm.done(SETS - 1))
                pipeline(pool, SETS, 2, (regather, 0))

            def c_residual(t, b, i):
                pool.wait_ge(c_q.sem, c_q.done(t))
                gate()
                pool.tensor_tensor(at(mixo, t), c_out[:, b, :], at(mixo, t), ALU.add).then_inc(c_x1.sem, 1)
            pool.wait_ge(q_mo.sem, q_mo.done(T - 1))
            pipeline(pool, T, 2, (c_residual, 0))

            pool.wait_ge(d_hout.sem, d_hout.done(T - 1))
            pool.wait_ge(x1_out, 16 * T)
            pool.wait_ge(routed, 1)

            def fetch(s, b, i):
                pool.wait_ge(e_o.sem, e_o.ago(s, 4))
                pool.wait_ge(e_scd.sem, e_scd.ago(s, 8))
                gate()
                pool.tensor_copy(ix[:, b:b + 1], order_i[:, ds(s, 1)]).then_inc(e_ix.sem, 1)
                pool.wait_ge(e_ix.sem, e_ix.done(s))
                gate()
                pool.indirect_dma_start(out=hsb[b % 4][:, :], out_offset=None, in_=hidden,
                                        in_offset=bass.IndirectOffsetOnAxis(ap=ix[:, b:b + 1], axis=0),
                                        bounds_check=N - 1, oob_is_err=False).then_inc(hs_in[b % 4], 16)

            def put(s, b, i):
                pool.wait_ge(e_o.sem, e_o.done(s))
                gate()
                pool.indirect_dma_start(out=out, out_offset=bass.IndirectOffsetOnAxis(ap=ix[:, b:b + 1], axis=0),
                                        in_=so[:, b % 2, :], in_offset=None, bounds_check=N - 1,
                                        oob_is_err=False).then_inc(out_done[b % 4], 16)
            pipeline(pool, ST, 8, (fetch, 3), (put, 0))

        @block.scalar
        def _(act):
            def gate():
                act.sem_inc(waited["act"], 1)

            act.wait_ge(stats_v, 1)
            act.activation(rstd[:, :], var[:, :], ACT.Sqrt).then_inc(stats_s, 1)

            def keep(t, b, i):
                act.wait_ge(a_tr.sem, a_tr.done(t))
                act.wait_ge(a_mm.sem, a_mm.ago(t, 2))
                act.wait_ge(a_xnT.sem, a_xnT.ago(t, 2))
                act.activation(xs[:, b, :, :], over(B[2 + b][:, :], 128, 0, [[P, 2], [1, P]]), ACT.Copy).then_inc(a_xs.sem, 1)

            def raw(t, b, i):
                act.wait_ge(a_mm.sem, a_mm.done(t))
                gate()
                act.activation(at(raw_all, t), B[4 + b][0:P, 0:XW], ACT.Copy).then_inc(a_raw.sem, 1)
            skewed(act, keep, raw)

            act.wait_ge(a_shifted, 1)
            act.activation(raw_all[:, :, C:XW], raw_all[:, :, C:XW], ACT.Exp).then_inc(weights_exp, 1)

            def part_hi(t, b, i):
                act.wait_ge(a_y.sem, a_y.done(t))
                gate()
                act.activation(at(tb_all, t, 0, C), yw[:, b, :], ACT.Copy).then_inc(a_hi.sem, 1)

            def part_mid(t, b, i):
                act.wait_ge(a_r1.sem, a_r1.done(t))
                gate()
                act.activation(at(tb_all, t, C, 2 * C), y1[:, b, :], ACT.Copy).then_inc(a_mid.sem, 1)
            pipeline(act, T, 4, (part_hi, 1), (part_mid, 0))

            def k_stage(t, b, i):
                act.wait_ge(k_mm.sem, k_mm.ago(t, 2))
                gate()
                act.activation(kxs[:, b, :, :], xnT_all[:, :, ds(t * P, P)], ACT.Copy).then_inc(k_xs.sem, 1)

            def k_norm(t, b, i):
                act.wait_ge(k_qkv.sem, k_qkv.done(t))
                act.wait_ge(k_ss.sem, k_ss.ago(t, 1))
                act.activation(sq[:, :], qkv[:, b, 0:2 * C], ACT.Square).then_inc(k_sq.sem, 1)
                act.wait_ge(k_mx.sem, k_mx.done(t))
                act.wait_ge(k_rc.sem, k_rc.ago(t, 1))
                act.activation(nrm[:, :], ss2[:, :], ACT.Sqrt).then_inc(k_nrm.sem, 1)

            def k_keep(t, b, i):
                act.wait_ge(k_kn.sem, k_kn.done(t))
                act.wait_ge(k_acc.sem, k_acc.ago(t, 2))
                act.activation(kkx[b][:, :, KW:KW + D], kd[:, :, 0:D], ACT.Copy)
                act.activation(over(kc[:, b, :], P, 0, [[D, H], [1, D]]), kd[:, :, 0:D], ACT.Copy).then_inc(k_kc.sem, 1)
            def k_onehot(u, b, i):
                act.wait_ge(g_mm.sem, g_mm.ago(u, 2))
                act.wait_ge(g_oh.sem, g_oh.ago(u, 1))
                gate()
                act.activation(doff[:, :], dloc_set[:, ds(u * SLOTS, SLOTS)], ACT.Copy).then_inc(g_do.sem, 1)
                act.wait_ge(g_do.sem, g_do.done(u))
                for j in range(SLOTS):
                    ins = act.activation(onehot[:, b, j, 0:WIN], iota_bf[:, 0:WIN], ACT.Abs, bias=doff[:, j:j + 1], scale=-1.0)
                ins.then_inc(g_dist.sem, 1)
                act.wait_ge(g_dist.sem, g_dist.done(u))
                act.activation(onehot[:, b, :, 0:WIN], onehot[:, b, :, 0:WIN], ACT.Relu, bias=1.0, scale=-1.0).then_inc(g_oh.sem, 1)
            act.wait_ge(spans, 1)
            act.wait_ge(consts, 1)
            act.wait_ge(a_lo.sem, a_lo.done(T - 1))
            act.wait_ge(xb_out, 80)
            act.wait_ge(a_xnT.sem, a_xnT.done(T - 1))

            def clear_sums(t, b, i):
                if isinstance(t, int) and t == 0:
                    act.wait_ge(tab_out, 16 * T)
                    act.activation(wsum[:, :], over(iota_bf[:, :], 128, 0, [[0, NACC]]), ACT.Copy, scale=0.0).then_inc(acc_clear, 1)
            pipeline(act, T, 2, (k_stage, 3), (k_norm, 1), (clear_sums, 1), (k_keep, 1), (k_onehot, 2))

            act.wait_ge(matrices, 1)

            def q_copy(t, b, i):
                act.wait_ge(q_t.sem, q_t.ago(t, 1))
                act.wait_ge(q_qq.sem, q_qq.ago(t * 2, 1))
                gate()
                act.activation(qd[:, :, 0:D], over(at(q_all, t), P, 0, [[D, H], [1, D]]), ACT.Copy)
                act.activation(qd[:, :, D:48], over(at(q_all, t), P, 0, [[D, H], [1, 16]]), ACT.Copy)
                act.activation(qs[:, :], at(q_all, t), ACT.Copy).then_inc(q_qd.sem, 1)

            def q_turned(t, b, i):
                act.wait_ge(q_t.sem, q_t.done(t))
                act.wait_ge(q_p.sem, q_p.ago(t * 2, 3))
                act.wait_ge(q_tq.sem, q_tq.ago(t, 2))
                act.activation(qT[:, b, :, :], over(B[7][:, :], 128, 0, [[P, 2], [1, P]]), ACT.Copy).then_inc(q_qT.sem, 1)
                act.activation(F0[:, b, :, :], over(B[7][:, :], 128, 0, [[P, 2], [1, P]]), ACT.Square).then_inc(q_f0.sem, 1)

            def q_pairs(h):
                def evacuate(t, b, i):
                    act.wait_ge(q_s.sem, q_s.done(t * 8 + h))
                    act.wait_ge(q_p.sem, q_p.ago(t * 2 + h // 4, 2))
                    act.activation(F[h // 4][:, h % 4, :, :], over(B[2 + h % 2][:, :], 128, 0, [[P, 4], [1, P]]),
                                   ACT.Copy).then_inc(q_f.sem, 1)
                return evacuate
            pipeline(act, T, 2, (q_turned, 1), (q_pairs(0), 1), (q_pairs(1), 1), (q_copy, 2),
                     *[(q_pairs(h), 1) for h in range(2, H)])

            act.wait_ge(g_final, 1)
            act.wait_ge(q_mo.sem, q_mo.done(T - 1))

            def c_stage(t, b, i):
                act.wait_ge(c_mm.sem, c_mm.ago(t, 2))
                gate()
                act.activation(c_w[:, b, :], wsum[:, ds(t * P, P)], ACT.Copy)
                act.activation(c_acc[:, b, :, :], acc[:, :, ds(t * P, P)], ACT.Copy).then_inc(c_in1.sem, 1)
            pipeline(act, T, 2, (c_stage, 0))

            act.wait_ge(stats_v, 2)
            act.activation(rstd[:, :], var[:, :], ACT.Sqrt).then_inc(stats_s, 1)

            def d_keep(t, b, i):
                act.wait_ge(d_tr.sem, d_tr.done(t))
                act.wait_ge(d_mm.sem, d_mm.ago(t * 2, 3))
                act.activation(dxs[:, b, :, :], over(B[2][:, :], 128, 0, [[P, 2], [1, P]]), ACT.Copy).then_inc(d_xs.sem, 1)

            def d_gelu(t, b, i):
                act.wait_ge(d_hout.sem, d_hout.ago(t, 2))
                act.wait_ge(d_ht.sem, d_ht.ago(t * 2, 3))
                for hf in range(2):
                    act.wait_ge(d_hb.sem, d_hb.done(t * 2 + hf))
                    act.activation(hb[b][:, 512 * hf:512 * hf + 512], hp[:, b, 512 * hf:512 * hf + 512],
                                   ACT.Gelu).then_inc(d_ge.sem, 1)

            def d_evac(t, b, i):
                act.wait_ge(d_ht.sem, d_ht.done(t * 2 + 1))
                act.wait_ge(d_lm.sem, d_lm.ago(t, 1))
                act.activation(hT[:, 4:8, :], over(B[6][:, :], 128, 0, [[P, 4], [1, P]]), ACT.Copy).then_inc(d_e1.sem, 1)

            def d_partial(t, b, i):
                act.wait_ge(d_lm.sem, d_lm.done(t))
                act.wait_ge(d_ls.sem, d_ls.ago(t, 1))
                act.activation(gl[:, :], B[7][:, 0:P], ACT.Copy).then_inc(d_gl.sem, 1)
            pipeline(act, T, 2, (d_partial, 0), (d_keep, 4), (d_gelu, 3), (d_evac, 2))

            act.wait_ge(r_shifted, 1)
            act.activation(ex[:, :, :], r_a[:, :, :], ACT.Exp).then_inc(logits_exp, 1)

            def e_evac(s, b, i):
                act.wait_ge(e_tr.sem, e_tr.done(s * 2 + 1))
                act.wait_ge(e_mm.sem, e_mm.ago(s, 2))
                act.activation(hsT[:, b, 1, :], B[5 + 2 * b][:, :], ACT.Copy).then_inc(e_e1.sem, 1)
            pipeline(act, ST, 2, (e_evac, 0))

        @block.vector
        def _(dve):
            n = [0]

            def link(ins):
                n[0] += 1
                ins.then_inc(dve_chain, 1)
                dve.wait_ge(dve_chain, n[0])

            def gate():
                dve.sem_inc(waited["dve"], 1)

            def layer_norm_stats(k):
                def col(c):
                    return st_all[:, :, c:c + 1].rearrange("p t o -> p (t o)")
                link(dve.memset(delta[:, :], 0.0))
                link(dve.tensor_tensor(mean[:, :], col(1), col(4), ALU.add))
                link(dve.tensor_tensor(delta[:, :], col(1), col(4), ALU.subtract))
                link(dve.tensor_tensor(var[:, :], col(2), col(5), ALU.add))
                link(dve.scalar_tensor_tensor(nmr[:, :], delta[:, :], 0.25, delta[:, :], ALU.mult, ALU.mult))
                link(dve.scalar_tensor_tensor(var[:, :], var[:, :], 1.0 / C, nmr[:, :], ALU.mult, ALU.add))
                dve.tensor_scalar(var[:, :], var[:, :], LN_EPS, None, ALU.add).then_inc(stats_v, 1)
                dve.wait_ge(stats_s, k)
                link(dve.reciprocal(delta[:, :], rstd[:, :]))
                link(dve.tensor_copy(rstd[:, :], delta[:, :]))
                link(dve.scalar_tensor_tensor(nmr[:, :], mean[:, :], -0.5, rstd[:, :], ALU.mult, ALU.mult))

            def row_stats(c):
                dve.wait_ge(x_in[c], 16)
                for t in range(5 * c, 5 * c + 5):
                    dve.bn_stats(st_all[:, t, :], x_all[:, t, :])
            for c in range(3):
                row_stats(c)
            dve.wait_ge(w_in, 32)
            link(dve.tensor_tensor(wa_prod[:, :, :], W_sb[:, :, 0:C], over(asrc_bc[:, :], 128, 0, [[0, 2], [1, C]]), ALU.mult))
            for k in range(2):
                link(dve.tensor_reduce(W_sb[:, k, C:XW], over(wa_prod[:, :, :], 128, k * C, [[D, H], [1, D]]), AX.X, ALU.add))
            for c in range(3, 5):
                row_stats(c)
            link(dve.memset(normeps[:, H:], 1e-24))
            layer_norm_stats(1)
            dve.memset(normeps[:, 0:H], (1e-12 / SCALE) ** 2).then_inc(head_cols, 1)

            def normalise(t, b, i):
                dve.wait_ge(a_tr.sem, a_tr.ago(t, 2))
                dve.tensor_scalar(xn[:, b, :], at(x_all, t), rstd[:, ds(t, 1)], nmr[:, ds(t, 1)],
                                  ALU.mult, ALU.add).then_inc(a_xn.sem, 1)
            pairs(dve, normalise)

            dve.wait_ge(e_in, 64)
            link(dve.tensor_tensor(dloc_tile[:, :], waste[:, :], baseb[:, :], ALU.subtract))
            link(dve.tensor_tensor(dloc_set[:, :], waste[:, :], over(baseb[:, :], 128, 0, [[SLOTS, SETS], [0, SLOTS]]),
                                   ALU.subtract))
            dve.tensor_reduce(span[:, :], dloc_set[:, :], AX.X, ALU.max).then_inc(spans, 1)
            dve.wait_ge(a_raw.sem, a_raw.done(T - 1))
            dve.tensor_reduce(hmax[:, :], raw_all[:, :, C:XW].rearrange("p t h -> p h t"), AX.X, ALU.max).then_inc(hmax_tile, 1)
            dve.wait_ge(hmax_all, 1)
            dve.tensor_tensor(raw_all[:, :, C:XW], raw_all[:, :, C:XW], over(hmaxall[:, :], P, 0, [[0, T], [1, H]]),
                              ALU.subtract).then_inc(a_shifted, 1)
            dve.wait_ge(weights_exp, 1)
            w0, wp = raw_all[:, :, C:XW], [tb_all[:, :, 3 * C + H * k:3 * C + H * k + H] for k in range(3)]
            link(dve.tensor_copy(wp[0], w0))
            link(dve.tensor_tensor(w1[:, :, :], w0, wp[0], ALU.subtract))
            link(dve.tensor_copy(wp[1], w1[:, :, :]))
            link(dve.tensor_tensor(wp[2], w1[:, :, :], wp[1], ALU.subtract))

            def weigh(t, b, i):
                dve.wait_ge(a_hi.sem, a_hi.ago(t, 4))
                dve.wait_ge(a_r1.sem, a_r1.ago(t, 4))
                dve.tensor_tensor(over(yw[:, b, :], P, 0, [[D, H], [1, D]]),
                                  over(at(raw_all, t), P, 0, [[D, H], [1, D]]),
                                  over(at(raw_all, t), P, C, [[1, H], [0, D]]), ALU.mult).then_inc(a_y.sem, 1)

            def rest(t, b, i):
                dve.wait_ge(a_hi.sem, a_hi.done(t))
                dve.wait_ge(a_lo.sem, a_lo.ago(t, 4))
                dve.tensor_tensor(y1[:, b, :], yw[:, b, :], at(tb_all, t, 0, C), ALU.subtract).then_inc(a_r1.sem, 1)

            def low(t, b, i):
                dve.wait_ge(a_mid.sem, a_mid.done(t))
                dve.tensor_tensor(at(tb_all, t, 2 * C, 3 * C), y1[:, b, :], at(tb_all, t, C, 2 * C),
                                  ALU.subtract).then_inc(a_lo.sem, 1)
            pipeline(dve, T, 4, (weigh, 3), (rest, 2), (low, 0))

            dve.wait_ge(consts, 1)
            dve.tensor_reduce(partsum[:, :], over(ident[:, :], 128, 8, [[1, NE], [32, 4], [8, 3]]), AX.XY, ALU.add)
            dve.tensor_reduce(gatesum[:, :], over(ident[:, :], 128, 0, [[1, NE], [32, 4]]), AX.X, ALU.add)

            def g_onehot(u, b, i):
                dve.wait_ge(g_mm.sem, g_mm.ago(u, 2))
                dve.tensor_tensor(onehot[:, b, :, 0:WIN], over(iota_bf[:, :], 128, 0, [[0, SLOTS], [1, WIN]]),
                                  over(dloc_set[:, ds(u * SLOTS, SLOTS)], 128, 0, [[1, SLOTS], [0, WIN]]),
                                  ALU.is_equal).then_inc(g_oh.sem, 1)

            def g_add(u, b, i):
                first = dve.value_load(base_row[0:1, ds(u * SLOTS, 1)], min_val=0, max_val=N - 1)
                dve.wait_ge(g_mm.sem, g_mm.done(u))
                dve.wait_ge(g_acc.sem, g_acc.ago(u, 1))
                dve.tensor_tensor(acc[:, :, ds(first, WIN)], acc[:, :, ds(first, WIN)],
                                  over(psG[b][:, :], 128, 0, [[EP, 2], [1, WIN]]), ALU.add)
                dve.tensor_tensor(wsum[:, ds(first, WIN)], wsum[:, ds(first, WIN)], psG[b][:, 2 * EP:2 * EP + WIN],
                                  ALU.add).then_inc(g_acc.sem, 1)

            dve.wait_ge(span_max, 1)
            dve.tensor_copy(span_i[:, :], span_all[:, :]).then_inc(span_int, 1)
            dve.wait_ge(c_in, 96)
            dve.wait_ge(xb_out, 80)
            link(dve.tensor_scalar(normfac[:, 0:H], temp_bc[:, :], SCALE, None, ALU.mult))
            link(dve.memset(normfac[:, H:], SCALE))
            dve.wait_ge(a_lo.sem, a_lo.done(T - 1))
            for b in range(2):
                link(dve.memset(kkx[b][:, :, KW + D:KROW], 1.0))
            dve.sem_inc(kkx_ones, 1)

            def clear_sums(t, b, i):
                if isinstance(t, int) and t == 0:
                    dve.wait_ge(tab_out, 16 * T)
                    dve.memset(acc[:, :, :], 0.0).then_inc(acc_clear, 1)
                    dve.wait_ge(acc_clear, 2)

            def k_bias(t, b, i):
                dve.wait_ge(k_mm.sem, k_mm.done(t))
                dve.wait_ge(k_acc.sem, k_acc.ago(t, 2))
                dve.tensor_tensor(qkv[:, b, 0:512], B[2][0:P, :], bqkv_bc[:, 0:512], ALU.add)
                dve.tensor_tensor(qkv[:, b, 512:768], B[3][0:P, 0:C], bqkv_bc[:, 512:768], ALU.add).then_inc(k_qkv.sem, 1)

            def k_sums(t, b, i):
                dve.wait_ge(k_sq.sem, k_sq.done(t))
                dve.wait_ge(k_mx.sem, k_mx.ago(t, 1))
                dve.tensor_reduce(ss[:, :], sq[:, :].rearrange("p (a d) -> p a d", d=D), AX.X, ALU.add).then_inc(k_ss.sem, 1)
                dve.wait_ge(k_ss.sem, k_ss.done(t))
                dve.wait_ge(k_nrm.sem, k_nrm.ago(t, 1))
                dve.tensor_tensor(ss2[:, :], ss[:, :], normeps[:, :], ALU.max).then_inc(k_mx.sem, 1)

            def k_features(t, b, i):
                dve.wait_ge(k_nrm.sem, k_nrm.done(t))
                dve.reciprocal(rcp[:, :], nrm[:, :]).then_inc(k_rc.sem, 1)
                dve.wait_ge(k_rc.sem, k_rc.done(t))
                dve.tensor_tensor(rn[:, :], rcp[:, :], normfac[:, :], ALU.mult).then_inc(k_rn.sem, 1)
                dve.wait_ge(k_rn.sem, k_rn.done(t))
                dve.wait_ge(k_kkv.sem, k_kkv.ago(t, 1))
                dve.wait_ge(k_kc.sem, k_kc.ago(t, 1))
                k_rnb = over(rn[:, :], P, H, [[1, H], [0, D]])
                dve.tensor_tensor(kd[:, :, 0:D], over(qkv[:, b, :], P, C, [[D, H], [1, D]]), k_rnb, ALU.mult)
                dve.tensor_tensor(kd[:, :, D:48], over(qkv[:, b, :], P, C, [[D, H], [1, 16]]),
                                  over(rn[:, :], P, H, [[1, H], [0, 16]]), ALU.mult)
                dve.tensor_tensor(over(at(q_all, t), P, 0, [[D, H], [1, D]]),
                                  over(qkv[:, b, :], P, 0, [[D, H], [1, D]]), over(rn[:, :], P, 0, [[1, H], [0, D]]),
                                  ALU.mult).then_inc(k_kn.sem, 1)
                dve.wait_ge(k_kn.sem, k_kn.done(t))
                dve.wait_ge(k_acc.sem, k_acc.ago(t, 2))
                dve.tensor_tensor(over(kkx[b][:, :, :], P, 0, [[KROW, H], [D, FD], [1, D]]),
                                  over(kd[:, :, :], P, 0, [[48, H], [0, FD], [1, D]]),
                                  over(kd[:, :, :], P, 0, [[48, H], [1, FD], [1, D]]), ALU.mult).then_inc(k_kkv.sem, 1)
            pipeline(dve, T, 2, (k_bias, 1), (g_add, 0), (k_sums, 1), (k_features, 1), (clear_sums, 1))

            dve.wait_ge(k_kc.sem, k_kc.done(T - 1))
            for u in BETWEEN:
                g_onehot(u, u % 2, u // 2)
            for g in range(2):
                dve.wait_ge(k_acc.sem, k_acc.done(T - 1))
                accA, accC = B[4 + g], B[6]
                for dd, nd, f in ((0, 1, 0.5 / N), (1, 15, 1.0 / N), (16, 1, 0.5 / N)):
                    srcA = over(accA[:, :], 128, dd * D, [[D, nd], [1, D]]) if dd < 16 else over(accC[:, :], 128, 66 * g, [[D, 1], [1, D]])
                    ins = dve.tensor_scalar(KV[:, g, dd:dd + nd, :], srcA, f, None, ALU.mult)
                ins.then_inc(kx_ready, 1)
                dve.tensor_scalar(KL[:, g, 0, :], accC[:, 66 * g + D:66 * g + 2 * D], SCALE ** 2 / N, None, ALU.mult)
                dve.tensor_scalar(vsum[:, g:g + 1], accC[:, 66 * g + 2 * D:66 * g + 2 * D + 1], SCALE ** 4 / N, None, ALU.mult)
                dve.tensor_scalar(ksum[:, g:g + 1], accC[:, 132 + 129 * g + 128:132 + 129 * g + 129], SCALE ** 2 / N, None, ALU.mult)
                link(dve.scalar_tensor_tensor(Mgram[:, g, :], accC[:, 132 + 129 * g:132 + 129 * g + 128], 0.5 / N,
                                              headmask[:, :], ALU.mult, ALU.mult))
                dve.transpose(KL[:, g, 2, :], KV[:, g, 0, :])
                link(dve.transpose(KL[:, g, 1, :], KL[:, g, 0, :]))
                for M, k in ((Mdiag, 2), (Mlin, 1)):
                    dve.tensor_tensor(over(M[:, g, :], 128, 0, [[D, 4], [1, D]]), over(KL[:, g, k, :], 128, 0, [[0, 4], [1, D]]),
                                      over(headmask[:, :], 128, 0, [[D, 4], [1, D]]), ALU.mult)
            for g in range(2):
                dve.wait_ge(kx_turned, g + 1)
                link(dve.tensor_copy(Mpair[:, g, :, :], over(B[2 + g][:, :], 128, 0, [[128, 4], [1, 128]])))
            dve.sem_inc(matrices, 1)

            def q_weigh(t, b, i):
                dve.wait_ge(q_T.sem, q_T.done(t))
                dve.wait_ge(q_nr.sem, q_nr.ago(t, 1))
                for g in range(2):
                    ins = dve.scalar_tensor_tensor(TQ[:, g, :], B[4][:, g * P:(g + 1) * P], ksum[:, g:g + 1],
                                                   qT[:, b, g, :], ALU.add, ALU.mult)
                ins.then_inc(q_tq.sem, 1)

            def q_features(hf):
                def multiply(t, b, i):
                    dve.wait_ge(q_qd.sem, q_qd.done(t))
                    dve.wait_ge(q_s.sem, q_s.ago(t * 8 + 4 * hf, 5))
                    dve.tensor_tensor(over(qq[:, :, :], P, 4 * hf * 16 * D, [[16 * D, 4], [D, 16], [1, D]]),
                                      over(qd[:, :, :], P, 4 * hf * 48, [[48, 4], [0, 16], [1, D]]),
                                      over(qd[:, :, :], P, 4 * hf * 48 + 1, [[48, 4], [1, 16], [1, D]]), ALU.mult).then_inc(q_qq.sem, 1)
                return multiply

            def q_divide(t, b, i):
                dve.wait_ge(q_nr.sem, q_nr.done(t))
                dve.wait_ge(q_rn.sem, q_rn.ago(t, 1))
                dve.tensor_scalar(nn[:, :, :], over(B[4][:, :], 128, 2 * P, [[P, 2], [1, P]]), SCALE ** 4, None,
                                  ALU.add).then_inc(q_nn.sem, 1)
                dve.wait_ge(q_nn.sem, q_nn.done(t))
                dve.wait_ge(q_yev.sem, q_yev.ago(t, 1))
                dve.reciprocal(rnn[:, :, :], nn[:, :, :]).then_inc(q_rn.sem, 1)

            def q_numerators(t, b, i):
                dve.wait_ge(q_rn.sem, q_rn.done(t))
                dve.wait_ge(q_p.sem, q_p.done(t * 2 + 1))
                dve.wait_ge(q_pm.sem, q_pm.ago(t, 1))
                for g in range(2):
                    ins = dve.scalar_tensor_tensor(yT[:, g, :], psN[b][:, g * P:(g + 1) * P], vsum[:, g:g + 1],
                                                   rnn[:, g, :], ALU.add, ALU.mult)
                ins.then_inc(q_yev.sem, 1)

            def q_residual(t, b, i):
                dve.wait_ge(q_pm.sem, q_pm.done(t))
                dve.tensor_tensor(at(mixo, t), B[7][0:P, 0:C], at(mixo, t), ALU.add).then_inc(q_mo.sem, 1)
            for u in BETWEEN:
                g_add(u, u % 2, u // 2)
            dve.wait_ge(xb_in, 80)
            pipeline(dve, T, 2, (q_weigh, 1), (beside_q(g_add), 0), (q_features(0), 2), (q_divide, 1), (q_residual, 0),
                     (beside_q(g_onehot), 2), (q_numerators, 1), (q_features(1), 2))

            def redo_onehot(m, j, i):
                dve.wait_ge(r_mm.sem, r_mm.ago(m, 4))
                dve.tensor_scalar(onehot[:, 0, j, :], iota_bf[:, :], dloc_tile[:, ds(m, 1)], None, ALU.is_equal).then_inc(r_oh.sem, 1)

            def redo_add(m, j, i):
                first = dve.value_load(base_row[0:1, ds(m, 1)], min_val=0, max_val=N - 1)
                dve.wait_ge(r_mm.sem, r_mm.done(m))
                dve.wait_ge(r_acc.sem, r_acc.ago(m, 1))
                dve.tensor_tensor(acc[:, :, ds(first, EP)], acc[:, :, ds(first, EP)],
                                  over(psG[j % 2][:, :], 128, 0, [[EP, 2], [1, EP]]), ALU.add)
                dve.tensor_tensor(wsum[0:32, ds(first, EP)], wsum[0:32, ds(first, EP)], psG[j % 2][0:32, 2 * EP:3 * EP],
                                  ALU.add).then_inc(r_acc.sem, 1)
            dve.wait_ge(g_acc.sem, g_acc.done(SETS - 1))
            with if_spread(dve):
                dve.memset(acc[:, :, :], 0.0)
                dve.memset(wsum[:, :], 0.0).then_inc(sums_cleared, 1)
                dve.wait_ge(sums_cleared, 1)
                pipeline(dve, ET, 4, (redo_onehot, 2), (redo_add, 0))
                dve.wait_ge(r_acc.sem, r_acc.done(ET - 1))
            dve.sem_inc(g_final, 1)

            def c_guard(t, b, i):
                dve.wait_ge(c_mm.sem, c_mm.done(t))
                dve.tensor_scalar(c_den[:, b, :], B[2 + b][0:P, C:C + H], 1e-16, None, ALU.add).then_inc(c_dn.sem, 1)

            def c_invert(t, b, i):
                dve.wait_ge(c_dn.sem, c_dn.done(t))
                dve.reciprocal(c_rcp[:, b, :], c_den[:, b, :]).then_inc(c_rc.sem, 1)

            def c_quotient(t, b, i):
                dve.wait_ge(c_rc.sem, c_rc.done(t))
                dve.wait_ge(c_x1.sem, c_x1.ago(t, 2))
                dve.tensor_tensor(over(c_out[:, b % 2, :], P, 0, [[D, H], [1, D]]), over(B[2 + b][:, :], P, 0, [[D, H], [1, D]]),
                                  over(c_rcp[:, b, :], P, 0, [[1, H], [0, D]]), ALU.mult).then_inc(c_q.sem, 1)

            def c_stats(t, b, i):
                dve.wait_ge(c_x1.sem, c_x1.done(t))
                gate()
                dve.bn_stats(at(st_all, t), at(mixo, t))
            dve.wait_ge(q_mo.sem, q_mo.done(T - 1))
            pipeline(dve, T, 4, (c_guard, 3), (c_quotient, 2), (c_invert, 3), (c_stats, 0))
            layer_norm_stats(2)

            dve.wait_ge(late_in, 64)
            dve.wait_ge(c_in1.sem, c_in1.done(T - 1))

            def d_norm(t, b, i):
                dve.wait_ge(d_tr.sem, d_tr.ago(t, 2))
                dve.tensor_scalar(dxn[:, b, :], at(mixo, t), rstd[:, ds(t, 1)], nmr[:, ds(t, 1)],
                                  ALU.mult, ALU.add).then_inc(d_xn.sem, 1)

            def d_bias(hf):
                def add(t, b, i):
                    dve.wait_ge(d_mm.sem, d_mm.done(t * 2 + hf))
                    dve.wait_ge(d_ge.sem, d_ge.ago(t * 2 + hf, 4))
                    dve.tensor_tensor(hp[:, b, 512 * hf:512 * hf + 512], B[psH[b] + hf][0:P, :],
                                      b1_bc[:, 512 * hf:512 * hf + 512], ALU.add).then_inc(d_hb.sem, 1)
                return add

            def d_evac(t, b, i):
                dve.wait_ge(d_ht.sem, d_ht.done(t * 2))
                dve.wait_ge(d_lm.sem, d_lm.ago(t, 1))
                dve.tensor_copy(hT[:, 0:4, :], over(B[5][:, :], 128, 0, [[P, 4], [1, P]])).then_inc(d_e0.sem, 1)

            def d_logits(t, b, i):
                dve.wait_ge(d_ls.sem, d_ls.done(t))
                dve.tensor_tensor(at(lg_all, t), B[7][0:P, P:P + NE], bg_bc[:, :], ALU.add).then_inc(d_lg.sem, 1)
            pipeline(dve, T, 2, (d_norm, 5), (d_bias(0), 3), (d_logits, 0), (d_bias(1), 3), (d_evac, 2))

            dve.wait_ge(d_lg.sem, d_lg.done(T - 1))
            link(dve.tensor_reduce(r_e[:, :], lg_all[:, :, :], AX.X, ALU.max))
            link(dve.tensor_tensor(r_a[:, :, :], lg_all[:, :, :], over(r_e[:, :], P, 0, [[1, T], [0, NE]]), ALU.subtract))
            dve.sem_inc(r_shifted, 1)
            dve.wait_ge(logits_exp, 1)
            link(dve.tensor_reduce(r_e[:, :], ex[:, :, :], AX.X, ALU.add))
            link(dve.reciprocal(prob[:, :], r_e[:, :]))
            link(dve.tensor_scalar(r_a[:, :, :], ex[:, :, :], 1.0, -8.0, ALU.is_ge, ALU.mult))
            link(dve.tensor_tensor(r_b[:, :, :], r_a[:, :, :], over(iota8[:, :], P, 0, [[0, T], [1, NE]]), ALU.add))
            link(dve.tensor_reduce(r_e[:, :], r_b[:, :, :], AX.X, ALU.min))
            link(dve.tensor_tensor(r_a[:, :, :], r_b[:, :, :], over(r_e[:, :], P, 0, [[1, T], [0, NE]]), ALU.is_equal))
            dve.sem_inc(r_chosen, 1)
            dve.wait_ge(r_counts, 1)
            link(dve.tensor_copy(r_c[:, :, :], over(B[3][:, :], P, 0, [[1, NE], [NE, T]])))
            for e in range(NE):
                link(dve.tensor_tensor_scan(r_d[:, e, :], rones[:, 0:T], r_c[:, e, :], 0.0, ALU.mult, ALU.add))
            link(dve.tensor_scalar(r_g[:, :], over(r_d[:, :, :], P, T - 1, [[T, NE]]), 127.0, None, ALU.add))
            link(dve.tensor_scalar(r_g[:, :], r_g[:, :], 7, 7, ALU.arith_shift_right, ALU.arith_shift_left))
            link(dve.tensor_copy(r_f[:, :], r_g[:, :]))
            link(dve.tensor_tensor_scan(r_h[:, :], rones[:, 0:NE], r_f[:, :], 0.0, ALU.mult, ALU.add))
            link(dve.tensor_tensor(r_f[:, :], r_h[:, :], r_f[:, :], ALU.subtract))
            link(dve.tensor_tensor(r_c[:, :, :], r_d[:, :, :], r_c[:, :, :], ALU.subtract))
            link(dve.tensor_tensor(r_b[:, :, :], over(B[2][:, :], P, 0, [[NE, T], [1, NE]]),
                                   over(r_c[:, :, :], P, 0, [[1, T], [T, NE]]), ALU.add))
            link(dve.tensor_tensor(r_b[:, :, :], r_b[:, :, :], over(r_f[:, :], P, 0, [[0, T], [1, NE]]), ALU.add))
            link(dve.tensor_tensor(r_b[:, :, :], r_b[:, :, :], r_a[:, :, :], ALU.mult))
            link(dve.tensor_reduce(r_e[:, :], r_b[:, :, :], AX.X, ALU.add))
            link(dve.tensor_copy(slot_i[:, :], r_e[:, :]))
            link(dve.tensor_scalar(slot_i[:, :], slot_i[:, :], 7, None, ALU.arith_shift_right))
            link(dve.tensor_copy(slot_hi[:, :], slot_i[:, :]))
            link(dve.scalar_tensor_tensor(slot_lo[:, :], slot_hi[:, :], -128.0, r_e[:, :], ALU.mult, ALU.add))
            dve.wait_ge(d_hout.sem, d_hout.done(T - 1))
            dve.tensor_tensor(is_hi[:, :, :], over(iota_bf[:, :], P, 0, [[0, T], [1, ST]]),
                              over(slot_hi[:, :], P, 0, [[1, T], [0, ST]]), ALU.is_equal)
            link(dve.tensor_tensor(is_lo[:, :, :], over(iota_bf[:, :], P, 0, [[0, T], [1, 128]]),
                                   over(slot_lo[:, :], P, 0, [[1, T], [0, 128]]), ALU.is_equal))
            for c, value in enumerate((node_f, prob)):
                ins = dve.tensor_tensor(spread[:, :, c, :], is_hi[:, :, :], over(value[:, :], P, 0, [[1, T], [0, ST]]), ALU.mult)
            ins.then_inc(r_spread, 1)
            link(dve.tensor_tensor(ev32[:, :, :], over(s128[:, :], 1, 0, [[1, ST], [0, NE]]),
                                   over(r_h[:, :], 1, 0, [[0, ST], [1, NE]]), ALU.is_ge))
            link(dve.tensor_reduce(rexp[:, :], ev32[:, :, :], AX.X, ALU.add))
            link(dve.tensor_scalar(rexp[:, :], rexp[:, :], float(NE - 1), float(C), ALU.min, ALU.mult))
            link(dve.tensor_copy(experts_i[:, :], rexp[:, :]))
            dve.wait_ge(r_ordered, 1)
            link(dve.tensor_scalar(order_f[:, :], B[4][:, 0:ST], float(NOBODY), None, ALU.add))
            link(dve.tensor_copy(order_i[:, :], order_f[:, :]))
            link(dve.tensor_copy(order_p[:, :], B[4][:, ST:2 * ST]))
            dve.sem_inc(routed, 1)


            def e_evac(s, b, i):
                dve.wait_ge(e_tr.sem, e_tr.done(s * 2))
                dve.wait_ge(e_mm.sem, e_mm.ago(s, 2))
                dve.tensor_copy(hsT[:, b % 2, 0, :], B[4 + 2 * (b % 2)][:, :]).then_inc(e_e0.sem, 1)

            def e_out(s, b, i):
                col = dve.value_load(experts_i[0:1, ds(s, 1)], min_val=0, max_val=(NE - 1) * C)
                dve.wait_ge(e_mm.sem, e_mm.done(s))
                dve.wait_ge(e_o.sem, e_o.ago(s, 1))
                dve.tensor_tensor(t1[:, :], B[2 + b % 2][:, 0:C], bd_bc[:, ds(col, C)], ALU.add).then_inc(e_t1.sem, 1)
                dve.wait_ge(e_scd.sem, e_scd.ago(s, 2))
                dve.wait_ge(e_t1.sem, e_t1.done(s))
                dve.scalar_tensor_tensor(so[:, b % 2, :], t1[:, :], order_p[:, ds(s, 1)], hsb[b][:, HID:HROW],
                                         ALU.mult, ALU.add).then_inc(e_o.sem, 1)
            pipeline(dve, ST, 4, (e_evac, 1), (e_out, 0))

        @block.tensor
        def _(pe):
            pe.wait_ge(pool_chain, 2)
            pe.wait_ge(head_cols, 1)

            def a_front(t, b, i):
                pe.wait_ge(a_xn.sem, a_xn.done(t))
                pe.wait_ge(a_xs.sem, a_xs.ago(t, 2))
                for k in range(2):
                    ins = pe.transpose(B[2 + b][:, k * P:(k + 1) * P], xn[:, b, 128 * k:128 * k + 128], ident[0:P, 0:P])
                ins.then_inc(a_tr.sem, 1)

            def a_back(t, b, i):
                pe.wait_ge(a_xs.sem, a_xs.done(t))
                pe.wait_ge(a_raw.sem, a_raw.ago(t, 2))
                for k in range(2):
                    ins = pe.matmul(B[4 + b][0:P, 0:XW], xs[:, b, k, :], W_sb[:, k, :], start=(k == 0), stop=(k == 1))
                ins.then_inc(a_mm.sem, 1)
            skewed(pe, a_front, a_back)

            def g_part(u, b, i, part):
                if part == 0:
                    pe.wait_ge(rows_in[b], i * (16 * SLOTS) + 16 * SLOTS)
                    pe.wait_ge(g_oh.sem, g_oh.done(u))
                    pe.wait_ge(g_acc.sem, g_acc.ago(u, 2))
                for j in range(2 * part, 2 * part + 2):
                    for c in range(2):
                        for low in range(3):
                            pe.matmul(psG[b][:, EP * c:EP * c + WIN], rows[:, b, j, low * C + 128 * c:low * C + 128 * c + 128],
                                      onehot[:, b, j, 0:WIN], start=(j == 0 and c == 0 and low == 0),
                                      stop=(j == SLOTS - 1 and low == 2), skip_group_check=True)
                for j in range(2 * part, 2 * part + 2):
                    q = j % 4
                    ins = pe.matmul(psG[b][32 * q:32 * q + 32, 2 * EP:2 * EP + WIN], rows[:, b, j, 3 * C - 8:ROW],
                                    onehot[:, b, j, 0:WIN], start=False, stop=(j >= 4), skip_group_check=True)
                if part == 3:
                    ins.then_inc(g_mm.sem, 1)

            def g_set(u, b, i):
                for part in range(4):
                    g_part(u, b, i, part)

            pe.wait_ge(consts, 1)
            pe.wait_ge(a_raw.sem, a_raw.done(T - 1))
            for bnk in (4, 5, 6):
                pe.matmul(B[bnk][:, :], Mdiag[:, 0, :], over(Mdiag[:, :, :], 128, 0, [[0, 4], [1, 128]]), start=True, stop=True)
            pe.wait_ge(c_in, 96)
            pe.wait_ge(kkx_ones, 1)

            def k_front(t, b, i):
                pe.wait_ge(k_xs.sem, k_xs.done(t))
                pe.wait_ge(k_qkv.sem, k_qkv.ago(t, 1))
                for k in range(2):
                    pe.matmul(B[2][0:P, :], kxs[:, b, k, :], WqkvT_sb[:, k, 0:512], start=(k == 0), stop=(k == 1))
                for k in range(2):
                    ins = pe.matmul(B[3][0:P, 0:C], kxs[:, b, k, :], WqkvT_sb[:, k, 512:768], start=(k == 0), stop=(k == 1))
                ins.then_inc(k_mm.sem, 1)

            def k_back(t, b, i):
                v = qkv[:, b, 2 * C:3 * C]
                pe.wait_ge(k_kkv.sem, k_kkv.done(t))
                pe.wait_ge(k_kc.sem, k_kc.done(t))
                for g in range(2):
                    for hq in range(4):
                        h = 4 * g + hq
                        pe.matmul(B[4 + g][D * hq:D * hq + D, :], v[:, D * h:D * h + D], kkx[b][:, h, 0:512],
                                  start=False, stop=False, skip_group_check=True)
                for g in range(2):
                    for hq in range(4):
                        h = 4 * g + hq
                        pe.matmul(B[6][D * hq:D * hq + D, 66 * g:66 * g + 65], v[:, D * h:D * h + D],
                                  kkx[b][:, h, 512:577], start=False, stop=False, skip_group_check=True)
                for g in range(2):
                    kn = kc[:, b, 128 * g:128 * g + 128]
                    pe.matmul(B[6][:, 132 + 129 * g:132 + 129 * g + 128], kn, kn, start=False, stop=False, skip_group_check=True)
                    ins = pe.matmul(B[6][:, 132 + 129 * g + 128:132 + 129 * g + 129], kn, kkx[b][:, 0, 576:577],
                                    start=False, stop=False, skip_group_check=True)
                ins.then_inc(k_acc.sem, 1)
            pipeline(pe, T, 2, (k_back, 0), (k_front, 2), (g_set, 1))

            for g in range(2):
                pe.wait_ge(kx_ready, 1 + g)
                for G in range(4):
                    ins = pe.transpose(B[2 + g][:, 128 * G:128 * G + 128], over(KV[:, g, :, :], 128, (4 * G + 1) * D, [[1, 128]]),
                                       ident[:, :])
                ins.then_inc(kx_turned, 1)
                u = BETWEEN[g]
                g_set(u, u % 2, u // 2)
            pe.wait_ge(matrices, 1)

            def q_turn(t, b, i):
                pe.wait_ge(q_qd.sem, q_qd.done(t))
                pe.wait_ge(q_mo.sem, q_mo.ago(t, 2))
                pe.wait_ge(q_f0.sem, q_f0.ago(t, 1))
                for g in range(2):
                    ins = pe.transpose(B[7][:, g * P:(g + 1) * P], qs[:, 128 * g:128 * g + 128], ident[0:P, 0:P])
                ins.then_inc(q_t.sem, 1)

            def q_products(t, b, g):
                pe.wait_ge(q_f.sem, q_f.done(t * 8 + 4 * g + 3))
                for G in range(4):
                    for hq in range(4):
                        ins = pe.matmul(psN[b][D * hq:D * hq + D, g * P:(g + 1) * P], Mpair[:, g, G, D * hq:D * hq + D],
                                        F[g][:, hq, G, :], start=False, stop=(G == 3), skip_group_check=True)
                ins.then_inc(q_p.sem, 1)

            BESIDE = (1, 3, 4, 6)

            def q_tile(t, b, i):
                ps = psN[b]

                def linear():
                    pe.wait_ge(q_f0.sem, q_f0.done(t))
                    pe.wait_ge(q_yev.sem, q_yev.ago(t, 2))
                    pe.wait_ge(q_nn.sem, q_nn.ago(t, 1))
                    for g in range(2):
                        ins = pe.matmul(B[4][:, g * P:(g + 1) * P], Mgram[:, g, :], qT[:, b, g, :], start=True, stop=True)
                    ins.then_inc(q_T.sem, 1)
                    for g in range(2):
                        pe.matmul(ps[:, g * P:(g + 1) * P], Mdiag[:, g, :], F0[:, b, g, :], start=(g == 0), stop=False, skip_group_check=True)
                    for g in range(2):
                        pe.matmul(ps[:, g * P:(g + 1) * P], Mlin[:, g, :], qT[:, b, g, :], start=False, stop=False, skip_group_check=True)

                for h in range(H):
                    if h % 4 == 0:
                        pe.wait_ge(q_qq.sem, q_qq.done(t * 2 + h // 4))
                    pe.wait_ge(q_f.sem, q_f.ago(t * 8 + h, 2))
                    for G in range(4):
                        ins = pe.transpose(B[2 + h % 2][:, G * P:(G + 1) * P], qq[:, h, 128 * G:128 * G + 128], ident[0:P, 0:P])
                    ins.then_inc(q_s.sem, 1)
                    if h in BESIDE:
                        beside_q(lambda u, p, k: g_part(u, p, k, BESIDE.index(h)))(t, b, i)
                    if h == 2:
                        linear()
                    if h == 5:
                        pe.wait_ge(q_tq.sem, q_tq.done(t))
                        pe.matmul(over(B[4][:, :], 128, 2 * P, [[1, 2 * P]]), blockones[:, :], over(TQ[:, :, :], 128, 0, [[1, 2 * P]]),
                                  start=True, stop=True).then_inc(q_nr.sem, 1)
                    if h == 5:
                        q_products(t, b, 0)

            def q_last_products(t, b, i):
                q_products(t, b, 1)

            def q_project(t, b, i):
                pe.wait_ge(q_yev.sem, q_yev.done(t))
                pe.wait_ge(q_mo.sem, q_mo.ago(t, 1))
                for g in range(2):
                    ins = pe.matmul(B[7][0:P, 0:C], yT[:, g, :], WprojT_sb[:, g, :], start=(g == 0), stop=(g == 1))
                ins.then_inc(q_pm.sem, 1)
            pipeline(pe, T, 2, (q_tile, 1), (q_project, 0), (q_last_products, 1), (q_turn, 2))

            def redo_tile(m, j, i):
                if j % SLOTS == 0:
                    pe.wait_ge(redo_in[j // SLOTS], i * (16 * SLOTS) + 16 * SLOTS)
                pe.wait_ge(r_oh.sem, r_oh.done(m))
                pe.wait_ge(r_acc.sem, r_acc.ago(m, 2))
                for c in range(2):
                    for part in range(3):
                        pe.matmul(psG[j % 2][:, EP * c:EP * c + EP],
                                  rows[:, j // SLOTS, j % SLOTS, part * C + 128 * c:part * C + 128 * c + 128],
                                  onehot[:, 0, j % 4, :], start=(part == 0), stop=(part == 2))
                pe.matmul(psG[j % 2][0:32, 2 * EP:3 * EP], rows[:, j // SLOTS, j % SLOTS, 3 * C - 8:ROW],
                          onehot[:, 0, j % 4, :], start=True, stop=True).then_inc(r_mm.sem, 1)
            with if_spread(pe):
                pipeline(pe, ET, 2 * SLOTS, (redo_tile, 0))

            pe.wait_ge(g_final, 1)

            def c_turn(t, b, i):
                pe.wait_ge(c_in1.sem, c_in1.done(t))
                pe.wait_ge(c_q.sem, c_q.ago(t, 4))
                for g in range(2):
                    pe.transpose(B[2 + b][0:P, 128 * g:128 * g + 128], c_acc[:, b % 2, g, :], ident[:, :])
                pe.matmul(B[2 + b][0:P, C:C + H], c_w[:, b % 2, :], partsum[:, :], start=True, stop=True).then_inc(c_mm.sem, 1)
            pipeline(pe, T, 4, (c_turn, 0))

            pe.wait_ge(late_in, 64)
            pe.wait_ge(c_in, 96)

            def d_turn(t, b, i):
                pe.wait_ge(d_xn.sem, d_xn.done(t))
                pe.wait_ge(d_xs.sem, d_xs.ago(t, 1))
                for k in range(2):
                    ins = pe.transpose(B[2][:, k * P:(k + 1) * P], dxn[:, b, 128 * k:128 * k + 128], ident[0:P, 0:P])
                ins.then_inc(d_tr.sem, 1)

            def d_hidden(hf):
                def product(t, b, i):
                    if hf == 0:
                        pe.wait_ge(d_xs.sem, d_xs.done(t))
                    pe.wait_ge(d_hb.sem, d_hb.ago(t * 2 + hf, 4))
                    for k in range(2):
                        ins = pe.matmul(B[psH[b] + hf][0:P, :], dxs[:, b, k, :], W1_sb[:, k, 512 * hf:512 * hf + 512], start=(k == 0), stop=(k == 1))
                    ins.then_inc(d_mm.sem, 1)
                return product

            def d_turn_hidden(t, b, i):
                for hf in range(2):
                    pe.wait_ge(d_ge.sem, d_ge.done(t * 2 + hf))
                    pe.wait_ge((d_e0, d_e1)[hf].sem, d_e0.ago(t, 1))
                    for k in range(4):
                        ins = pe.transpose(B[5 + hf][:, k * P:(k + 1) * P], hb[b][:, 512 * hf + 128 * k:512 * hf + 128 * k + 128], ident[0:P, 0:P])
                    ins.then_inc(d_ht.sem, 1)

            def d_gate(t, b, i):
                pe.wait_ge(d_e0.sem, d_e0.done(t))
                pe.wait_ge(d_e1.sem, d_e1.done(t))
                pe.wait_ge(d_lg.sem, d_lg.ago(t, 1))
                for k in range(8):
                    q = k % 4
                    ins = pe.matmul(B[7][32 * q:32 * q + 32, 0:P], Wg_sb[:, k, :], hT[:, k, :], start=(k < 4), stop=(k >= 4),
                                    skip_group_check=True)
                ins.then_inc(d_lm.sem, 1)

            def d_gate_sum(t, b, i):
                pe.wait_ge(d_gl.sem, d_gl.done(t))
                pe.matmul(B[7][0:P, P:P + NE], gl[:, :], gatesum[:, :], start=True, stop=True).then_inc(d_ls.sem, 1)
            pipeline(pe, T, 2, (d_turn, 4), (d_hidden(0), 3), (d_gate_sum, 0), (d_hidden(1), 3), (d_gate, 1), (d_turn_hidden, 2))

            pe.wait_ge(r_chosen, 1)
            pe.matmul(B[2][0:P, 0:T * NE], rtri[:, :], r_a[:, :, :].rearrange("p t e -> p (t e)"), start=True, stop=True)
            pe.matmul(B[3][0:P, 0:T * NE], rones[:, :], r_a[:, :, :].rearrange("p t e -> p (t e)"), start=True, stop=True).then_inc(r_counts, 1)

            pe.wait_ge(r_spread, 1)
            for t in range(T):
                ins = pe.matmul(B[4][:, 0:2 * ST], is_lo[:, t, :], spread[:, t, :, :].rearrange("p c s -> p (c s)"),
                                start=(t == 0), stop=(t == T - 1))
            ins.then_inc(r_ordered, 1)

            pe.wait_ge(wd_in, 16 * NE)
            pe.wait_ge(routed, 1)

            def e_turn(s, b, i):
                pe.wait_ge(hs_in[b], i * 16 + 16)
                for hf in range(2):
                    for k in range(4):
                        ins = pe.transpose(B[4 + 2 * (b % 2) + hf][:, 128 * k:128 * k + 128],
                                           hsb[b][:, 512 * hf + 128 * k:512 * hf + 128 * k + 128], ident[:, :])
                    ins.then_inc(e_tr.sem, 1)

            def e_product(s, b, i):
                col = pe.value_load(experts_i[0:1, ds(s, 1)], min_val=0, max_val=(NE - 1) * C)
                pe.wait_ge(e_e0.sem, e_e0.done(s))
                pe.wait_ge(e_e1.sem, e_e1.done(s))
                pe.wait_ge(e_t1.sem, e_t1.ago(s, 2))
                for k in range(8):
                    ins = pe.matmul(B[2 + b % 2][:, 0:C], hsT[:, b % 2, k // 4, 128 * (k % 4):128 * (k % 4) + 128], Wd_sb[:, k, ds(col, C)],
                                    start=(k == 0), stop=(k == 7))
                ins.then_inc(e_mm.sem, 1)
            pipeline(pe, ST, 4, (e_turn, 1), (e_product, 0))


def kernel(**inputs):
    import numpy as _np
    import concourse.bacc as _bacc
    from concourse import mybir as _mybir
    from concourse.bass_utils import run_bass_kernel_spmd as _run

    def edges(a, fill):
        return _np.concatenate([_np.asarray(a), _np.full(ET * EP - E, fill, _np.asarray(a).dtype)]).reshape(ET, EP)

    f = {k: _np.asarray(v) for k, v in inputs.items()}
    src, dst = edges(f["src"], 0), edges(f["dst"], -1)
    laid_out = {
        "x": f["x"], "src": src.T, "dst": dst.T, "dst0": dst[:, 0], "W": f["L0_gnn_W"],
        "a_src": f["L0_gnn_a_src"].reshape(-1), "WqkvT": f["L0_mix_Wqkv"].T, "bqkv": f["L0_mix_bqkv"],
        "WprojT": f["L0_mix_Wproj"].T, "bproj": f["L0_mix_bproj"], "temp": f["L0_mix_temperature"].reshape(-1),
        "W1": f["L0_ffn_W1"], "b1": f["L0_ffn_b1"], "Wg": f["L0_ffn_Wg"], "bg": f["L0_ffn_bg"],
        "Wd": f["L0_ffn_Wd"], "bd": f["L0_ffn_bd"].reshape(-1),
    }
    nc = _bacc.Bacc("TRN2", target_bir_lowering=False, num_devices=1)
    arrays, args = {}, []
    for name, a in laid_out.items():
        a = _np.ascontiguousarray(a)
        arrays[f"in_{name}"] = a
        args.append(nc.dram_tensor(f"in_{name}", a.shape, _mybir.dt.from_np(a.dtype), kind="ExternalInput").ap())
    args.append(nc.dram_tensor("out_0", (N, C), _mybir.dt.float32, kind="ExternalOutput").ap())
    args.append(nc.dram_tensor("table", (N, ROW), _mybir.dt.bfloat16, kind="Internal").ap())
    args.append(nc.dram_tensor("hidden", (N, HROW), _mybir.dt.float32, kind="Internal").ap())
    build(nc, *args)
    r = _run(nc, [arrays], core_ids=[0])
    return r.results[0]["out_0"]
```
